# Optimizing a Trainium2 kernel written in Bass

```python
import numpy as np
import jax
import jax.numpy as jnp

def _softmax(x, axis=-1):
    return jax.nn.softmax(x, axis=axis)

def _gelu(x):
    return jax.nn.gelu(x, approximate=True)

def _silu(x):
    return jax.nn.silu(x)

def _sigmoid(x):
    return jax.nn.sigmoid(x)

def _layernorm(x, axis=-1, eps=1e-05):
    m = jnp.mean(x, axis=axis, keepdims=True)
    v = jnp.var(x, axis=axis, keepdims=True)
    return (x - m) / jnp.sqrt(v + eps)

def _scatter_add(tgt, idx, src, axis=0):
    return tgt.at[idx].add(src)

def _segment_sum(src, seg, n):
    return jax.ops.segment_sum(src, seg, n)
kernel_name = 'mk_sandwich_d2_jaxref_r8_a3d55a'

def setup_inputs(seed: int=0):
    np.random.seed(seed)
    _w = jnp.asarray

    def _L0_attn_setup():
        import jax, jax.numpy as jnp
        import numpy as np
        DIM = 128
        H = 16
        HD = DIM // H
        EPS_DENOM = 1e-06
        EPS_LN = 1e-05
        key = jax.random.key(seed)
        ks = jax.random.split(key, 8)
        B, N = (4, 512)
        s = 1.0 / np.sqrt(DIM)
        return {'x': jax.random.normal(ks[0], (B, N, DIM), dtype=jnp.float32), 'Wq': jax.random.normal(ks[1], (DIM, DIM), dtype=jnp.float32) * s, 'bq': jnp.zeros((DIM,), dtype=jnp.float32), 'Wk': jax.random.normal(ks[2], (DIM, DIM), dtype=jnp.float32) * s, 'bk': jnp.zeros((DIM,), dtype=jnp.float32), 'Wv': jax.random.normal(ks[3], (DIM, DIM), dtype=jnp.float32) * s, 'bv': jnp.zeros((DIM,), dtype=jnp.float32), 'gamma': jnp.ones((DIM,), dtype=jnp.float32), 'beta': jnp.zeros((DIM,), dtype=jnp.float32)}
    _L0_attn_in = _L0_attn_setup()

    def _L0_ffn_setup():
        import jax, jax.numpy as jnp
        import numpy as np
        from math import ceil
        CAPACITY_FACTOR = 2.0
        MIN_CAPACITY = 4
        key = jax.random.key(seed)
        ks = jax.random.split(key, 4)
        B, S, D, Di, E = (4, 256, 128, 512, 8)
        x = jax.random.normal(ks[0], (B, S, D), dtype=jnp.float32)
        Wr = jax.random.normal(ks[1], (D, E), dtype=jnp.float32) * D ** (-0.5)
        W1 = jax.random.normal(ks[2], (E, D, Di), dtype=jnp.float32) * D ** (-0.5)
        b1 = jnp.zeros((E, Di), dtype=jnp.float32)
        W2 = jax.random.normal(ks[3], (E, Di, D), dtype=jnp.float32) * Di ** (-0.5)
        b2 = jnp.zeros((E, D), dtype=jnp.float32)
        return {'x': x, 'Wr': Wr, 'W1': W1, 'b1': b1, 'W2': W2, 'b2': b2}
    _L0_ffn_in = _L0_ffn_setup()

    def _L1_attn_setup():
        import jax, jax.numpy as jnp
        import numpy as np
        HIDDEN = 128
        D_COMPLEX = HIDDEN // 2
        key = jax.random.key(seed)
        ks = jax.random.split(key, 9)
        B, S, H = (4, 512, HIDDEN)
        scale = 1.0 / np.sqrt(H)
        inp = {'x': jax.random.normal(ks[0], (B, S, H), dtype=jnp.float32), 'Wq': jax.random.normal(ks[1], (H, H), dtype=jnp.float32) * scale, 'bq': jnp.zeros((H,), dtype=jnp.float32), 'Wk': jax.random.normal(ks[2], (H, H), dtype=jnp.float32) * scale, 'bk': jnp.zeros((H,), dtype=jnp.float32), 'Wv': jax.random.normal(ks[3], (H, H), dtype=jnp.float32) * scale, 'bv': jnp.zeros((H,), dtype=jnp.float32), 'Wo': jax.random.normal(ks[4], (H, H), dtype=jnp.float32) * scale, 'bo': jnp.zeros((H,), dtype=jnp.float32)}
        return inp
    _L1_attn_in = _L1_attn_setup()

    def _L1_ffn_setup():
        import jax, jax.numpy as jnp
        import numpy as np
        GROUP = 16
        EPS = 1e-05

        def _dequant(q, scale):
            w = q.astype(jnp.float32) / 7.5 - 1.0
            return w * jnp.repeat(scale, GROUP, axis=1)

        def _qlora_linear(x, q, scale, bias, la, lb):
            w = _dequant(q, scale)
            base = jnp.einsum('btd,od->bto', x, w) + bias
            lora = jnp.einsum('btr,or->bto', jnp.einsum('btd,rd->btr', x, la), lb)
            return base + lora

        def _layernorm(x, g, b):
            mu = jnp.mean(x, axis=-1, keepdims=True)
            var = jnp.mean(jnp.square(x - mu), axis=-1, keepdims=True)
            return (x - mu) * jax.lax.rsqrt(var + EPS) * g + b
        key = jax.random.key(seed)
        ks = jax.random.split(key, 6)
        D, R, B, T = (128, 32, 8, 512)
        x = jax.random.normal(ks[0], (B, T, D), dtype=jnp.float32)
        qweights = jax.random.randint(ks[1], (6, D, D), 0, 16, dtype=jnp.int32)
        scales = jax.random.uniform(ks[2], (6, D, D // GROUP), dtype=jnp.float32)
        biases = jax.random.normal(ks[3], (6, D), dtype=jnp.float32) * 0.02
        lora_a = jax.random.normal(ks[4], (6, R, D), dtype=jnp.float32) * 0.02
        lora_b = jax.random.normal(ks[5], (6, D, R), dtype=jnp.float32) * 0.02
        ln_gamma = jnp.ones((3, D), dtype=jnp.float32)
        ln_beta = jnp.zeros((3, D), dtype=jnp.float32)
        return {'x': x, 'qweights': qweights, 'scales': scales, 'biases': biases, 'lora_a': lora_a, 'lora_b': lora_b, 'ln_gamma': ln_gamma, 'ln_beta': ln_beta}
    _L1_ffn_in = _L1_ffn_setup()
    _d = {'L0_attn_x': _L0_attn_in['x'], 'L0_attn_Wq': _L0_attn_in['Wq'], 'L0_attn_bq': _L0_attn_in['bq'], 'L0_attn_Wk': _L0_attn_in['Wk'], 'L0_attn_bk': _L0_attn_in['bk'], 'L0_attn_Wv': _L0_attn_in['Wv'], 'L0_attn_bv': _L0_attn_in['bv'], 'L0_attn_gamma': _L0_attn_in['gamma'], 'L0_attn_beta': _L0_attn_in['beta'], 'L0_ffn_Wr': _L0_ffn_in['Wr'], 'L0_ffn_W1': _L0_ffn_in['W1'], 'L0_ffn_b1': _L0_ffn_in['b1'], 'L0_ffn_W2': _L0_ffn_in['W2'], 'L0_ffn_b2': _L0_ffn_in['b2'], 'L1_attn_Wq': _L1_attn_in['Wq'], 'L1_attn_bq': _L1_attn_in['bq'], 'L1_attn_Wk': _L1_attn_in['Wk'], 'L1_attn_bk': _L1_attn_in['bk'], 'L1_attn_Wv': _L1_attn_in['Wv'], 'L1_attn_bv': _L1_attn_in['bv'], 'L1_attn_Wo': _L1_attn_in['Wo'], 'L1_attn_bo': _L1_attn_in['bo'], 'L1_ffn_qweights': _L1_ffn_in['qweights'], 'L1_ffn_scales': _L1_ffn_in['scales'], 'L1_ffn_biases': _L1_ffn_in['biases'], 'L1_ffn_lora_a': _L1_ffn_in['lora_a'], 'L1_ffn_lora_b': _L1_ffn_in['lora_b'], 'L1_ffn_ln_gamma': _L1_ffn_in['ln_gamma'], 'L1_ffn_ln_beta': _L1_ffn_in['ln_beta']}
    _x0 = _d['L0_attn_x']
    _d['L0_attn_x'] = jax.random.normal(jax.random.fold_in(jax.random.key(seed), 1), (8, 256, 128), dtype=_x0.dtype)
    del _x0
    return _d

def reference(L0_attn_x, L0_attn_Wq, L0_attn_bq, L0_attn_Wk, L0_attn_bk, L0_attn_Wv, L0_attn_bv, L0_attn_gamma, L0_attn_beta, L0_ffn_Wr, L0_ffn_W1, L0_ffn_b1, L0_ffn_W2, L0_ffn_b2, L1_attn_Wq, L1_attn_bq, L1_attn_Wk, L1_attn_bk, L1_attn_Wv, L1_attn_bv, L1_attn_Wo, L1_attn_bo, L1_ffn_qweights, L1_ffn_scales, L1_ffn_biases, L1_ffn_lora_a, L1_ffn_lora_b, L1_ffn_ln_gamma, L1_ffn_ln_beta):

    def _L0_attn_ref(x, Wq, bq, Wk, bk, Wv, bv, gamma, beta):
        import jax, jax.numpy as jnp
        import numpy as np
        DIM = 128
        H = 16
        HD = DIM // H
        EPS_DENOM = 1e-06
        EPS_LN = 1e-05
        B, N, C = x.shape
        q = (x @ Wq.T + bq).reshape(B, N, H, HD)
        k = (x @ Wk.T + bk).reshape(B, N, H, HD)
        v = (x @ Wv.T + bv).reshape(B, N, H, HD)
        q = jax.nn.relu(q)
        k = jax.nn.relu(k)
        kv = jnp.einsum('bnhd,bnhp->bhdp', k, v)
        k_sum = k.sum(axis=1)
        denom = jnp.einsum('bnhd,bhd->bnh', q, k_sum)
        denom = jnp.maximum(denom, EPS_DENOM)[..., None]
        ctx = jnp.einsum('bnhd,bhdp->bnhp', q, kv)
        out = (ctx / denom).reshape(B, N, C)
        y = out + x
        mu = y.mean(axis=-1, keepdims=True)
        var = y.var(axis=-1, keepdims=True)
        return (y - mu) / jnp.sqrt(var + EPS_LN) * gamma + beta

    def _L0_ffn_ref(x, Wr, W1, b1, W2, b2):
        import jax, jax.numpy as jnp
        import numpy as np
        from math import ceil
        CAPACITY_FACTOR = 2.0
        MIN_CAPACITY = 4
        B, S, D = x.shape
        E = Wr.shape[1]
        N = B * S
        k = max(MIN_CAPACITY, ceil(N * CAPACITY_FACTOR / E))
        xt = x.reshape(N, D)
        scores = jax.nn.softmax(xt @ Wr, axis=-1)
        G, idx = jax.lax.top_k(scores.T, k)
        X_in = xt[idx]
        h = jax.nn.gelu(jnp.einsum('ekd,edh->ekh', X_in, W1) + b1[:, None, :], approximate=False)
        X_e = jnp.einsum('ekh,ehd->ekd', h, W2) + b2[:, None, :]
        contrib = (G[..., None] * X_e).reshape(E * k, D)
        out = jnp.zeros((N, D), dtype=x.dtype).at[idx.reshape(-1)].add(contrib)
        return out.reshape(B, S, D)

    def _L1_attn_ref(x, Wq, bq, Wk, bk, Wv, bv, Wo, bo):
        import jax, jax.numpy as jnp
        import numpy as np
        HIDDEN = 128
        D_COMPLEX = HIDDEN // 2
        Q = x @ Wq.T + bq
        K = x @ Wk.T + bk
        V = x @ Wv.T + bv
        scores = jnp.einsum('bqd,bkd->bqk', Q, K) / np.sqrt(D_COMPLEX)
        weights = jax.nn.softmax(scores, axis=-1)
        out = jnp.einsum('bqk,bkd->bqd', weights, V)
        return out @ Wo.T + bo

    def _L1_ffn_ref(x, qweights, scales, biases, lora_a, lora_b, ln_gamma, ln_beta):
        import jax, jax.numpy as jnp
        import numpy as np
        GROUP = 16
        EPS = 1e-05

        def _dequant(q, scale):
            w = q.astype(jnp.float32) / 7.5 - 1.0
            return w * jnp.repeat(scale, GROUP, axis=1)

        def _qlora_linear(x, q, scale, bias, la, lb):
            w = _dequant(q, scale)
            base = jnp.einsum('btd,od->bto', x, w) + bias
            lora = jnp.einsum('btr,or->bto', jnp.einsum('btd,rd->btr', x, la), lb)
            return base + lora

        def _layernorm(x, g, b):
            mu = jnp.mean(x, axis=-1, keepdims=True)
            var = jnp.mean(jnp.square(x - mu), axis=-1, keepdims=True)
            return (x - mu) * jax.lax.rsqrt(var + EPS) * g + b
        h = x
        for blk in range(3):
            i0, i1 = (2 * blk, 2 * blk + 1)
            y = _qlora_linear(h, qweights[i0], scales[i0], biases[i0], lora_a[i0], lora_b[i0])
            y = _layernorm(y, ln_gamma[blk], ln_beta[blk])
            y = jax.nn.gelu(y, approximate=False)
            y = _qlora_linear(y, qweights[i1], scales[i1], biases[i1], lora_a[i1], lora_b[i1])
            h = y + h
        return h
    x = L0_attn_x
    x = x + _layernorm(_L0_attn_ref(_layernorm(x, axis=-1), L0_attn_Wq, L0_attn_bq, L0_attn_Wk, L0_attn_bk, L0_attn_Wv, L0_attn_bv, L0_attn_gamma, L0_attn_beta), axis=-1)
    x = x + _layernorm(_L0_ffn_ref(_layernorm(x, axis=-1), L0_ffn_Wr, L0_ffn_W1, L0_ffn_b1, L0_ffn_W2, L0_ffn_b2), axis=-1)
    x = x + _layernorm(_L1_attn_ref(_layernorm(x, axis=-1), L1_attn_Wq, L1_attn_bq, L1_attn_Wk, L1_attn_bk, L1_attn_Wv, L1_attn_bv, L1_attn_Wo, L1_attn_bo), axis=-1)
    x = x + _layernorm(_L1_ffn_ref(_layernorm(x, axis=-1), L1_ffn_qweights, L1_ffn_scales, L1_ffn_biases, L1_ffn_lora_a, L1_ffn_lora_b, L1_ffn_ln_gamma, L1_ffn_ln_beta), axis=-1)
    return x

_drawn_inputs = setup_inputs


def setup_inputs(seed=0):
    import zlib

    import numpy as np

    out = dict(_drawn_inputs(seed))
    spreads = {'L0_attn_bq': (0.0, 0.322),
     'L0_attn_bk': (0.0, 0.361),
     'L0_attn_bv': (0.0, 0.1),
     'L0_attn_gamma': (1.0, 0.2),
     'L0_attn_beta': (0.0, 0.1),
     'L0_ffn_b1': (0.0, 0.1),
     'L0_ffn_b2': (0.0, 0.1),
     'L1_attn_bq': (0.0, 0.1),
     'L1_attn_bk': (0.0, 0.8),
     'L1_attn_bv': (0.0, 0.1),
     'L1_attn_bo': (0.0, 0.1),
     'L1_ffn_ln_gamma': (1.0, 0.2),
     'L1_ffn_ln_beta': (0.0, 0.1)}
    factors = {'L1_ffn_biases': 8.0, 'L1_ffn_lora_a': 8.0, 'L1_ffn_lora_b': 8.0}
    for name, (base, spread) in spreads.items():
        noise = np.random.default_rng([zlib.crc32(name.encode()), seed]).standard_normal(out[name].shape)
        drawn = base * np.exp(spread * noise) if base else spread * noise
        out[name] = jnp.asarray(drawn.astype(out[name].dtype))
    for name, factor in factors.items():
        out[name] = (out[name] * factor).astype(out[name].dtype)
    return out
```

```python
from contextlib import ExitStack

import concourse.bass as bass
from concourse import mybir

ALU = mybir.AluOpType
ACT = mybir.ActivationFunctionType
AX = mybir.AxisListType
F32 = mybir.dt.float32
F16 = mybir.dt.float16
BF16 = mybir.dt.bfloat16
I32 = mybir.dt.int32
U32 = mybir.dt.uint32

P = 128
LN_EPS = 1e-5
DENOM_EPS = 1e-6
SCORE_BITS = 30


def staggered(phases, groups):
    for step in range(groups + len(phases) - 1):
        for phase in reversed(range(len(phases))):
            g = step - phase
            if 0 <= g < groups and phases[phase] is not None:
                phases[phase](g)


def sandwich_kernel(nc, a):
    B, S, D = a["L0_attn_x"].shape
    E, _, HID = a["L0_ffn_W1"].shape
    N = B * S
    T = N // P
    GT = 4
    G = T // GT
    GN = GT * P
    BT = S // P
    GB = GT // BT
    H = 16
    HD = D // H
    KEEP = max(4, -(-N * 2 // E))
    SC = KEEP // P
    J = HID // P
    ROW = D + E
    NL = a["L1_ffn_qweights"].shape[0]
    R = a["L1_ffn_lora_a"].shape[1]
    NS = a["L1_ffn_scales"].shape[2]
    ATT_SCALE = 1.0 / float(D // 2) ** 0.5
    assert D == P and E * T == P and GT % BT == 0 and KEEP % P == 0

    ctx = ExitStack()
    with ctx:
        def sb(name, shape, dt=F32):
            return ctx.enter_context(nc.sbuf_tensor(name, shape, dt))

        def ps(name, shape, dt=F32):
            return ctx.enter_context(nc.psum_tensor(name, shape, dt))

        def sem(name):
            return ctx.enter_context(nc.semaphore(name))

        table = nc.dram_tensor("token_table", [N, ROW], F32, kind="Internal").ap()
        moe_sum = nc.dram_tensor("moe_sum", [N, D], F32, kind="Internal").ap()

        ident = sb("ident", [P, P])
        head_block = sb("head_block", [P, P])
        head_col = sb("head_col", [P, H])
        same_expert = sb("same_expert", [P, P], BF16)
        tile_before = sb("tile_before", [P, P], BF16)
        own_expert = sb("own_expert", [P, E], F16)
        tile_start_i = sb("tile_start_i", [P, E], I32)
        tile_start = sb("tile_start", [P, E], F16)
        tile_start_f = sb("tile_start_f", [P, E])
        slot_i = sb("slot_i", [P, KEEP], I32)
        slot_free = sb("slot_free", [P, KEEP])
        slot_part_i = sb("slot_part_i", [P, SC], I32)
        slot_part = sb("slot_part", [P, SC])
        zeros = sb("zeros", [P, T * D])
        ones3 = sb("ones3", [3, P], BF16)
        ones_row = sb("ones_row", [1, P])
        minus_half = sb("minus_half", [P, GT])

        w_raw = sb("w_raw", [P, 7, P])
        w_qT = sb("w_qT", [P, P])
        w_kvT = sb("w_kvT", [P, 2, P])
        w1_qT = sb("w1_qT", [P, P])
        w1_kT = sb("w1_kT", [P, P])
        w1_oT = sb("w1_oT", [P, P])
        w1_vo = sb("w1_vo", [P, P])
        bv_cols = sb("bv_cols", [P, P])
        bo_row = sb("bo_row", [1, P])
        bo_all = sb("bo_all", [P, P])
        NV = 32 + 16
        vec_rows = sb("vec_rows", [NV, P])
        vec = sb("vec", [P, NV])
        NB = 2 * D + E * D + 4 * D
        bias3 = sb("bias3", [3, NB], BF16)
        gamma_all = sb("gamma_all", [P, D])
        beta_all = sb("beta_all", [P, D])
        wr = sb("wr", [P, E])
        w1 = sb("w1", [P, E, HID])
        w2 = sb("w2", [P, E, J, D])
        q_int = sb("q_int", [P, NL, D], I32)
        q_scale = sb("q_scale", [P, NL, NS])
        q_w = sb("q_w", [P, NL, D])
        q_ws = sb("q_ws", [P, NL, D])
        lora_a = sb("lora_a", [R, NL, D])
        lora_b = sb("lora_b", [P, NL, R])
        lora_bT = sb("lora_bT", [R, NL, D])
        w_effT = sb("w_effT", [P, NL, D])

        x0 = sb("x0", [P, T, D])
        a_tok = sb("a_tok", [P, T, D])
        hT = sb("hT", [P, 2, J, KEEP])
        hT_flat = hT[:, :, :, :].rearrange("p a j k -> p (a j k)")
        aT = hT_flat[:, 0:T * P]
        qT = hT_flat[:, T * P:2 * T * P]
        xg = sb("xg", [P, E, SC, ROW])
        xg_flat = xg[:, :, :, :].rearrange("p e c r -> p (e c r)")
        k_tok = xg_flat[:, 0:T * D].rearrange("p (t d) -> p t d", d=D)
        VW = D + 4
        v_tok = xg_flat[:, T * D:T * (D + VW)].rearrange("p (t d) -> p t d", d=VW)
        kv_blk = sb("kv_blk", [P, B, D + H])
        den = sb("den", [P, T, H])
        rden = sb("rden", [P, T, H])
        y0 = sb("y0", [P, T, D])
        y1 = sb("y1", [P, T, D])
        z = sb("z", [P, T, D])
        u = y0
        x1 = sb("x1", [P, T, D])
        tab = sb("tab", [P, T, ROW])
        bT = sb("bT", [P, T * P])
        bias_rows = bT[0:3, 0:NB]
        bias_hi = x1[0:3, :, :].rearrange("p t d -> p (t d)").bitcast(BF16)[:, 0:NB]
        bias_mid = x1[0:3, :, :].rearrange("p t d -> p (t d)").bitcast(BF16)[:, NB:2 * NB]
        bias_lo = y1[0:3, :, :].rearrange("p t d -> p (t d)").bitcast(BF16)[:, 0:NB]
        stats = sb("stats", [P, T, 6])

        class Norm:
            def __init__(self, name):
                self.mv = sb(f"mv_{name}", [P, T, 2])
                self.ve = sb(f"ve_{name}", [P, T])
                self.rstd = sb(f"rstd_{name}", [P, T])
                self.stats_ready = sem(f"stats_{name}")
                self.rstd_ready = sem(f"rstd_{name}_ready")

        ln = {n: Norm(n) for n in ("a_in", "a_mid", "a_out", "b_in", "b_out", "c_in", "c_out",
                                   "d_in", "d0", "d1", "d2", "d_out")}

        logit_max = sb("logit_max", [P, T])
        shifted = sb("shifted", [P, T, E])
        expd = sb("expd", [P, T, E])
        expsum = sb("expsum", [P, T])
        rexpsum = sb("rexpsum", [P, T])
        sc_et = sb("sc_et", [P, E, T])
        scoreT = sb("scoreT", [P, P])
        cand = sb("cand", [P, 2], I32)
        below = sb("below", [P, 1], I32)
        hits = sb("hits", [P, P], BF16)
        hit_count = sb("hit_count", [P, 1], BF16)
        above = sb("above", [P, P], BF16)
        tied = sb("tied", [P, P], BF16)
        above_count = sb("above_count", [P, 1], BF16)
        tied_count = sb("tied_count", [P, 1], BF16)
        tie_room = sb("tie_room", [P, 2])
        tie_rank = sb("tie_rank", [P, P])
        tie_kept = sb("tie_kept", [P, P])
        kept_rank = sb("kept_rank", [P, P])
        kept_count = sb("kept_count", [P, 1], BF16)
        kept_first = sb("kept_first", [P, 1])
        rank_all = sb("rank_all", [P, P], F16)
        rank_last = sb("rank_last", [P, 1])
        rank_by_expert = sb("rank_by_expert", [P, E, P], F16)
        from_first = sb("from_first", [P, KEEP], F16)
        slot_row = sb("slot_row", [P, KEEP], F16)
        passed = sb("passed", [P, E, P], BF16)
        passed_count = sb("passed_count", [P, SC, E])
        token_f = sb("token_f", [P, SC, E])
        token_of = sb("token_of", [P, SC, E], U32)

        a_flat = a_tok[:, :, :].rearrange("p t d -> p (t d)")
        xgT = a_flat[:, 0:2 * KEEP].rearrange("p (a k) -> p a k", a=2)
        yg = a_flat[:, 2 * KEEP:2 * KEEP + 2 * SC * D].rearrange("p (a c d) -> p a c d", a=2, c=SC)
        moe = y1

        x2 = x0
        c_tok = a_tok
        cT = aT
        q1T = qT
        k1T = xg_flat[:, T * D:2 * T * D]
        v1 = k_tok
        smax = sb("smax", [P, T])
        nsmax = sb("nsmax", [P, T])
        prob = w1[:, :, :].rearrange("p e h -> p (e h)").rearrange("p (t s) -> p t s", s=S)
        psum_p = sb("psum_p", [P, T])
        rsum = sb("rsum", [P, T])
        probT = w2[:, :, :, :].rearrange("p e j d -> p (e j d)").rearrange("p (b k q) -> p b k q", b=B, k=BT)
        o_tok = y0
        x3 = x1
        d_tok = y0
        h_T = [bT, q1T, k1T]
        n_tok = y1
        g_T = aT
        w_out = z
        h_out = z
        y_out = zeros[:, :].rearrange("p (t d) -> p t d", d=D)

        banks = ps("banks", [P, 8, 512])
        bank = [banks[:, i, :] for i in range(8)]

        names = """consts_z consts ones_set
        ld_w ld_vec ld_bias ld_small ld_w1 ld_w2 ld_q ld_lora ld_bo
        wT_done wT_copied vecT_done vec_copied lbT_done lbT_copied q_ready vo_done vo_copied bo_done bo_copied bv_ready fin_done fin_ready
        eff_done eff_copied bias_ready
        a_ready aT_done aT_copied q_done qT_ready kv_done kv0_ready kv1_ready ksum_done kv_ready ctx_done y0_ready y1_ready
        u_ready x1_ready
        b_ready bT_done bT_copied logit_done shifted_ready exp_ready scores_ready scoreT_done scoreT_ready
        cand_counted cand_summed cand_taken room_ready first_ready sel_counted sel_summed kept_counted kept_summed slots_ready slots_done slots_used start_done
        token_ready table_written zero_written moe_loaded
        gT_done gT_copied h_done h_ready y_done yg_ready
        uc_ready x2_ready c_ready cT_done cT_copied q1_done q1_ready k1_done k1_ready v1_done v1_ready
        s_done smax_ready p_ready pT_done pT0_copied pT1_copied o_done o_ready ud_ready x3_ready
        d_ready dT_done dT_copied uo_ready out_ready out_written
        dve_step pool_step""".split()
        sm = {n: sem(n) for n in names}
        ld_x = [sem(f"ld_x{g}") for g in range(G)]
        gathered = [sem(f"gathered{i}") for i in range(4)]
        scattered = [sem(f"scattered{i}") for i in range(2)]
        lin_done = [sem(f"lin_done{k}") for k in range(3)]
        n_ready = [sem(f"n_ready{k}") for k in range(3)]
        nT_done = [sem(f"nT_done{k}") for k in range(3)]
        gelu_ready = [sem(f"gelu_ready{k}") for k in range(3)]
        res_done = [sem(f"res_done{k}") for k in range(3)]
        hT_ready = [sem(f"hT_ready{k}") for k in range(3)]

        x_dram = a["L0_attn_x"].rearrange("b (t p) d -> p (b t) d", p=P)
        out_dram = a["out"].rearrange("b (t p) d -> p (b t) d", p=P)
        moe_dram = moe_sum.rearrange("(t p) d -> p t d", p=P)

        def tiles(g):
            return range(g * GT, (g + 1) * GT)

        def toks(g):
            return slice(g * GN, (g + 1) * GN)

        V_B1, V_BQ, V_BQ1, V_BK1, V_BV1, V_G, V_BE, V_BIAS = 0, 32, 33, 34, 35, 36, 39, 42
        R_KV, R_B2, R_LIN = 0, 2 * D, 2 * D + E * D

        block = ctx.enter_context(nc.Block())

        @block.sync
        def _(sp):
            for g in range(G):
                sp.dma_start(x0[:, g * GT:(g + 1) * GT, :], x_dram[:, g * GT:(g + 1) * GT, :]).then_inc(ld_x[g], 16)
                if g == 0:
                    for i, n in enumerate(("L0_attn_Wq", "L0_attn_Wk", "L0_attn_Wv", "L1_attn_Wq", "L1_attn_Wk",
                                           "L1_attn_Wv", "L1_attn_Wo")):
                        sp.dma_start(w_raw[:, i, :], a[n]).then_inc(sm["ld_w"], 16)
            row = lambda n: a[n].rearrange("(o d) -> o d", o=1)
            for dst, n in ((V_BQ, "L0_attn_bq"), (V_BQ1, "L1_attn_bq"), (V_BK1, "L1_attn_bk"), (V_BV1, "L1_attn_bv")):
                sp.dma_start(vec_rows[dst:dst + 1, :], row(n)).then_inc(sm["ld_vec"], 16)
            sp.dma_start(vec_rows[V_B1:V_B1 + E * J, :], a["L0_ffn_b1"].rearrange("e (j p) -> (e j) p", p=P)).then_inc(sm["ld_vec"], 16)
            sp.dma_start(vec_rows[V_G:V_G + 3, :], a["L1_ffn_ln_gamma"]).then_inc(sm["ld_vec"], 16)
            sp.dma_start(vec_rows[V_BE:V_BE + 3, :], a["L1_ffn_ln_beta"]).then_inc(sm["ld_vec"], 16)
            sp.dma_start(vec_rows[V_BIAS:V_BIAS + NL, :], a["L1_ffn_biases"]).then_inc(sm["ld_vec"], 16)
            three = lambda r, at: sp.dma_start(bias_rows[:, at:at + r.shape[1]],
                                               r.to_broadcast([3, r.shape[1]])).then_inc(sm["ld_bias"], 16)
            three(row("L0_attn_bk"), R_KV)
            three(row("L0_attn_bv"), R_KV + D)
            three(a["L0_ffn_b2"].rearrange("(o e) d -> o (e d)", o=1), R_B2)
            for k, i in enumerate((0, 2, 4, 5)):
                three(a["L1_ffn_biases"][i:i + 1, :], R_LIN + k * D)
            sp.dma_start(gamma_all[:, :], row("L0_attn_gamma").to_broadcast([P, D])).then_inc(sm["ld_small"], 16)
            sp.dma_start(beta_all[:, :], row("L0_attn_beta").to_broadcast([P, D])).then_inc(sm["ld_small"], 16)
            sp.dma_start(wr[:, :], a["L0_ffn_Wr"]).then_inc(sm["ld_small"], 16)
            sp.dma_start(bo_row[:, :], row("L1_attn_bo")).then_inc(sm["ld_small"], 16)
            sp.dma_start(q_int[:, :, :], a["L1_ffn_qweights"].rearrange("l o i -> o l i")).then_inc(sm["ld_q"], 16)
            sp.dma_start(q_scale[:, :, :], a["L1_ffn_scales"].rearrange("l o s -> o l s")).then_inc(sm["ld_q"], 16)
            sp.dma_start(lora_a[:, :, :], a["L1_ffn_lora_a"].rearrange("l r i -> r l i")).then_inc(sm["ld_lora"], 16)
            sp.dma_start(lora_b[:, :, :], a["L1_ffn_lora_b"].rearrange("l o r -> o l r")).then_inc(sm["ld_lora"], 16)
            sp.dma_start(w1[:, :, :], a["L0_ffn_W1"].rearrange("e d h -> d e h")).then_inc(sm["ld_w1"], 16)
            sp.dma_start(w2[:, :, :, :], a["L0_ffn_W2"].rearrange("e (j p) d -> p e j d", p=P)).then_inc(sm["ld_w2"], 16)
            sp.wait_ge(sm["consts"], 1)
            sp.dma_start(moe_dram, zeros[:, :].rearrange("p (t d) -> p t d", d=D)).then_inc(sm["zero_written"], 16)
            sp.wait_ge(sm["scores_ready"], 1)
            sp.dma_start(table.rearrange("(t p) c -> p t c", p=P), tab[:, :, :]).then_inc(sm["table_written"], 16)
            sp.wait_ge(scattered[(E - 1) % 2], 16 * SC * (E // 2))
            sp.dma_start(moe[:, :, :], moe_dram).then_inc(sm["moe_loaded"], 16)
            for g in range(G):
                sp.wait_ge(sm["out_ready"], g + 1)
                sp.dma_start(out_dram[:, g * GT:(g + 1) * GT, :], y_out[:, g * GT:(g + 1) * GT, :]).then_inc(sm["out_written"], 16)
            sp.wait_ge(sm["out_written"], 16 * G)

        @block.gpsimd
        def _(pool):
            step = [0]

            def link(ins):
                step[0] += 1
                ins.then_inc(sm["pool_step"], 1)
                pool.wait_ge(sm["pool_step"], step[0])

            def band(view, pattern, mult):
                base, pat = pattern
                link(pool.affine_select(out=view, in_=view, compare_op=ALU.is_ge, fill=0.0, base=base,
                                        pattern=pat, channel_multiplier=mult))

            pool.memset(minus_half[:, :], -0.5)
            link(pool.memset(ident[:, :], 0.0))
            pool.affine_select(out=ident[:, :], in_=ident[:, :], compare_op=ALU.not_equal, fill=1.0, base=0,
                               pattern=[[-1, P]], channel_multiplier=1).then_inc(sm["ones_set"], 1)
            pool.memset(v_tok[:, :, D:D + 1], 1.0).then_inc(sm["ones_set"], 1)
            pool.memset(ones3[:, :], 1.0)
            link(pool.memset(ones_row[:, :], 1.0))
            link(pool.memset(head_block[:, :], 1.0))
            hb = head_block[:, :].rearrange("p (h d) -> p h d", d=HD)
            band(hb, (0, [[-HD, H], [0, HD]]), 1)
            band(hb, (HD - 1, [[HD, H], [0, HD]]), -1)
            link(pool.memset(head_col[:, :], 1.0))
            band(head_col[:, :], (0, [[-HD, H]]), 1)
            band(head_col[:, :], (HD - 1, [[HD, H]]), -1)
            link(pool.memset(same_expert[:, :], 1.0))
            se = same_expert[:, :].rearrange("p (e t) -> p e t", t=T)
            band(se, (0, [[-T, E], [0, T]]), 1)
            band(se, (T - 1, [[T, E], [0, T]]), -1)
            link(pool.tensor_copy(tile_before[:, :], same_expert[:, :]))
            band(tile_before[:, :], (-1, [[1, P]]), -1)
            link(pool.memset(own_expert[:, :], 1.0))
            band(own_expert[:, :], (0, [[-T, E]]), 1)
            band(own_expert[:, :], (T - 1, [[T, E]]), -1)
            link(pool.iota(tile_start_i[:, :], [[-T * P, E]], base=0, channel_multiplier=P))
            link(pool.tensor_copy(tile_start_f[:, :], tile_start_i[:, :]))
            link(pool.tensor_tensor(tile_start[:, :], tile_start_f[:, :], own_expert[:, :], ALU.mult))
            link(pool.iota(slot_i[:, :], [[1, KEEP]], base=0, channel_multiplier=0))
            link(pool.tensor_copy(slot_free[:, :], slot_i[:, :]))
            link(pool.iota(slot_part_i[:, :], [[P, SC]], base=0, channel_multiplier=1))
            link(pool.tensor_copy(slot_part[:, :], slot_part_i[:, :]))
            pool.memset(zeros[:, :], 0.0).then_inc(sm["consts"], 1)

            def rstd(n):
                def run(g):
                    L = ln[n]
                    c = slice(g * GT, (g + 1) * GT)
                    pool.wait_ge(L.stats_ready, g + 1)
                    link(pool.tensor_scalar(L.ve[:, c], L.mv[:, c, 1], LN_EPS, None, ALU.add))
                    pool.tensor_tensor(L.rstd[:, c], L.ve[:, c], minus_half[:, :], ALU.pow).then_inc(L.rstd_ready, 1)
                return run

            def add(out, in0, in1, waits, done):
                def run(g):
                    c = slice(g * GT, (g + 1) * GT)
                    for s in waits:
                        pool.wait_ge(sm[s], g + 1)
                    pool.tensor_tensor(out[:, c, :], in0[:, c, :], in1[:, c, :], ALU.add).then_inc(sm[done], 1)
                return run

            staggered([rstd("a_in"), None, None, None,
                       add(y1, y0, a_tok, ["y0_ready"], "y1_ready"),
                       rstd("a_mid"), rstd("a_out"),
                       add(x1, x0, u, ["u_ready"], "x1_ready"), rstd("b_in"), None], G)

            pool.wait_ge(sm["ld_q"], 32)
            link(pool.tensor_scalar(q_w[:, :, :], q_int[:, :, :], 1.0 / 7.5, -1.0, ALU.mult, ALU.add))
            pool.tensor_tensor(q_ws[:, :, :].rearrange("p l (s k) -> p (l s) k", s=NS),
                               q_w[:, :, :].rearrange("p l (s k) -> p (l s) k", s=NS),
                               q_scale[:, :, :].rearrange("p l s -> p (l s)").unsqueeze(2).to_broadcast([P, NL * NS, D // NS]),
                               ALU.mult).then_inc(sm["q_ready"], 1)

            def gather(e):
                for c in range(SC):
                    pool.indirect_dma_start(
                        out=xg[:, e, c, :], out_offset=None, in_=table,
                        in_offset=bass.IndirectOffsetOnAxis(ap=token_of[:, c, e:e + 1], axis=0)).then_inc(gathered[e % 4], 16)

            def scatter(e):
                pool.wait_ge(sm["yg_ready"], e + 1)
                if e:
                    pool.wait_ge(scattered[(e - 1) % 2], 16 * SC * ((e - 1) // 2 + 1))
                else:
                    pool.wait_ge(sm["zero_written"], 16)
                for c in range(SC):
                    pool.indirect_dma_start(
                        out=moe_sum, out_offset=bass.IndirectOffsetOnAxis(ap=token_of[:, c, e:e + 1], axis=0),
                        in_=yg[:, e % 2, c, :], in_offset=None, compute_op=ALU.add).then_inc(scattered[e % 2], 16)

            pool.wait_ge(sm["table_written"], 16)
            pool.wait_ge(sm["token_ready"], 1)
            AHEAD = 3
            for e in range(AHEAD):
                gather(e)
            for e in range(E):
                if e + AHEAD < E:
                    gather(e + AHEAD)
                scatter(e)

            staggered([rstd("b_out"),
                       add(x2, x1, z, ["uc_ready"], "x2_ready"), rstd("c_in"), None, None, None, None,
                       rstd("c_out"), add(x3, x2, w_out, ["ud_ready"], "x3_ready"), rstd("d_in"), None,
                       rstd("d0"), None, rstd("d1"), None, rstd("d2"), None, rstd("d_out"),
                       add(y_out, x3, u, ["uo_ready"], "out_ready")], G)

        @block.scalar
        def _(act):
            def copy(dst, src, func=ACT.Copy, **kw):
                return act.activation(dst, src, func, **kw)

            act.wait_ge(sm["wT_done"], 1)
            copy(w_qT[:, :], bank[0][:, 0:P])
            copy(w_kvT[:, :, :], bank[0][:, P:3 * P].rearrange("p (a b) -> p a b", a=2)).then_inc(sm["wT_copied"], 1)
            act.wait_ge(sm["wT_done"], 2)
            copy(w1_qT[:, :], bank[1][:, 0:P])
            copy(w1_kT[:, :], bank[1][:, P:2 * P])
            copy(w1_oT[:, :], bank[1][:, 2 * P:3 * P]).then_inc(sm["wT_copied"], 1)
            act.wait_ge(sm["vecT_done"], 1)
            copy(vec[:, :], bank[2][:, 0:NV]).then_inc(sm["vec_copied"], 1)

            def a_evac(g):
                act.wait_ge(sm["aT_done"], g + 1)
                copy(aT[:, toks(g)], bank[0]).then_inc(sm["aT_copied"], 1)

            def qk_evac(g):
                act.wait_ge(sm["vec_copied"], 1)
                act.wait_ge(sm["q_done"], g + 1)
                copy(qT[:, toks(g)], bank[1], ACT.Relu, bias=vec[:, V_BQ:V_BQ + 1]).then_inc(sm["qT_ready"], 1)
                act.wait_ge(sm["kv_done"], 2 * g + 1)
                t = g * GT
                kv = bank[2].rearrange("p (t c) -> p t c", t=2)
                copy(k_tok[:, t:t + 2, :], kv[:, :, 0:D], ACT.Relu)
                copy(v_tok[:, t:t + 2, 0:D], kv[:, :, D:2 * D]).then_inc(sm["kv0_ready"], 1)

            def b_evac(g):
                act.wait_ge(sm["bT_done"], g + 1)
                copy(bT[:, toks(g)], bank[7]).then_inc(sm["bT_copied"], 1)

            staggered([None, a_evac, qk_evac, None, None, None, None, None, None, b_evac], G)

            act.wait_ge(sm["shifted_ready"], 1)
            copy(expd[:, :, :], shifted[:, :, :], ACT.Exp).then_inc(sm["exp_ready"], 1)

            for h in range(2):
                act.wait_ge(sm["lbT_done"], h + 1)
                copy(lora_bT[:, 3 * h:3 * h + 3, :], bank[1 + h][0:R, 0:3 * P].rearrange("p (a b) -> p a b", a=3)).then_inc(sm["lbT_copied"], 1)
            act.wait_ge(sm["vo_done"], 1)
            copy(w1_vo[:, :], bank[3][:, 0:P]).then_inc(sm["vo_copied"], 1)
            act.wait_ge(sm["bo_done"], 1)
            copy(bo_all[:, :], bank[3][:, 0:P]).then_inc(sm["bo_copied"], 1)
            for h in range(2):
                act.wait_ge(sm["eff_done"], h + 1)
                copy(w_effT[:, 3 * h:3 * h + 3, :], bank[5 + h][:, 0:3 * P].rearrange("p (a b) -> p a b", a=3)).then_inc(sm["eff_copied"], 1)

            for e in range(E):
                for j in range(J):
                    act.wait_ge(sm["h_done"], e * J + j + 1)
                    if j == 0 and e >= 2:
                        act.wait_ge(sm["y_done"], e - 1)
                    copy(hT[:, e % 2, j, :], bank[2 + j], ACT.Gelu,
                         bias=vec[:, V_B1 + e * J + j:V_B1 + e * J + j + 1]).then_inc(sm["h_ready"], 1)

            def c_evac(g):
                act.wait_ge(sm["cT_done"], g + 1)
                copy(cT[:, toks(g)], bank[0]).then_inc(sm["cT_copied"], 1)

            def qk1_evac(g):
                act.wait_ge(sm["q1_done"], g + 1)
                copy(q1T[:, toks(g)], bank[1], ACT.Identity, bias=vec[:, V_BQ1:V_BQ1 + 1]).then_inc(sm["q1_ready"], 1)
                act.wait_ge(sm["k1_done"], g + 1)
                copy(k1T[:, toks(g)], bank[2], ACT.Identity, bias=vec[:, V_BK1:V_BK1 + 1]).then_inc(sm["k1_ready"], 1)

            def exps(g):
                act.wait_ge(sm["smax_ready"], g + 1)
                for t in tiles(g):
                    i = t - g * GT
                    ins = copy(prob[:, t, :], bank[4 + i // 2][:, (i % 2) * S:(i % 2 + 1) * S], ACT.Exp,
                               bias=nsmax[:, t:t + 1], scale=ATT_SCALE, accum_out=psum_p[:, t:t + 1])
                ins.then_inc(sm["p_ready"], 1)

            def p_evac(g):
                act.wait_ge(sm["pT_done"], GB * g + GB)
                copy(probT[:, GB * g + 1, :, :], bank[7].rearrange("p (k q) -> p k q", k=BT)).then_inc(sm["pT1_copied"], 1)

            def d_evac(g):
                act.wait_ge(sm["dT_done"], g + 1)
                copy(h_T[0][:, toks(g)], bank[0]).then_inc(sm["dT_copied"], 1)

            def gelu(k):
                def run(g):
                    act.wait_ge(nT_done[k], g + 1)
                    if k:
                        act.wait_ge(res_done[k - 1], g + 1)
                    copy(g_T[:, toks(g)], bank[4 + (g + k) % 2], ACT.Gelu, scale=vec[:, V_G + k:V_G + k + 1],
                         bias=vec[:, V_BE + k:V_BE + k + 1]).then_inc(gelu_ready[k], 1)
                return run

            def gelu_last(g):
                gelu(2)(g)
                act.wait_ge(sm["fin_done"], g + 1)
                copy(h_out[:, g * GT:(g + 1) * GT, :], bank[0].rearrange("p (t d) -> p t d", t=GT)).then_inc(sm["fin_ready"], 1)

            staggered([None, None, None, c_evac, qk1_evac, exps, p_evac, None, None, None, d_evac,
                       None, gelu(0), None, gelu(1), None, gelu_last, None, None], G)

        @block.tensor
        def _(pe):
            tenant = {}

            def claim(b, leaves, count):
                if b in tenant:
                    pe.wait_ge(*tenant[b])
                tenant[b] = (leaves, count)
                return bank[b]

            def mm(out, lhsT, rhs, start=True, stop=True):
                return pe.matmul(out, lhsT, rhs, start=start, stop=stop)

            def turn(out, in_, n=P):
                return pe.transpose(out, in_, ident[0:n, 0:n])

            def turn4(o, src, g, done):
                for i, t in enumerate(tiles(g)):
                    ins = turn(o[:, i * P:(i + 1) * P], src[:, t, 0:P])
                ins.then_inc(done, 1)

            pe.wait_ge(sm["ones_set"], 1)
            pe.wait_ge(sm["ld_w"], 16 * 7)
            o = claim(0, sm["wT_copied"], 1)
            for i in range(3):
                ins = turn(o[:, i * P:(i + 1) * P], w_raw[:, i, :])
            ins.then_inc(sm["wT_done"], 1)
            o = claim(1, sm["wT_copied"], 2)
            for i, w in enumerate((3, 4, 6)):
                ins = turn(o[:, i * P:(i + 1) * P], w_raw[:, w, :])
            ins.then_inc(sm["wT_done"], 1)
            pe.wait_ge(sm["ld_vec"], 16 * 8)
            turn(claim(2, sm["vec_copied"], 1)[:, 0:NV], vec_rows[:, :], NV).then_inc(sm["vecT_done"], 1)

            def a_turn(g):
                pe.wait_ge(sm["a_ready"], g + 1)
                turn4(claim(0, sm["aT_copied"], g + 1), a_tok, g, sm["aT_done"])

            def a_proj(g):
                pe.wait_ge(sm["aT_copied"], g + 1)
                mm(claim(1, sm["qT_ready"], g + 1), w_qT[:, :], aT[:, toks(g)]).then_inc(sm["q_done"], 1)
                pe.wait_ge(sm["bias_ready"], 1)
                pe.wait_ge(sm["consts"], 1)
                for i in range(2):
                    o = claim(2 + i, sm[f"kv{i}_ready"], g + 1)
                    for j in range(2):
                        t = g * GT + 2 * i + j
                        oj = o[:, j * 2 * D:(j + 1) * 2 * D]
                        mm(oj, aT[:, t * P:(t + 1) * P], w_kvT[:, :, :].rearrange("p a b -> p (a b)"), True, False)
                        ins = mm(oj, ones3[:, :], bias3[:, R_KV:R_KV + 2 * D], False, True)
                    ins.then_inc(sm["kv_done"], 1)

            def a_mix(g):
                pe.wait_ge(sm["kv0_ready"], g + 1)
                pe.wait_ge(sm["kv1_ready"], g + 1)
                if g == 0:
                    pe.wait_ge(sm["ones_set"], 2)
                o = claim(4, sm["kv_ready"], g + 1)
                for b in range(GB):
                    for i in range(BT):
                        t = g * GT + b * BT + i
                        ins = mm(o[:, b * 256:b * 256 + D + 1], k_tok[:, t, :], v_tok[:, t, 0:D + 1], i == 0, i == BT - 1)
                ins.then_inc(sm["ksum_done"], 1)
                pe.wait_ge(sm["kv_ready"], g + 1)
                pe.wait_ge(sm["qT_ready"], g + 1)
                o2 = [claim(5 + i, sm["y0_ready"], g + 1) for i in range(2)]
                for i, t in enumerate(tiles(g)):
                    ins = mm(o2[i // 2][:, (i % 2) * 256:(i % 2) * 256 + D + H], qT[:, t * P:(t + 1) * P], kv_blk[:, t // BT, :])
                ins.then_inc(sm["ctx_done"], 1)

            def b_turn(g):
                pe.wait_ge(sm["b_ready"], g + 1)
                turn4(claim(7, sm["bT_copied"], g + 1), tab, g, sm["bT_done"])
                pe.wait_ge(sm["bT_copied"], g + 1)
                if g == 0:
                    pe.wait_ge(sm["ld_small"], 64)
                    claim(0, sm["shifted_ready"], 1)
                for t in tiles(g):
                    ins = mm(bank[0][:, t * E:(t + 1) * E], bT[:, t * P:(t + 1) * P], wr[:, :])
                ins.then_inc(sm["logit_done"], 1)

            staggered([None, a_turn, a_proj, a_mix, None, None, None, None, None, b_turn], G)

            pe.wait_ge(sm["scores_ready"], 1)
            turn(claim(7, sm["scoreT_ready"], 1)[:, 0:P], sc_et[:, :, :].rearrange("p e t -> p (e t)")).then_inc(sm["scoreT_done"], 1)

            def lora_turn(h):
                def run():
                    pe.wait_ge(sm["ld_lora"], 32)
                    o = claim(1 + h, sm["lbT_copied"], h + 1)
                    for i in range(3):
                        ins = turn(o[0:R, i * P:(i + 1) * P], lora_b[:, 3 * h + i, :])
                    ins.then_inc(sm["lbT_done"], 1)
                return run

            def value_out():
                mm(claim(3, sm["vo_copied"], 1)[:, 0:P], w_raw[:, 5, :], w1_oT[:, :]).then_inc(sm["vo_done"], 1)

            def bias_out():
                pe.wait_ge(sm["bv_ready"], 1)
                pe.wait_ge(sm["ld_small"], 64)
                o = claim(3, sm["bo_copied"], 1)[:, 0:P]
                mm(o, bv_cols[:, :], w1_oT[:, :], True, False)
                mm(o, ones_row[:, :], bo_row[:, :], False, True).then_inc(sm["bo_done"], 1)

            def effective(i):
                def run():
                    if i == 0:
                        pe.wait_ge(sm["q_ready"], 1)
                        pe.wait_ge(sm["lbT_copied"], 2)
                    if i % 3 == 0:
                        claim(5 + i // 3, sm["eff_copied"], i // 3 + 1)
                    o = bank[5 + i // 3][:, (i % 3) * P:(i % 3 + 1) * P]
                    mm(o, q_ws[:, i, :], ident[:, :], True, False)
                    ins = mm(o, lora_a[:, i, :], lora_bT[:, i, :], False, True)
                    if i % 3 == 2:
                        ins.then_inc(sm["eff_done"], 1)
                return run

            between = dict(zip(range(6, SCORE_BITS, 2),
                               [lora_turn(0), lora_turn(1), value_out, bias_out] + [effective(i) for i in range(NL)]))
            for k in range(SCORE_BITS):
                pe.wait_ge(sm["cand_counted"], k + 1)
                o = claim(0, sm["cand_taken"], k + 1) if k else claim(0, sm["cand_taken"], 1)
                mm(o[:, 0:1], same_expert[:, :], hit_count[:, :]).then_inc(sm["cand_summed"], 1)
                if k in between:
                    between[k]()
            pe.wait_ge(sm["sel_counted"], 1)
            o = claim(0, sm["room_ready"], 1)
            mm(o[:, 0:1], same_expert[:, :], above_count[:, :])
            mm(o[:, 1:2], tile_before[:, :], tied_count[:, :]).then_inc(sm["sel_summed"], 1)
            pe.wait_ge(sm["kept_counted"], 1)
            mm(claim(7, sm["first_ready"], 1)[:, 0:1], tile_before[:, :], kept_count[:, :]).then_inc(sm["kept_summed"], 1)
            pe.wait_ge(sm["slots_ready"], 1)
            rbe = rank_by_expert[:, :, :].rearrange("p e k -> p (e k)")
            for c in range(SC):
                o2 = [claim(2 * (c % 3) + h, sm["slots_used"], c + 1) for h in range(2)]
                for h in range(2):
                    ins = mm(o2[h], slot_row[:, c * P:(c + 1) * P], rbe[:, h * 512:(h + 1) * 512])
                ins.then_inc(sm["slots_done"], 1)
            o = claim(6, sm["token_ready"], 1)
            for c in range(SC):
                ins = mm(o[:, c * E:(c + 1) * E], slot_row[:, c * P:(c + 1) * P], tile_start[:, :])
            ins.then_inc(sm["start_done"], 1)

            def g_turn(e):
                pe.wait_ge(gathered[e % 4], 16 * SC * (e // 4 + 1))
                o = claim(e % 2, sm["gT_copied"], e + 1)
                for c in range(SC):
                    ins = turn(o[:, c * P:(c + 1) * P], xg[:, e, c, 0:D])
                ins.then_inc(sm["gT_done"], 1)

            def hidden(e):
                pe.wait_ge(sm["gT_copied"], e + 1)
                if e == 0:
                    pe.wait_ge(sm["ld_w1"], 16)
                for j in range(J):
                    mm(claim(2 + j, sm["h_ready"], e * J + j + 1), w1[:, e, j * P:(j + 1) * P],
                       xgT[:, e % 2, :]).then_inc(sm["h_done"], 1)

            def outer(e):
                pe.wait_ge(sm["h_ready"], (e + 1) * J)
                if e == 0:
                    pe.wait_ge(sm["ld_w2"], 16)
                o = claim(6 + e % 2, sm["yg_ready"], e + 1)
                for c in range(SC):
                    oc = o[:, c * D:(c + 1) * D]
                    for j in range(J):
                        mm(oc, hT[:, e % 2, j, c * P:(c + 1) * P], w2[:, e, j, :], j == 0, False)
                    ins = mm(oc, ones3[:, :], bias3[:, R_B2 + e * D:R_B2 + (e + 1) * D], False, True)
                ins.then_inc(sm["y_done"], 1)

            g_turn(0)
            for e in range(E):
                hidden(e)
                if e + 1 < E:
                    g_turn(e + 1)
                if e:
                    outer(e - 1)
            outer(E - 1)

            def c_turn(g):
                pe.wait_ge(sm["c_ready"], g + 1)
                turn4(claim(0, sm["cT_copied"], g + 1), c_tok, g, sm["cT_done"])

            def c_proj(g):
                pe.wait_ge(sm["cT_copied"], g + 1)
                mm(claim(1, sm["q1_ready"], g + 1), w1_qT[:, :], cT[:, toks(g)]).then_inc(sm["q1_done"], 1)
                mm(claim(2, sm["k1_ready"], g + 1), w1_kT[:, :], cT[:, toks(g)]).then_inc(sm["k1_done"], 1)
                o = claim(3, sm["v1_ready"], g + 1)
                for i, t in enumerate(tiles(g)):
                    ins = mm(o[:, i * D:(i + 1) * D], cT[:, t * P:(t + 1) * P], w1_vo[:, :])
                ins.then_inc(sm["v1_done"], 1)

            def c_score(g):
                pe.wait_ge(sm["q1_ready"], g + 1)
                pe.wait_ge(sm["k1_ready"], g + 1)
                o2 = [claim(4 + i, sm["p_ready"], g + 1) for i in range(2)]
                for i, t in enumerate(tiles(g)):
                    b = t // BT
                    ins = mm(o2[i // 2][:, (i % 2) * S:(i % 2 + 1) * S], q1T[:, t * P:(t + 1) * P], k1T[:, b * S:(b + 1) * S])
                ins.then_inc(sm["s_done"], 1)

            def c_pturn(g):
                pe.wait_ge(sm["p_ready"], g + 1)
                o2 = [claim(6, sm["pT0_copied"], g + 1), claim(7, sm["pT1_copied"], g + 1)]
                for b in range(GB):
                    for kb in range(BT):
                        for i in range(BT):
                            t = g * GT + b * BT + i
                            ins = turn(o2[b][:, kb * S + i * P:kb * S + (i + 1) * P], prob[:, t, kb * P:(kb + 1) * P])
                    ins.then_inc(sm["pT_done"], 1)

            def c_out(g):
                pe.wait_ge(sm["pT0_copied"], g + 1)
                pe.wait_ge(sm["pT1_copied"], g + 1)
                pe.wait_ge(sm["v1_ready"], g + 1)
                o = claim(0, sm["o_ready"], g + 1)
                for i, t in enumerate(tiles(g)):
                    b = t // BT
                    for kb in range(BT):
                        ins = mm(o[:, i * D:(i + 1) * D], probT[:, b, kb, (t % BT) * P:(t % BT + 1) * P],
                                 v1[:, b * BT + kb, :], kb == 0, kb == BT - 1)
                ins.then_inc(sm["o_done"], 1)

            def d_turn(g):
                pe.wait_ge(sm["d_ready"], g + 1)
                turn4(claim(0, sm["dT_copied"], g + 1), d_tok, g, sm["dT_done"])

            def linear(k):
                def run(g):
                    if k:
                        pe.wait_ge(hT_ready[k - 1], g + 1)
                    else:
                        pe.wait_ge(sm["dT_copied"], g + 1)
                    o = claim(1 + k, n_ready[k], g + 1)
                    for i, t in enumerate(tiles(g)):
                        oi = o[:, i * D:(i + 1) * D]
                        mm(oi, h_T[k][:, t * P:(t + 1) * P], w_effT[:, 2 * k, :], True, False)
                        ins = mm(oi, ones3[:, :], bias3[:, R_LIN + k * D:R_LIN + (k + 1) * D], False, True)
                    ins.then_inc(lin_done[k], 1)
                return run

            def n_turn(k, g):
                pe.wait_ge(n_ready[k], g + 1)
                turn4(claim(4 + (g + k) % 2, gelu_ready[k], g + 1), n_tok, g, nT_done[k])
                pe.wait_ge(gelu_ready[k], g + 1)

            def back(k):
                def run(g):
                    n_turn(k, g)
                    mm(claim(6 + (g + k) % 2, hT_ready[k], g + 1), w_effT[:, 2 * k + 1, :],
                       g_T[:, toks(g)]).then_inc(res_done[k], 1)
                return run

            def back_last(g):
                n_turn(2, g)
                o = claim(0, sm["fin_ready"], g + 1)
                for i, t in enumerate(tiles(g)):
                    oi = o[:, i * D:(i + 1) * D]
                    mm(oi, g_T[:, t * P:(t + 1) * P], w_effT[:, 5, :], True, False)
                    mm(oi, h_T[2][:, t * P:(t + 1) * P], ident[:, :], False, False)
                    ins = mm(oi, ones3[:, :], bias3[:, R_LIN + 3 * D:R_LIN + 4 * D], False, True)
                ins.then_inc(sm["fin_done"], 1)

            staggered([None, None, None, c_turn, c_proj, c_score, c_pturn, c_out, None, None, d_turn,
                       linear(0), back(0), linear(1), back(1), linear(2), back_last, None, None], G)

        @block.vector
        def _(dve):
            step = [0]

            def mark(ins):
                step[0] += 1
                ins.then_inc(sm["dve_step"], 1)

            def settle():
                dve.wait_ge(sm["dve_step"], step[0])

            def link(ins):
                mark(ins)
                settle()

            def layer_stats(n, src, g):
                L = ln[n]
                for i, t in enumerate(tiles(g)):
                    ins = dve.bn_stats(stats[:, t, :], src(i, t))
                link(ins)
                for t in tiles(g):
                    ins = dve.bn_aggr(L.mv[:, t, :], stats[:, t, :])
                ins.then_inc(L.stats_ready, 1)

            def normalise(n, dst, src, g, done):
                L = ln[n]
                dve.wait_ge(L.rstd_ready, g + 1)
                for i, t in enumerate(tiles(g)):
                    ins = dve.tensor_scalar(dst[:, t, 0:D], src(i, t), L.mv[:, t, 0:1], L.rstd[:, t:t + 1],
                                            ALU.subtract, ALU.mult)
                ins.then_inc(done, 1)

            def of(tensor):
                return lambda i, t: tensor[:, t, 0:D]

            def of_bank(b):
                return lambda i, t: bank[b][:, i * D:(i + 1) * D]

            dve.wait_ge(sm["ld_bias"], 16 * 7)
            dve.wait_ge(sm["ones_set"], 1)
            link(dve.tensor_copy(bias_hi[:, :], bias_rows[:, :]))
            link(dve.tensor_tensor(bias_rows[:, :], bias_rows[:, :], bias_hi[:, :], ALU.subtract))
            link(dve.tensor_copy(bias_mid[:, :], bias_rows[:, :]))
            link(dve.tensor_tensor(bias_rows[:, :], bias_rows[:, :], bias_mid[:, :], ALU.subtract))
            link(dve.tensor_copy(bias_lo[:, :], bias_rows[:, :]))
            link(dve.tensor_scalar(bias_hi[:, :], bias_hi[:, :], ident[0:3, 0:1], None, ALU.mult))
            link(dve.scalar_tensor_tensor(bias_hi[:, :], bias_mid[:, :], ident[0:3, 1:2], bias_hi[:, :], ALU.mult, ALU.add))
            dve.scalar_tensor_tensor(bias3[:, :], bias_lo[:, :], ident[0:3, 2:3], bias_hi[:, :], ALU.mult, ALU.add).then_inc(sm["bias_ready"], 1)

            def a_stats(g):
                dve.wait_ge(ld_x[g], 16)
                layer_stats("a_in", of(x0), g)

            def a_norm(g):
                normalise("a_in", a_tok, of(x0), g, sm["a_ready"])

            def kv_evac(g):
                dve.wait_ge(sm["kv_done"], 2 * g + 2)
                t = g * GT + 2
                kv = bank[3].rearrange("p (t c) -> p t c", t=2)
                dve.tensor_scalar(k_tok[:, t:t + 2, :], kv[:, :, 0:D], 0.0, None, ALU.max)
                dve.tensor_copy(v_tok[:, t:t + 2, 0:D], kv[:, :, D:2 * D]).then_inc(sm["kv1_ready"], 1)

            def kv_mask(g):
                dve.wait_ge(sm["ksum_done"], g + 1)
                dve.wait_ge(sm["consts"], 1)
                kv = bank[4].rearrange("p (b c) -> p b c", b=GB)
                bs = slice(g * GB, (g + 1) * GB)
                dve.tensor_tensor(kv_blk[:, bs, 0:D], kv[:, :, 0:D],
                                  head_block[:, :].unsqueeze(1).to_broadcast([P, GB, D]), ALU.mult)
                dve.tensor_tensor(kv_blk[:, bs, D:D + H], kv[:, :, D:D + 1].to_broadcast([P, GB, H]),
                                  head_col[:, :].unsqueeze(1).to_broadcast([P, GB, H]), ALU.mult).then_inc(sm["kv_ready"], 1)

            def divide(g):
                dve.wait_ge(sm["ctx_done"], g + 1)
                c = slice(g * GT, (g + 1) * GT)
                o = banks[:, 5:7, :].rearrange("p b (i c) -> p (b i) c", i=2)
                link(dve.tensor_scalar(den[:, c, :], o[:, :, D:D + H], DENOM_EPS, None, ALU.max))
                link(dve.reciprocal(rden[:, c, :], den[:, c, :]))
                for i, t in enumerate(tiles(g)):
                    ins = dve.tensor_tensor(y0[:, t, :].rearrange("p (h d) -> p h d", h=H),
                                            o[:, i, 0:D].rearrange("p (h d) -> p h d", h=H),
                                            rden[:, t, :].unsqueeze(2).to_broadcast([P, H, HD]), ALU.mult)
                ins.then_inc(sm["y0_ready"], 1)

            def mid_stats(g):
                dve.wait_ge(sm["y1_ready"], g + 1)
                layer_stats("a_mid", of(y1), g)

            def mid_norm(g):
                L = ln["a_mid"]
                dve.wait_ge(sm["ld_small"], 64)
                for t in tiles(g):
                    ins = dve.scalar_tensor_tensor(z[:, t, :], y1[:, t, :], L.mv[:, t, 0:1], gamma_all[:, :], ALU.subtract, ALU.mult)
                mark(ins)
                dve.wait_ge(L.rstd_ready, g + 1)
                settle()
                for t in tiles(g):
                    ins = dve.scalar_tensor_tensor(z[:, t, :], z[:, t, :], L.rstd[:, t:t + 1], beta_all[:, :], ALU.mult, ALU.add)
                link(ins)
                layer_stats("a_out", of(z), g)

            def a_out(g):
                normalise("a_out", u, of(z), g, sm["u_ready"])

            def b_stats(g):
                dve.wait_ge(sm["x1_ready"], g + 1)
                layer_stats("b_in", of(x1), g)

            def b_norm(g):
                normalise("b_in", tab, of(x1), g, sm["b_ready"])

            staggered([a_stats, a_norm, kv_evac, kv_mask, divide, mid_stats, mid_norm, a_out, b_stats, b_norm], G)

            dve.wait_ge(sm["vec_copied"], 1)
            dve.tensor_scalar(bv_cols[:, :], zeros[:, 0:P], vec[:, V_BV1:V_BV1 + 1], None, ALU.add).then_inc(sm["bv_ready"], 1)
            dve.wait_ge(sm["logit_done"], G)
            logits = bank[0][:, 0:T * E].rearrange("p (t e) -> p t e", t=T)
            spread = lambda v: v.unsqueeze(2).to_broadcast([P, T, E])
            link(dve.tensor_reduce(logit_max[:, :], logits, AX.X, ALU.max))
            dve.tensor_tensor(shifted[:, :, :], logits, spread(logit_max[:, :]), ALU.subtract).then_inc(sm["shifted_ready"], 1)
            dve.wait_ge(sm["exp_ready"], 1)
            link(dve.tensor_reduce(expsum[:, :], expd[:, :, :], AX.X, ALU.add))
            link(dve.reciprocal(rexpsum[:, :], expsum[:, :]))
            link(dve.tensor_tensor(tab[:, :, D:ROW], expd[:, :, :], spread(rexpsum[:, :]), ALU.mult))
            dve.tensor_copy(sc_et[:, :, :], tab[:, :, D:ROW].rearrange("p t e -> p e t")).then_inc(sm["scores_ready"], 1)

            mark(dve.memset(cand[:, :], 1 << (SCORE_BITS - 1)))
            dve.wait_ge(sm["scoreT_done"], 1)
            dve.tensor_copy(scoreT[:, :], bank[7][:, 0:P]).then_inc(sm["scoreT_ready"], 1)
            dve.wait_ge(sm["scoreT_ready"], 1)
            settle()
            for k in range(SCORE_BITS):
                bit = SCORE_BITS - 1 - k
                now, then = cand[:, k % 2:k % 2 + 1], cand[:, (k + 1) % 2:(k + 1) % 2 + 1]
                dve.tensor_scalar(hits[:, :], scoreT[:, :], now.bitcast(F32), None, ALU.is_ge, ALU.add,
                                  accum_out=hit_count[:, :]).then_inc(sm["cand_counted"], 1)
                mark(dve.tensor_scalar(then, now, (1 << bit) >> 1, None, ALU.bitwise_xor))
                dve.wait_ge(sm["cand_summed"], k + 1)
                dve.tensor_scalar(below[:, :], bank[0][:, 0:1], float(KEEP) - 0.5, None, ALU.is_lt).then_inc(sm["cand_taken"], 1)
                dve.wait_ge(sm["cand_taken"], k + 1)
                settle()
                link(dve.scalar_tensor_tensor(then, below[:, :], bit, then, ALU.logical_shift_left, ALU.bitwise_xor))
            cut = cand[:, SCORE_BITS % 2:SCORE_BITS % 2 + 1].bitcast(F32)

            dve.tensor_scalar(above[:, :], scoreT[:, :], cut, None, ALU.is_gt, ALU.add, accum_out=above_count[:, :])
            mark(dve.tensor_scalar(tied[:, :], scoreT[:, :], cut, None, ALU.is_equal, ALU.add, accum_out=tied_count[:, :]))
            settle()
            dve.tensor_tensor_scan(tie_rank[:, :], tied[:, :], zeros[:, 0:P], 0.0, ALU.add, ALU.add).then_inc(sm["sel_counted"], 1)
            dve.wait_ge(sm["sel_summed"], 1)
            dve.wait_ge(sm["sel_counted"], 1)
            link(dve.tensor_scalar(tie_room[:, 0:1], bank[0][:, 0:1], -1.0, float(KEEP), ALU.mult, ALU.add))
            dve.tensor_tensor(tie_room[:, 1:2], tie_room[:, 0:1], bank[0][:, 1:2], ALU.subtract).then_inc(sm["room_ready"], 1)
            dve.wait_ge(sm["room_ready"], 1)
            link(dve.scalar_tensor_tensor(tie_kept[:, :], tie_rank[:, :], tie_room[:, 1:2], tied[:, :], ALU.is_le, ALU.mult))
            link(dve.tensor_tensor_scan(kept_rank[:, :], above[:, :], tie_kept[:, :], 0.0, ALU.add, ALU.add))
            dve.tensor_copy(kept_count[:, :], kept_rank[:, P - 1:P]).then_inc(sm["kept_counted"], 1)
            dve.wait_ge(sm["kept_summed"], 1)
            dve.tensor_copy(kept_first[:, :], bank[7][:, 0:1]).then_inc(sm["first_ready"], 1)
            dve.wait_ge(sm["first_ready"], 1)
            dve.tensor_scalar(rank_all[:, :], kept_rank[:, :], kept_first[:, :], None, ALU.add)
            link(dve.tensor_scalar(rank_last[:, :], kept_rank[:, P - 1:P], kept_first[:, :], None, ALU.add))
            dve.tensor_tensor(rank_by_expert[:, :, :], own_expert[:, :].unsqueeze(2).to_broadcast([P, E, P]),
                              rank_all[:, :].unsqueeze(1).to_broadcast([P, E, P]), ALU.mult)
            link(dve.tensor_scalar(from_first[:, :], slot_free[:, :], kept_first[:, :], None, ALU.is_ge))
            dve.scalar_tensor_tensor(slot_row[:, :], slot_free[:, :], rank_last[:, :], from_first[:, :], ALU.is_lt, ALU.mult).then_inc(sm["slots_ready"], 1)
            for c in range(SC):
                b = 2 * (c % 3)
                dve.wait_ge(sm["slots_done"], c + 1)
                dve.tensor_scalar(passed[:, :, :], banks[:, b:b + 2, :].rearrange("p b (e k) -> p (b e) k", k=P),
                                  slot_part[:, c:c + 1], None, ALU.is_le).then_inc(sm["slots_used"], 1)
                dve.wait_ge(sm["slots_used"], c + 1)
                link(dve.tensor_reduce(passed_count[:, c, :], passed[:, :, :], AX.X, ALU.add))
            dve.wait_ge(sm["start_done"], 1)
            dve.tensor_tensor(token_of[:, :, :], passed_count[:, :, :],
                              bank[6][:, 0:SC * E].rearrange("p (c e) -> p c e", c=SC), ALU.add).then_inc(sm["token_ready"], 1)

            def g_evac(e):
                if e >= 2:
                    dve.wait_ge(sm["h_done"], (e - 1) * J)
                dve.wait_ge(sm["gT_done"], e + 1)
                dve.tensor_copy(xgT[:, e % 2, :], bank[e % 2]).then_inc(sm["gT_copied"], 1)

            def gate(e):
                if e >= 2:
                    dve.wait_ge(scattered[e % 2], 16 * SC * (e // 2))
                dve.wait_ge(sm["y_done"], e + 1)
                for c in range(SC):
                    ins = dve.tensor_scalar(yg[:, e % 2, c, :], bank[6 + e % 2][:, c * D:(c + 1) * D],
                                            xg[:, e, c, D + e:D + e + 1], None, ALU.mult)
                ins.then_inc(sm["yg_ready"], 1)

            dve.wait_ge(gathered[0], 16 * SC)
            g_evac(0)
            for e in range(E):
                if e + 1 < E:
                    g_evac(e + 1)
                if e:
                    gate(e - 1)
            gate(E - 1)

            def c_first(g):
                dve.wait_ge(sm["moe_loaded"], 16)
                layer_stats("b_out", of(moe), g)

            def c_u(g):
                normalise("b_out", z, of(moe), g, sm["uc_ready"])

            def c_stats(g):
                dve.wait_ge(sm["x2_ready"], g + 1)
                layer_stats("c_in", of(x2), g)

            def c_norm(g):
                normalise("c_in", c_tok, of(x2), g, sm["c_ready"])

            def v1_evac(g):
                dve.wait_ge(sm["v1_done"], g + 1)
                dve.tensor_copy(v1[:, g * GT:(g + 1) * GT, :], bank[3].rearrange("p (t d) -> p t d", t=GT)).then_inc(sm["v1_ready"], 1)

            def score_max(g):
                c = slice(g * GT, (g + 1) * GT)
                dve.wait_ge(sm["s_done"], g + 1)
                link(dve.tensor_reduce(smax[:, c], banks[:, 4:6, :].rearrange("p b (i k) -> p (b i) k", k=S), AX.X, ALU.max))
                dve.tensor_scalar(nsmax[:, c], smax[:, c], -ATT_SCALE, None, ALU.mult).then_inc(sm["smax_ready"], 1)

            def p_evac(g):
                dve.wait_ge(sm["pT_done"], GB * g + 1)
                dve.tensor_copy(probT[:, GB * g, :, :], bank[6].rearrange("p (k q) -> p k q", k=BT)).then_inc(sm["pT0_copied"], 1)

            def o_norm(g):
                c = slice(g * GT, (g + 1) * GT)
                dve.wait_ge(sm["p_ready"], g + 1)
                mark(dve.reciprocal(rsum[:, c], psum_p[:, c]))
                dve.wait_ge(sm["bo_copied"], 1)
                dve.wait_ge(sm["o_done"], g + 1)
                settle()
                for i, t in enumerate(tiles(g)):
                    ins = dve.scalar_tensor_tensor(o_tok[:, t, :], bank[0][:, i * D:(i + 1) * D], rsum[:, t:t + 1],
                                                   bo_all[:, :], ALU.mult, ALU.add)
                ins.then_inc(sm["o_ready"], 1)
                dve.wait_ge(sm["o_ready"], g + 1)
                layer_stats("c_out", of(o_tok), g)

            def d_u(g):
                normalise("c_out", w_out, of(o_tok), g, sm["ud_ready"])

            def d_stats(g):
                dve.wait_ge(sm["x3_ready"], g + 1)
                layer_stats("d_in", of(x3), g)

            def d_norm(g):
                normalise("d_in", d_tok, of(x3), g, sm["d_ready"])

            def lin_stats(k):
                def run(g):
                    dve.wait_ge(lin_done[k], g + 1)
                    layer_stats(f"d{k}", of_bank(1 + k), g)
                return run

            def lin_norm(k):
                def run(g):
                    normalise(f"d{k}", n_tok, of_bank(1 + k), g, n_ready[k])
                    if k < 2:
                        dve.wait_ge(res_done[k], g + 1)
                        b = V_BIAS + 2 * k + 1
                        dve.scalar_tensor_tensor(h_T[k + 1][:, toks(g)], bank[6 + (g + k) % 2], vec[:, b:b + 1],
                                                 h_T[k][:, toks(g)], ALU.add, ALU.add).then_inc(hT_ready[k], 1)
                return run

            def out_stats(g):
                dve.wait_ge(sm["fin_ready"], g + 1)
                layer_stats("d_out", of(h_out), g)

            def out_norm(g):
                normalise("d_out", u, of(h_out), g, sm["uo_ready"])

            staggered([c_first, c_u, c_stats, c_norm, v1_evac, score_max, p_evac, o_norm, d_u, d_stats, d_norm,
                       lin_stats(0), lin_norm(0), lin_stats(1), lin_norm(1), lin_stats(2), lin_norm(2),
                       out_stats, out_norm], G)


_INS = ['L0_attn_x', 'L0_attn_Wq', 'L0_attn_bq', 'L0_attn_Wk', 'L0_attn_bk', 'L0_attn_Wv', 'L0_attn_bv',
        'L0_attn_gamma', 'L0_attn_beta', 'L0_ffn_Wr', 'L0_ffn_W1', 'L0_ffn_b1', 'L0_ffn_W2', 'L0_ffn_b2',
        'L1_attn_Wq', 'L1_attn_bq', 'L1_attn_Wk', 'L1_attn_bk', 'L1_attn_Wv', 'L1_attn_bv', 'L1_attn_Wo',
        'L1_attn_bo', 'L1_ffn_qweights', 'L1_ffn_scales', 'L1_ffn_biases', 'L1_ffn_lora_a', 'L1_ffn_lora_b',
        'L1_ffn_ln_gamma', 'L1_ffn_ln_beta']


def kernel(**inputs):
    import numpy as _np
    import concourse.bacc as _bacc
    from concourse import mybir as _mybir
    from concourse.bass_utils import run_bass_kernel_spmd as _run

    nc = _bacc.Bacc("TRN2", target_bir_lowering=False, num_devices=1)
    arrays, args = {}, {}
    for name in _INS:
        x = _np.ascontiguousarray(inputs[name])
        arrays[f"in_{name}_dram"] = x
        args[name] = nc.dram_tensor(f"in_{name}_dram", x.shape, _mybir.dt.from_np(x.dtype), kind="ExternalInput").ap()
    shape = inputs["L0_attn_x"].shape
    args["out"] = nc.dram_tensor("out_0_dram", shape, _mybir.dt.float32, kind="ExternalOutput").ap()
    sandwich_kernel(nc, args)
    r = _run(nc, [arrays], core_ids=[0])
    return r.results[0]["out_0_dram"]
```

```python
from contextlib import ExitStack

import concourse.bass as bass
from concourse import mybir

ALU = mybir.AluOpType
ACT = mybir.ActivationFunctionType
AX = mybir.AxisListType
F32 = mybir.dt.float32
F16 = mybir.dt.float16
BF16 = mybir.dt.bfloat16
I32 = mybir.dt.int32
U32 = mybir.dt.uint32

P = 128
LN_EPS = 1e-5
DENOM_EPS = 1e-6
SCORE_BITS = 30


def flow(beats, every, groups, **steps):
    for _, g, name in sorted((beats[name] + every * g, g, name) for name in steps for g in range(groups)):
        steps[name](g)


def sandwich_kernel(nc, a):
    B, S, D = a["L0_attn_x"].shape
    E, _, HID = a["L0_ffn_W1"].shape
    N = B * S
    T = N // P
    GT = 4
    G = T // GT
    GN = GT * P
    BT = S // P
    GB = GT // BT
    H = 16
    HD = D // H
    KEEP = max(4, -(-N * 2 // E))
    SC = KEEP // P
    J = HID // P
    ROW = D + E
    NL = a["L1_ffn_qweights"].shape[0]
    R = a["L1_ffn_lora_a"].shape[1]
    NS = a["L1_ffn_scales"].shape[2]
    ATT_SCALE = 1.0 / float(D // 2) ** 0.5
    assert D == P and E * T == P and GT % BT == 0 and KEEP % P == 0

    ctx = ExitStack()
    with ctx:
        def sb(name, shape, dt=F32):
            return ctx.enter_context(nc.sbuf_tensor(name, shape, dt))

        def ps(name, shape, dt=F32):
            return ctx.enter_context(nc.psum_tensor(name, shape, dt))

        def sem(name):
            return ctx.enter_context(nc.semaphore(name))

        table = nc.dram_tensor("token_table", [N, ROW], F32, kind="Internal").ap()
        moe_sum = nc.dram_tensor("moe_sum", [N, D], F32, kind="Internal").ap()

        ident = sb("ident", [P, P])
        head_block = sb("head_block", [P, P])
        head_col = sb("head_col", [P, H])
        same_expert = sb("same_expert", [P, P], BF16)
        tile_before = sb("tile_before", [P, P], BF16)
        own_expert = sb("own_expert", [P, E], F16)
        tile_start_i = sb("tile_start_i", [P, E], I32)
        tile_start = sb("tile_start", [P, E], F16)
        tile_start_f = sb("tile_start_f", [P, E])
        slot_i = sb("slot_i", [P, KEEP], I32)
        slot_free = sb("slot_free", [P, KEEP])
        slot_part_i = sb("slot_part_i", [P, SC], I32)
        slot_part = sb("slot_part", [P, SC])
        zeros = sb("zeros", [P, T * D])
        ones3 = sb("ones3", [3, P], BF16)
        ones_row = sb("ones_row", [1, P])
        minus_half = sb("minus_half", [P, GT])

        w_raw = sb("w_raw", [P, 7, P])
        w_qT = sb("w_qT", [P, P])
        w_kvT = sb("w_kvT", [P, 2, P])
        w1_qT = sb("w1_qT", [P, P])
        w1_kT = sb("w1_kT", [P, P])
        w1_oT = sb("w1_oT", [P, P])
        w1_vo = sb("w1_vo", [P, P])
        bv_cols = sb("bv_cols", [P, P])
        bo_row = sb("bo_row", [1, P])
        bo_all = sb("bo_all", [P, P])
        NV = 32 + 15
        bq_col = sb("bq_col", [P, 1])
        vec_rows = sb("vec_rows", [NV, P])
        vec = sb("vec", [P, NV])
        NB = 2 * D + E * D + 4 * D
        NR = NB // D
        bias_rows = sb("bias_rows", [NR, D])
        bias_mean = sb("bias_mean", [NR, 1])
        centred = sb("centred", [NR, 1])
        bias_hi = sb("bias_hi", [NR, D], BF16)
        bias_mid = sb("bias_mid", [NR, D], BF16)
        bias_lo = sb("bias_lo", [NR, D], BF16)
        w_sum = sb("w_sum", [P, NL])
        w_nmean = sb("w_nmean", [P, NL])
        bias3 = sb("bias3", [3, NB], BF16)
        gamma_all = sb("gamma_all", [P, D])
        beta_all = sb("beta_all", [P, D])
        wr = sb("wr", [P, E])
        w1 = sb("w1", [P, E, HID])
        w2 = sb("w2", [P, E, J, D])
        q_int = sb("q_int", [P, NL, D], I32)
        q_scale = sb("q_scale", [P, NL, NS])
        q_w = sb("q_w", [P, NL, D])
        q_ws = sb("q_ws", [P, NL, D])
        lora_a = sb("lora_a", [R, NL, D])
        lora_b = sb("lora_b", [P, NL, R])
        lora_bT = sb("lora_bT", [R, NL, D])
        w_effT = sb("w_effT", [P, NL, D])

        x0 = sb("x0", [P, T, D])
        a_tok = sb("a_tok", [P, T, D])
        hT = sb("hT", [P, 2, J, KEEP])
        hT_flat = hT[:, :, :, :].rearrange("p a j k -> p (a j k)")
        aT = hT_flat[:, 0:T * P]
        qT = hT_flat[:, T * P:2 * T * P]
        xg = sb("xg", [P, E, SC, ROW])
        xg_flat = xg[:, :, :, :].rearrange("p e c r -> p (e c r)")
        k_tok = xg_flat[:, 0:T * D].rearrange("p (t d) -> p t d", d=D)
        VW = D + 4
        v_tok = xg_flat[:, T * D:T * (D + VW)].rearrange("p (t d) -> p t d", d=VW)
        kv_blk = sb("kv_blk", [P, B, D + H])
        den = sb("den", [P, T, H])
        rden = sb("rden", [P, T, H])
        y0 = sb("y0", [P, T, D])
        y1 = sb("y1", [P, T, D])
        z = sb("z", [P, T, D])
        u = y0
        x1 = sb("x1", [P, T, D])
        tab = sb("tab", [P, T, ROW])
        bT = sb("bT", [P, T * P])
        stats = sb("stats", [P, T, 6])

        class Norm:
            def __init__(self, name):
                self.mv = sb(f"mv_{name}", [P, T, 2])
                self.ve = sb(f"ve_{name}", [P, T])
                self.rstd = sb(f"rstd_{name}", [P, T])
                self.nmean = sb(f"nmean_{name}", [P, T])
                self.shift = sb(f"shift_{name}", [P, T])
                self.stats_ready = sem(f"stats_{name}")
                self.rstd_ready = sem(f"rstd_{name}_ready")

        ln = {n: Norm(n) for n in ("a_in", "a_mid", "a_out", "b_in", "b_out", "c_in", "c_out",
                                   "d_in", "d0", "d1", "d2", "d_out")}

        logit_max = sb("logit_max", [P, T])
        shifted = sb("shifted", [P, T, E])
        expd = sb("expd", [P, T, E])
        expsum = sb("expsum", [P, T])
        rexpsum = sb("rexpsum", [P, T])
        sc_et = sb("sc_et", [P, E, T])
        scoreT = sb("scoreT", [P, P])
        cand = sb("cand", [P, 2], I32)
        below = sb("below", [P, 1], I32)
        hits = sb("hits", [P, P], BF16)
        hit_count = sb("hit_count", [P, 1], BF16)
        above = sb("above", [P, P], BF16)
        tied = sb("tied", [P, P], BF16)
        above_count = sb("above_count", [P, 1], BF16)
        tied_count = sb("tied_count", [P, 1], BF16)
        tie_room = sb("tie_room", [P, 2])
        tie_rank = sb("tie_rank", [P, P])
        tie_kept = sb("tie_kept", [P, P])
        kept_rank = sb("kept_rank", [P, P])
        kept_count = sb("kept_count", [P, 1], BF16)
        kept_first = sb("kept_first", [P, 1])
        rank_all = sb("rank_all", [P, P], F16)
        rank_last = sb("rank_last", [P, 1])
        rank_by_expert = sb("rank_by_expert", [P, E, P], F16)
        from_first = sb("from_first", [P, KEEP], F16)
        slot_row = sb("slot_row", [P, KEEP], F16)
        passed = sb("passed", [P, 2, SC, P], BF16)
        passed_count = sb("passed_count", [P, SC, E])
        first_token = sb("first_token", [P, SC, E])
        token_of = sb("token_of", [P, SC, E], U32)

        SLOT_BANKS = (0, 1, 2, 3, 4, 5, 7, 0)

        a_flat = a_tok[:, :, :].rearrange("p t d -> p (t d)")
        xgT = a_flat[:, 0:2 * KEEP].rearrange("p (a k) -> p a k", a=2)
        yg = a_flat[:, 2 * KEEP:2 * KEEP + 2 * SC * D].rearrange("p (a c d) -> p a c d", a=2, c=SC)
        moe = y1

        x2 = x0
        c_tok = a_tok
        cT = aT
        q1T = qT
        k1T = xg_flat[:, T * D:2 * T * D]
        v1 = k_tok
        smax = sb("smax", [P, T])
        nsmax = sb("nsmax", [P, T])
        prob = w1[:, :, :].rearrange("p e h -> p (e h)").rearrange("p (t s) -> p t s", s=S)
        psum_p = sb("psum_p", [P, T])
        rsum = sb("rsum", [P, T])
        probT = w2[:, :, :, :].rearrange("p e j d -> p (e j d)").rearrange("p (b k q) -> p b k q", b=B, k=BT)
        o_tok = y0
        x3 = x1
        d_tok = y0
        h_T = [bT, q1T, k1T]
        n_tok = y1
        g_T = aT
        w_out = z
        h_out = z
        y_out = zeros[:, :].rearrange("p (t d) -> p t d", d=D)

        banks = ps("banks", [P, 8, 512])
        bank = [banks[:, i, :] for i in range(8)]

        names = """consts ones_set heads_set experts_set ld_bq
        ld_w0 ld_w ld_vec ld_bias ld_small ld_experts ld_lin ld_bo
        prep_done prep_copied q_ready bv_ready fin_done fin_ready
        eff_mean bias_parts bias_ready centred_set
        a_ready aT_done aT_copied q_done qT_ready kv0_done kv1_done kv0_ready kv1_ready ksum_done kv_ready ctx_done y0_ready y1_ready mid_ready
        u_ready x1_ready
        b_ready bT_done bT_copied logit_done shifted_ready exp_ready scores_ready scoreT_done scoreT_ready
        cand_counted cand_summed cand_taken room_ready first_ready sel_counted sel_summed kept_counted kept_summed slots_ready slots_done slots_used start_done first_token_ready
        token_ready table_written zero_written moe_loaded
        gT_done gT_copied h_done h_ready y_done yg_ready
        uc_ready x2_ready c_ready cT_done cT_copied q1_done q1_ready k1_done k1_ready v1_done v1_ready
        s_done smax_ready p_ready pT_done pT0_copied pT1_copied o_done o_ready ud_ready x3_ready
        d_ready dT_done dT_copied uo_ready out_ready out_written
        dve_step pool_step""".split()
        sm = {n: sem(n) for n in names}
        ld_x = [sem(f"ld_x{g}") for g in range(G)]
        gathered = [sem(f"gathered{i}") for i in range(4)]
        scattered = [sem(f"scattered{i}") for i in range(2)]
        lin_done = [sem(f"lin_done{k}") for k in range(3)]
        n_ready = [sem(f"n_ready{k}") for k in range(3)]
        nT_done = [sem(f"nT_done{k}") for k in range(3)]
        gelu_ready = [sem(f"gelu_ready{k}") for k in range(3)]
        res_done = [sem(f"res_done{k}") for k in range(2)]
        hT_ready = [sem(f"hT_ready{k}") for k in range(2)]

        x_dram = a["L0_attn_x"].rearrange("b (t p) d -> p (b t) d", p=P)
        out_dram = a["out"].rearrange("b (t p) d -> p (b t) d", p=P)
        moe_dram = moe_sum.rearrange("(t p) d -> p t d", p=P)

        def tiles(g):
            return range(g * GT, (g + 1) * GT)

        def toks(g):
            return slice(g * GN, (g + 1) * GN)

        V_B1, V_BQ1, V_BK1, V_BV1, V_G, V_BE, V_BIAS = 0, 32, 33, 34, 35, 38, 41
        R_KV, R_B2, R_LIN = 0, 2 * D, 2 * D + E * D

        A_BANK = dict(T=1, Q=0, KV0=4, KV1=3, MIX=4, C0=5, C1=6, BT=4)
        C_BANK = dict(TURN=6, Q=1, K=3, V=6, O=0, S0=4, S1=5, P0=7, P1=2, DT=1, L0=2, L1=5, L2=4, NT0=0, NT1=0, NT2=1, R0=3, R1=6, FIN=2)
        FIRST_BEATS = dict(a_stats=0, bias=0.1, r_a_in=2.5, masks=2.6, a_norm=8.4, a_turn=11.7, a_evac=12.6, kv1=14.1,
                           kv0=16.1, kv1_evac=16.1, kv0_evac=17.4, q=17.7, mix=18.6, q_evac=18.8, mask=19.7, ctx=20.6,
                           divide=23.6, weights=24.7, vectors=24.8, weights_out=25, m_stats=26, y1=26.1, r_a_mid=29.8,
                           m_norm=31.1, m_scale=34.1, o_stats=35.4, r_a_out=37.6, o_norm=39.2, x1=46, b_stats=47.2,
                           b_turn=47.2, r_b_in=52.8, logits=52.9, b_norm=53.1, b_evac=56.4)
        SECOND_BEATS = dict(c_first=0, r_b_out=6.7, n_b_out=13.2, x2=14.2, c_stats=17.1, r_c_in=19.5, c_norm=21.4,
                            c_evac=21.5, c_turn=22.1, k1=23, q1=23.9, v1=24.1, k1_evac=24.3, q1_evac=26, score=26.5,
                            v1_evac=27.6, exps=28.6, score_max=29.3, pturn=32.6, p1=33.7, p0=35.3, out=35.3, o_norm=39.6,
                            o_stats=39.8, n_c_out=40.6, r_c_out=41, x3=45.8, d_stats=47.4, r_d_in=49.7, d_norm=51,
                            d_evac=51.4, d_turn=51.5, lin0=54.4, lstats0=54.8, lnorm0=57.2, r_d0=57.7, gelu0=58.9,
                            nturn0=60.2, back0=62.9, res0=63, lstats1=64, lin1=64.3, r_d1=65.6, lnorm1=68, gelu1=68.2,
                            nturn1=70.2, res1=71.8, back1=72.9, lin2=76.3, lstats2=76.7, r_d2=77.5, lnorm2=79.7, gelu2=81.2,
                            nturn2=85.2, back2=85.9, fin=87.4, ostats=90.1, r_out=91.2, onorm=97.1, y=98.9)
        WEIGHT_BANK, VECTOR_BANK = A_BANK["Q"], A_BANK["BT"]
        FIRST_EVERY, SECOND_EVERY = 5.3, 6.5

        block = ctx.enter_context(nc.Block())

        @block.sync
        def _(sp):
            row = lambda n: a[n].rearrange("(o d) -> o d", o=1)

            def load_x(g):
                sp.dma_start(x0[:, g * GT:(g + 1) * GT, :], x_dram[:, g * GT:(g + 1) * GT, :]).then_inc(ld_x[g], 16)

            load_x(0)
            sp.dma_start(bias_rows[2:2 + E, :], a["L0_ffn_b2"]).then_inc(sm["ld_bias"], 16)
            sp.dma_start(bias_rows[2 + E:5 + E, :], a["L1_ffn_biases"][0:5:2, :]).then_inc(sm["ld_bias"], 16)
            sp.dma_start(bias_rows[5 + E:6 + E, :], a["L1_ffn_biases"][5:6, :]).then_inc(sm["ld_bias"], 16)
            sp.dma_start(bq_col[:, :], a["L0_attn_bq"].rearrange("(d o) -> d o", o=1)).then_inc(sm["ld_bq"], 16)
            load_x(1)
            load_x(2)
            for r, part in enumerate((bias_hi, bias_mid, bias_lo)):
                sp.wait_ge(sm["bias_parts"], r + 1)
                sp.dma_start(bias3[r:r + 1, :].rearrange("o (r d) -> o r d", d=D), part[:, :]).then_inc(sm["bias_ready"], 16)
            load_x(3)
            for i, n in ((3, "L1_attn_Wq"), (4, "L1_attn_Wk"), (5, "L1_attn_Wv"), (6, "L1_attn_Wo")):
                sp.dma_start(w_raw[:, i, :], a[n]).then_inc(sm["ld_w"], 16)
            for dst, n in ((V_BQ1, "L1_attn_bq"), (V_BK1, "L1_attn_bk"), (V_BV1, "L1_attn_bv")):
                sp.dma_start(vec_rows[dst:dst + 1, :], row(n)).then_inc(sm["ld_vec"], 16)
            sp.dma_start(vec_rows[V_B1:V_B1 + E * J, :], a["L0_ffn_b1"].rearrange("e (j p) -> (e j) p", p=P)).then_inc(sm["ld_vec"], 16)
            sp.dma_start(vec_rows[V_G:V_G + 3, :], a["L1_ffn_ln_gamma"]).then_inc(sm["ld_vec"], 16)
            sp.dma_start(vec_rows[V_BE:V_BE + 3, :], a["L1_ffn_ln_beta"]).then_inc(sm["ld_vec"], 16)
            sp.dma_start(vec_rows[V_BIAS:V_BIAS + NL, :], a["L1_ffn_biases"]).then_inc(sm["ld_vec"], 16)
            sp.dma_start(gamma_all[:, :], row("L0_attn_gamma").to_broadcast([P, D])).then_inc(sm["ld_small"], 16)
            sp.dma_start(beta_all[:, :], row("L0_attn_beta").to_broadcast([P, D])).then_inc(sm["ld_small"], 16)
            sp.dma_start(wr[:, :], a["L0_ffn_Wr"]).then_inc(sm["ld_small"], 16)
            sp.dma_start(bo_row[:, :], row("L1_attn_bo")).then_inc(sm["ld_small"], 16)
            sp.dma_start(q_int[:, :, :], a["L1_ffn_qweights"].rearrange("l o i -> o l i")).then_inc(sm["ld_lin"], 16)
            sp.dma_start(q_scale[:, :, :], a["L1_ffn_scales"].rearrange("l o s -> o l s")).then_inc(sm["ld_lin"], 16)
            sp.dma_start(lora_a[:, :, :], a["L1_ffn_lora_a"].rearrange("l r i -> r l i")).then_inc(sm["ld_lin"], 16)
            sp.dma_start(lora_b[:, :, :], a["L1_ffn_lora_b"].rearrange("l o r -> o l r")).then_inc(sm["ld_lin"], 16)
            sp.dma_start(w1[:, :, :], a["L0_ffn_W1"].rearrange("e d h -> d e h")).then_inc(sm["ld_experts"], 16)
            sp.dma_start(w2[:, :, :, :], a["L0_ffn_W2"].rearrange("e (j p) d -> p e j d", p=P)).then_inc(sm["ld_experts"], 16)
            sp.wait_ge(sm["consts"], 1)
            sp.dma_start(moe_dram, zeros[:, :].rearrange("p (t d) -> p t d", d=D)).then_inc(sm["zero_written"], 16)
            sp.wait_ge(sm["scores_ready"], 1)
            sp.dma_start(table.rearrange("(t p) c -> p t c", p=P), tab[:, :, :]).then_inc(sm["table_written"], 16)
            sp.wait_ge(scattered[(E - 1) % 2], 16 * SC * (E // 2))
            sp.dma_start(moe[:, :, :], moe_dram).then_inc(sm["moe_loaded"], 16)
            for g in range(G):
                sp.wait_ge(sm["out_ready"], g + 1)
                sp.dma_start(out_dram[:, g * GT:(g + 1) * GT, :], y_out[:, g * GT:(g + 1) * GT, :]).then_inc(sm["out_written"], 16)
            sp.wait_ge(sm["out_written"], 16 * G)

        @block.gpsimd
        def _(pool):
            step = [0]

            def link(ins):
                step[0] += 1
                ins.then_inc(sm["pool_step"], 1)
                pool.wait_ge(sm["pool_step"], step[0])

            def band(view, pattern, mult):
                base, pat = pattern
                link(pool.affine_select(out=view, in_=view, compare_op=ALU.is_ge, fill=0.0, base=base,
                                        pattern=pat, channel_multiplier=mult))

            pool.memset(minus_half[:, :], -0.5)
            link(pool.memset(ident[:, :], 0.0))
            pool.affine_select(out=ident[:, :], in_=ident[:, :], compare_op=ALU.not_equal, fill=1.0, base=0,
                               pattern=[[-1, P]], channel_multiplier=1).then_inc(sm["ones_set"], 1)
            pool.memset(ones3[:, :], 1.0)
            pool.memset(ones_row[:, :], 1.0)
            pool.memset(v_tok[:, :, D:D + 1], 1.0).then_inc(sm["ones_set"], 1)
            link(pool.memset(centred[:, :], 1.0 / D))
            band(centred[:, :], (-(2 + E), [[0, 1]]), 1)
            pool.affine_select(out=centred[:, :], in_=centred[:, :], compare_op=ALU.is_ge, fill=0.0, base=2 + E + 2,
                               pattern=[[0, 1]], channel_multiplier=-1).then_inc(sm["centred_set"], 1)

            def masks(g):
                if g:
                    return
                link(pool.memset(head_block[:, :], 1.0))
                hb = head_block[:, :].rearrange("p (h d) -> p h d", d=HD)
                band(hb, (0, [[-HD, H], [0, HD]]), 1)
                band(hb, (HD - 1, [[HD, H], [0, HD]]), -1)
                link(pool.memset(head_col[:, :], 1.0))
                band(head_col[:, :], (0, [[-HD, H]]), 1)
                pool.affine_select(out=head_col[:, :], in_=head_col[:, :], compare_op=ALU.is_ge, fill=0.0, base=HD - 1,
                                   pattern=[[HD, H]], channel_multiplier=-1).then_inc(sm["heads_set"], 1)

            def route_masks():
                link(pool.memset(same_expert[:, :], 1.0))
                se = same_expert[:, :].rearrange("p (e t) -> p e t", t=T)
                band(se, (0, [[-T, E], [0, T]]), 1)
                band(se, (T - 1, [[T, E], [0, T]]), -1)
                link(pool.tensor_copy(tile_before[:, :], same_expert[:, :]))
                pool.affine_select(out=tile_before[:, :], in_=tile_before[:, :], compare_op=ALU.is_ge, fill=0.0, base=-1,
                                   pattern=[[1, P]], channel_multiplier=-1).then_inc(sm["experts_set"], 1)

            def slot_constants():
                link(pool.memset(own_expert[:, :], 1.0))
                band(own_expert[:, :], (0, [[-T, E]]), 1)
                band(own_expert[:, :], (T - 1, [[T, E]]), -1)
                link(pool.iota(tile_start_i[:, :], [[-T * P, E]], base=0, channel_multiplier=P))
                link(pool.tensor_copy(tile_start_f[:, :], tile_start_i[:, :]))
                pool.tensor_tensor(tile_start[:, :], tile_start_f[:, :], own_expert[:, :], ALU.mult)
                link(pool.iota(slot_i[:, :], [[1, KEEP]], base=0, channel_multiplier=0))
                pool.tensor_copy(slot_free[:, :], slot_i[:, :])
                link(pool.iota(slot_part_i[:, :], [[P, SC]], base=0, channel_multiplier=1))
                pool.tensor_copy(slot_part[:, :], slot_part_i[:, :])
                pool.memset(zeros[:, :], 0.0).then_inc(sm["consts"], 1)

            def rstd(n, shift=False):
                def run(g):
                    L = ln[n]
                    c = slice(g * GT, (g + 1) * GT)
                    pool.wait_ge(L.stats_ready, g + 1)
                    ve = pool.tensor_scalar(L.ve[:, c], L.mv[:, c, 1], LN_EPS, None, ALU.add)
                    step[0] += 1
                    ve.then_inc(sm["pool_step"], 1)
                    if shift:
                        nm = pool.tensor_scalar(L.nmean[:, c], L.mv[:, c, 0], -1.0, None, ALU.mult)
                        step[0] += 1
                        nm.then_inc(sm["pool_step"], 1)
                    pool.wait_ge(sm["pool_step"], step[0])
                    root = pool.tensor_tensor(L.rstd[:, c], L.ve[:, c], minus_half[:, :], ALU.pow)
                    if shift:
                        link(root)
                        pool.tensor_tensor(L.shift[:, c], L.nmean[:, c], L.rstd[:, c], ALU.mult).then_inc(L.rstd_ready, 1)
                    else:
                        root.then_inc(L.rstd_ready, 1)
                return run

            def add(out, in0, in1, waits, done):
                def run(g):
                    c = slice(g * GT, (g + 1) * GT)
                    for s in waits:
                        pool.wait_ge(sm[s], g + 1)
                    pool.tensor_tensor(out[:, c, :], in0[:, c, :], in1[:, c, :], ALU.add).then_inc(sm[done], 1)
                return run

            flow(FIRST_BEATS, FIRST_EVERY, G, r_a_in=rstd("a_in", True), masks=masks,
                 y1=add(y1, y0, a_tok, ["y0_ready"], "y1_ready"), r_a_mid=rstd("a_mid", True), r_a_out=rstd("a_out", True),
                 x1=add(x1, x0, u, ["u_ready"], "x1_ready"), r_b_in=rstd("b_in"))
            route_masks()

            pool.wait_ge(sm["ld_lin"], 64)
            link(pool.tensor_scalar(q_w[:, :, :], q_int[:, :, :], 1.0 / 7.5, -1.0, ALU.mult, ALU.add))
            pool.tensor_tensor(q_ws[:, :, :].rearrange("p l (s k) -> p (l s) k", s=NS),
                               q_w[:, :, :].rearrange("p l (s k) -> p (l s) k", s=NS),
                               q_scale[:, :, :].rearrange("p l s -> p (l s)").unsqueeze(2).to_broadcast([P, NL * NS, D // NS]),
                               ALU.mult).then_inc(sm["q_ready"], 1)
            slot_constants()

            def gather(e):
                pool.wait_ge(sm["token_ready"], e + 1)
                for c in range(SC):
                    pool.indirect_dma_start(
                        out=xg[:, e, c, :], out_offset=None, in_=table,
                        in_offset=bass.IndirectOffsetOnAxis(ap=token_of[:, c, e:e + 1], axis=0)).then_inc(gathered[e % 4], 16)

            def scatter(e):
                pool.wait_ge(sm["yg_ready"], e + 1)
                if e:
                    pool.wait_ge(scattered[(e - 1) % 2], 16 * SC * ((e - 1) // 2 + 1))
                else:
                    pool.wait_ge(sm["zero_written"], 16)
                for c in range(SC):
                    pool.indirect_dma_start(
                        out=moe_sum, out_offset=bass.IndirectOffsetOnAxis(ap=token_of[:, c, e:e + 1], axis=0),
                        in_=yg[:, e % 2, c, :], in_offset=None, compute_op=ALU.add).then_inc(scattered[e % 2], 16)

            pool.wait_ge(sm["table_written"], 16)
            AHEAD = 3
            for e in range(AHEAD):
                gather(e)
            for e in range(E):
                if e + AHEAD < E:
                    gather(e + AHEAD)
                scatter(e)

            flow(SECOND_BEATS, SECOND_EVERY, G, r_b_out=rstd("b_out", True), x2=add(x2, x1, z, ["uc_ready"], "x2_ready"),
                 r_c_in=rstd("c_in"), r_c_out=rstd("c_out", True), x3=add(x3, x2, w_out, ["ud_ready"], "x3_ready"),
                 r_d_in=rstd("d_in"), r_d0=rstd("d0"), r_d1=rstd("d1"), r_d2=rstd("d2"), r_out=rstd("d_out"),
                 y=add(y_out, x3, u, ["uo_ready"], "out_ready"))

        @block.scalar
        def _(act):
            def copy(dst, src, func=ACT.Copy, **kw):
                return act.activation(dst, src, func, **kw)

            def normalise(n, dst, src, g, done):
                L = ln[n]
                act.wait_ge(L.rstd_ready, g + 1)
                for t in tiles(g):
                    ins = copy(dst[:, t, :], src[:, t, :], ACT.Identity, scale=L.rstd[:, t:t + 1], bias=L.shift[:, t:t + 1])
                ins.then_inc(done, 1)

            row = lambda n: a[n].rearrange("(o d) -> o d", o=1)
            for i, n in enumerate(("L0_attn_Wq", "L0_attn_Wk", "L0_attn_Wv")):
                act.dma_start(w_raw[:, i, :], a[n]).then_inc(sm["ld_w0"], 16)
            for r, n in enumerate(("L0_attn_bk", "L0_attn_bv")):
                act.dma_start(bias_rows[r:r + 1, :], row(n)).then_inc(sm["ld_bias"], 16)

            act.wait_ge(sm["prep_done"], 1)
            copy(w_qT[:, :], bank[0][:, 0:P])
            copy(w_kvT[:, :, :], bank[0][:, P:3 * P].rearrange("p (a b) -> p a b", a=2)).then_inc(sm["prep_copied"], 1)

            def weights_out(g):
                if g:
                    return
                act.wait_ge(sm["prep_done"], 2)
                copy(w1_qT[:, :], bank[WEIGHT_BANK][:, 0:P])
                copy(w1_kT[:, :], bank[WEIGHT_BANK][:, P:2 * P])
                copy(w1_oT[:, :], bank[WEIGHT_BANK][:, 2 * P:3 * P]).then_inc(sm["prep_copied"], 1)
                act.wait_ge(sm["prep_done"], 3)
                copy(vec[:, :], bank[VECTOR_BANK][:, 0:NV]).then_inc(sm["prep_copied"], 1)

            def a_evac(g):
                act.wait_ge(sm["aT_done"], g + 1)
                copy(aT[:, toks(g)], bank[A_BANK["T"]]).then_inc(sm["aT_copied"], 1)

            def qk_evac(g):
                if g == 0:
                    act.wait_ge(sm["ld_bq"], 16)
                act.wait_ge(sm["q_done"], g + 1)
                copy(qT[:, toks(g)], bank[A_BANK["Q"]], ACT.Relu, bias=bq_col[:, :]).then_inc(sm["qT_ready"], 1)

            def kv_evac(g):
                act.wait_ge(sm["kv0_done"], g + 1)
                t = g * GT
                kv = bank[A_BANK["KV0"]].rearrange("p (t c) -> p t c", t=2)
                copy(k_tok[:, t:t + 2, :], kv[:, :, 0:D], ACT.Relu)
                copy(v_tok[:, t:t + 2, 0:D], kv[:, :, D:2 * D]).then_inc(sm["kv0_ready"], 1)

            def b_evac(g):
                act.wait_ge(sm["bT_done"], g + 1)
                copy(bT[:, toks(g)], bank[A_BANK["BT"]]).then_inc(sm["bT_copied"], 1)

            flow(FIRST_BEATS, FIRST_EVERY, G, a_norm=lambda g: normalise("a_in", a_tok, x0, g, sm["a_ready"]), a_evac=a_evac,
                 q_evac=qk_evac, kv0_evac=kv_evac, m_norm=lambda g: normalise("a_mid", z, y1, g, sm["mid_ready"]),
                 o_norm=lambda g: normalise("a_out", u, z, g, sm["u_ready"]), weights_out=weights_out, b_evac=b_evac)

            act.wait_ge(sm["shifted_ready"], 1)
            copy(expd[:, :, :], shifted[:, :, :], ACT.Exp).then_inc(sm["exp_ready"], 1)

            for h in range(2):
                act.wait_ge(sm["prep_done"], 4 + h)
                copy(lora_bT[:, 3 * h:3 * h + 3, :], bank[1 + h][0:R, 0:3 * P].rearrange("p (a b) -> p a b", a=3)).then_inc(sm["prep_copied"], 1)
            act.wait_ge(sm["prep_done"], 6)
            copy(w1_vo[:, :], bank[3][:, 0:P]).then_inc(sm["prep_copied"], 1)
            act.wait_ge(sm["prep_done"], 7)
            copy(bo_all[:, :], bank[3][:, 0:P]).then_inc(sm["prep_copied"], 1)
            for h in range(2):
                act.wait_ge(sm["prep_done"], 8 + h)
                for i in range(3 * h, 3 * h + 3):
                    ins = copy(w_effT[:, i, :], bank[5 + h][:, (i % 3) * P:(i % 3 + 1) * P], accum_out=w_sum[:, i:i + 1])
                ins.then_inc(sm["prep_copied"], 1)
            act.wait_ge(sm["prep_copied"], 9)
            copy(w_nmean[:, :], w_sum[:, :], scale=-1.0 / D).then_inc(sm["eff_mean"], 1)
            act.wait_ge(sm["eff_mean"], 1)
            for i in range(0, NL, 2):
                ins = copy(w_effT[:, i, :], w_effT[:, i, :], ACT.Identity, bias=w_nmean[:, i:i + 1])
            ins.then_inc(sm["eff_mean"], 1)

            for e in range(E):
                for j in range(J):
                    act.wait_ge(sm["h_done"], e * J + j + 1)
                    if j == 0 and e >= 2:
                        act.wait_ge(sm["y_done"], e - 1)
                    copy(hT[:, e % 2, j, :], bank[2 + j], ACT.Gelu,
                         bias=vec[:, V_B1 + e * J + j:V_B1 + e * J + j + 1]).then_inc(sm["h_ready"], 1)

            def c_evac(g):
                act.wait_ge(sm["cT_done"], g + 1)
                copy(cT[:, toks(g)], bank[C_BANK["TURN"]]).then_inc(sm["cT_copied"], 1)

            def q1_evac(g):
                act.wait_ge(sm["q1_done"], g + 1)
                copy(q1T[:, toks(g)], bank[C_BANK["Q"]], ACT.Identity, bias=vec[:, V_BQ1:V_BQ1 + 1]).then_inc(sm["q1_ready"], 1)

            def k1_evac(g):
                act.wait_ge(sm["k1_done"], g + 1)
                copy(k1T[:, toks(g)], bank[C_BANK["K"]], ACT.Identity, bias=vec[:, V_BK1:V_BK1 + 1]).then_inc(sm["k1_ready"], 1)

            def exps(g):
                act.wait_ge(sm["smax_ready"], g + 1)
                for t in tiles(g):
                    i = t - g * GT
                    ins = copy(prob[:, t, :], bank[C_BANK[f"S{i // 2}"]][:, (i % 2) * S:(i % 2 + 1) * S], ACT.Exp,
                               bias=nsmax[:, t:t + 1], scale=ATT_SCALE, accum_out=psum_p[:, t:t + 1])
                ins.then_inc(sm["p_ready"], 1)

            def p_evac(g):
                act.wait_ge(sm["pT_done"], GB * g + GB)
                copy(probT[:, GB * g + 1, :, :], bank[C_BANK["P1"]].rearrange("p (k q) -> p k q", k=BT)).then_inc(sm["pT1_copied"], 1)

            def d_evac(g):
                act.wait_ge(sm["dT_done"], g + 1)
                copy(h_T[0][:, toks(g)], bank[C_BANK["DT"]]).then_inc(sm["dT_copied"], 1)

            def gelu(k):
                def run(g):
                    act.wait_ge(nT_done[k], g + 1)
                    if k:
                        act.wait_ge(res_done[k - 1], g + 1)
                    copy(g_T[:, toks(g)], bank[C_BANK[f"NT{k}"]], ACT.Gelu, scale=vec[:, V_G + k:V_G + k + 1],
                         bias=vec[:, V_BE + k:V_BE + k + 1]).then_inc(gelu_ready[k], 1)
                return run

            def lin_norm(k):
                def run(g):
                    L = ln[f"d{k}"]
                    act.wait_ge(L.rstd_ready, g + 1)
                    for i, t in enumerate(tiles(g)):
                        ins = copy(n_tok[:, t, :], bank[C_BANK[f"L{k}"]][:, i * D:(i + 1) * D], scale=L.rstd[:, t:t + 1])
                    ins.then_inc(n_ready[k], 1)
                return run

            def fin_evac(g):
                act.wait_ge(sm["fin_done"], g + 1)
                copy(h_out[:, g * GT:(g + 1) * GT, :], bank[C_BANK["FIN"]].rearrange("p (t d) -> p t d", t=GT)).then_inc(sm["fin_ready"], 1)

            flow(SECOND_BEATS, SECOND_EVERY, G, n_b_out=lambda g: normalise("b_out", z, moe, g, sm["uc_ready"]), c_evac=c_evac,
                 q1_evac=q1_evac, k1_evac=k1_evac, exps=exps, p1=p_evac,
                 n_c_out=lambda g: normalise("c_out", w_out, o_tok, g, sm["ud_ready"]), d_evac=d_evac,
                 lnorm0=lin_norm(0), lnorm1=lin_norm(1), lnorm2=lin_norm(2), gelu0=gelu(0), gelu1=gelu(1), gelu2=gelu(2),
                 fin=fin_evac)

        @block.tensor
        def _(pe):
            tenant = {}

            def claim(b, leaves, count):
                if b in tenant:
                    pe.wait_ge(*tenant[b])
                tenant[b] = (leaves, count)
                return bank[b]

            def mm(out, lhsT, rhs, start=True, stop=True):
                return pe.matmul(out, lhsT, rhs, start=start, stop=stop)

            def turn(out, in_, n=P):
                return pe.transpose(out, in_, ident[0:n, 0:n])

            def turn4(o, src, g, done):
                for i, t in enumerate(tiles(g)):
                    ins = turn(o[:, i * P:(i + 1) * P], src[:, t, 0:P])
                ins.then_inc(done, 1)

            pe.wait_ge(sm["ones_set"], 1)
            pe.wait_ge(sm["ld_w0"], 16 * 3)
            o = claim(0, sm["prep_copied"], 1)
            for i in range(3):
                ins = turn(o[:, i * P:(i + 1) * P], w_raw[:, i, :])
            ins.then_inc(sm["prep_done"], 1)

            def weights(g):
                if g:
                    return
                pe.wait_ge(sm["ld_w"], 16 * 4)
                o = claim(WEIGHT_BANK, sm["prep_copied"], 2)
                for i, w in enumerate((3, 4, 6)):
                    ins = turn(o[:, i * P:(i + 1) * P], w_raw[:, w, :])
                ins.then_inc(sm["prep_done"], 1)

            def vectors(g):
                if g:
                    return
                pe.wait_ge(sm["ld_vec"], 16 * 7)
                turn(claim(VECTOR_BANK, sm["prep_copied"], 3)[:, 0:NV], vec_rows[:, :], NV).then_inc(sm["prep_done"], 1)

            def a_turn(g):
                pe.wait_ge(sm["a_ready"], g + 1)
                turn4(claim(A_BANK["T"], sm["aT_copied"], g + 1), a_tok, g, sm["aT_done"])

            def a_query(g):
                pe.wait_ge(sm["aT_copied"], g + 1)
                if g == 0:
                    pe.wait_ge(sm["prep_copied"], 1)
                mm(claim(A_BANK["Q"], sm["qT_ready"], g + 1), w_qT[:, :], aT[:, toks(g)]).then_inc(sm["q_done"], 1)

            def a_key_value(i):
                def run(g):
                    pe.wait_ge(sm["aT_copied"], g + 1)
                    if g == 0:
                        pe.wait_ge(sm["bias_ready"], 48)
                        pe.wait_ge(sm["ones_set"], 2)
                    o = claim(A_BANK[f"KV{i}"], sm[f"kv{i}_ready"], g + 1)
                    for j in range(2):
                        t = g * GT + 2 * i + j
                        oj = o[:, j * 2 * D:(j + 1) * 2 * D]
                        mm(oj, aT[:, t * P:(t + 1) * P], w_kvT[:, :, :].rearrange("p a b -> p (a b)"), True, False)
                        ins = mm(oj, ones3[:, :], bias3[:, R_KV:R_KV + 2 * D], False, True)
                    ins.then_inc(sm[f"kv{i}_done"], 1)
                return run

            def a_mix(g):
                pe.wait_ge(sm["kv0_ready"], g + 1)
                pe.wait_ge(sm["kv1_ready"], g + 1)
                if g == 0:
                    pe.wait_ge(sm["ones_set"], 2)
                o = claim(A_BANK["MIX"], sm["kv_ready"], g + 1)
                for b in range(GB):
                    for i in range(BT):
                        t = g * GT + b * BT + i
                        ins = mm(o[:, b * 256:b * 256 + D + 1], k_tok[:, t, :], v_tok[:, t, 0:D + 1], i == 0, i == BT - 1)
                ins.then_inc(sm["ksum_done"], 1)

            def a_ctx(g):
                pe.wait_ge(sm["kv_ready"], g + 1)
                pe.wait_ge(sm["qT_ready"], g + 1)
                o2 = [claim(A_BANK[f"C{i}"], sm["y0_ready"], g + 1) for i in range(2)]
                for i, t in enumerate(tiles(g)):
                    ins = mm(o2[i // 2][:, (i % 2) * 256:(i % 2) * 256 + D + H], qT[:, t * P:(t + 1) * P], kv_blk[:, t // BT, :])
                ins.then_inc(sm["ctx_done"], 1)

            def b_turn(g):
                pe.wait_ge(sm["b_ready"], g + 1)
                turn4(claim(A_BANK["BT"], sm["bT_copied"], g + 1), tab, g, sm["bT_done"])

            def logits(g):
                pe.wait_ge(sm["bT_copied"], g + 1)
                if g == 0:
                    pe.wait_ge(sm["ld_small"], 64)
                    claim(7, sm["shifted_ready"], 1)
                for t in tiles(g):
                    ins = mm(bank[7][:, t * E:(t + 1) * E], bT[:, t * P:(t + 1) * P], wr[:, :])
                ins.then_inc(sm["logit_done"], 1)

            flow(FIRST_BEATS, FIRST_EVERY, G, a_turn=a_turn, q=a_query, kv0=a_key_value(0), kv1=a_key_value(1), mix=a_mix,
                 ctx=a_ctx, weights=weights, vectors=vectors, b_turn=b_turn, logits=logits)

            pe.wait_ge(sm["scores_ready"], 1)
            turn(claim(7, sm["scoreT_ready"], 1)[:, 0:P], sc_et[:, :, :].rearrange("p e t -> p (e t)")).then_inc(sm["scoreT_done"], 1)

            def lora_turn(h):
                def run():
                    pe.wait_ge(sm["ld_lin"], 64)
                    o = claim(1 + h, sm["prep_copied"], 3 + h + 1)
                    for i in range(3):
                        ins = turn(o[0:R, i * P:(i + 1) * P], lora_b[:, 3 * h + i, :])
                    ins.then_inc(sm["prep_done"], 1)
                return run

            def value_out():
                mm(claim(3, sm["prep_copied"], 6)[:, 0:P], w_raw[:, 5, :], w1_oT[:, :]).then_inc(sm["prep_done"], 1)

            def bias_out():
                pe.wait_ge(sm["bv_ready"], 1)
                pe.wait_ge(sm["ld_small"], 64)
                o = claim(3, sm["prep_copied"], 7)[:, 0:P]
                mm(o, bv_cols[:, :], w1_oT[:, :], True, False)
                mm(o, ones_row[:, :], bo_row[:, :], False, True).then_inc(sm["prep_done"], 1)

            def effective(i):
                def run():
                    if i == 0:
                        pe.wait_ge(sm["q_ready"], 1)
                        pe.wait_ge(sm["prep_copied"], 5)
                    if i % 3 == 0:
                        claim(5 + i // 3, sm["prep_copied"], 7 + i // 3 + 1)
                    o = bank[5 + i // 3][:, (i % 3) * P:(i % 3 + 1) * P]
                    mm(o, q_ws[:, i, :], ident[:, :], True, False)
                    ins = mm(o, lora_a[:, i, :], lora_bT[:, i, :], False, True)
                    if i % 3 == 2:
                        ins.then_inc(sm["prep_done"], 1)
                return run

            between = dict(zip(range(6, SCORE_BITS, 2),
                               [lora_turn(0), lora_turn(1), value_out, bias_out] + [effective(i) for i in range(NL)]))
            pe.wait_ge(sm["experts_set"], 1)
            for k in range(SCORE_BITS):
                pe.wait_ge(sm["cand_counted"], k + 1)
                o = claim(0, sm["cand_taken"], k + 1) if k else claim(0, sm["cand_taken"], 1)
                mm(o[:, 0:1], same_expert[:, :], hit_count[:, :]).then_inc(sm["cand_summed"], 1)
                if k in between:
                    between[k]()
            pe.wait_ge(sm["sel_counted"], 1)
            o = claim(0, sm["room_ready"], 1)
            mm(o[:, 0:1], same_expert[:, :], above_count[:, :])
            mm(o[:, 1:2], tile_before[:, :], tied_count[:, :]).then_inc(sm["sel_summed"], 1)
            pe.wait_ge(sm["kept_counted"], 1)
            mm(claim(7, sm["first_ready"], 1)[:, 0:1], tile_before[:, :], kept_count[:, :]).then_inc(sm["kept_summed"], 1)
            pe.wait_ge(sm["slots_ready"], 1)
            o = claim(6, sm["first_token_ready"], 1)
            pe.wait_ge(sm["consts"], 1)
            for c in range(SC):
                ins = mm(o[:, c * E:(c + 1) * E], slot_row[:, c * P:(c + 1) * P], tile_start[:, :])
            ins.then_inc(sm["start_done"], 1)
            for e in range(E):
                o = claim(SLOT_BANKS[e], sm["slots_used"], e + 1)
                for c in range(SC):
                    ins = mm(o[:, c * P:(c + 1) * P], slot_row[:, c * P:(c + 1) * P], rank_by_expert[:, e, :])
                ins.then_inc(sm["slots_done"], 1)

            def g_turn(e):
                pe.wait_ge(gathered[e % 4], 16 * SC * (e // 4 + 1))
                o = claim(e % 2, sm["gT_copied"], e + 1)
                for c in range(SC):
                    ins = turn(o[:, c * P:(c + 1) * P], xg[:, e, c, 0:D])
                ins.then_inc(sm["gT_done"], 1)

            def hidden(e):
                pe.wait_ge(sm["gT_copied"], e + 1)
                if e == 0:
                    pe.wait_ge(sm["ld_experts"], 32)
                for j in range(J):
                    mm(claim(2 + j, sm["h_ready"], e * J + j + 1), w1[:, e, j * P:(j + 1) * P],
                       xgT[:, e % 2, :]).then_inc(sm["h_done"], 1)

            def outer(e):
                pe.wait_ge(sm["h_ready"], (e + 1) * J)
                if e == 0:
                    pe.wait_ge(sm["ld_experts"], 32)
                o = claim(6 + e % 2, sm["yg_ready"], e + 1)
                for c in range(SC):
                    oc = o[:, c * D:(c + 1) * D]
                    for j in range(J):
                        mm(oc, hT[:, e % 2, j, c * P:(c + 1) * P], w2[:, e, j, :], j == 0, False)
                    ins = mm(oc, ones3[:, :], bias3[:, R_B2 + e * D:R_B2 + (e + 1) * D], False, True)
                ins.then_inc(sm["y_done"], 1)

            g_turn(0)
            for e in range(E):
                hidden(e)
                if e + 1 < E:
                    g_turn(e + 1)
                if e:
                    outer(e - 1)
            outer(E - 1)

            def c_turn(g):
                pe.wait_ge(sm["c_ready"], g + 1)
                turn4(claim(C_BANK["TURN"], sm["cT_copied"], g + 1), c_tok, g, sm["cT_done"])

            def c_query(g):
                pe.wait_ge(sm["cT_copied"], g + 1)
                mm(claim(C_BANK["Q"], sm["q1_ready"], g + 1), w1_qT[:, :], cT[:, toks(g)]).then_inc(sm["q1_done"], 1)

            def c_key(g):
                pe.wait_ge(sm["cT_copied"], g + 1)
                mm(claim(C_BANK["K"], sm["k1_ready"], g + 1), w1_kT[:, :], cT[:, toks(g)]).then_inc(sm["k1_done"], 1)

            def c_value(g):
                pe.wait_ge(sm["cT_copied"], g + 1)
                o = claim(C_BANK["V"], sm["v1_ready"], g + 1)
                for i, t in enumerate(tiles(g)):
                    ins = mm(o[:, i * D:(i + 1) * D], cT[:, t * P:(t + 1) * P], w1_vo[:, :])
                ins.then_inc(sm["v1_done"], 1)

            def c_score(g):
                pe.wait_ge(sm["q1_ready"], g + 1)
                pe.wait_ge(sm["k1_ready"], g + 1)
                o2 = [claim(C_BANK[f"S{i}"], sm["p_ready"], g + 1) for i in range(2)]
                for i, t in enumerate(tiles(g)):
                    b = t // BT
                    ins = mm(o2[i // 2][:, (i % 2) * S:(i % 2 + 1) * S], q1T[:, t * P:(t + 1) * P], k1T[:, b * S:(b + 1) * S])
                ins.then_inc(sm["s_done"], 1)

            def c_pturn(g):
                pe.wait_ge(sm["p_ready"], g + 1)
                o2 = [claim(C_BANK["P0"], sm["pT0_copied"], g + 1), claim(C_BANK["P1"], sm["pT1_copied"], g + 1)]
                for b in range(GB):
                    for kb in range(BT):
                        for i in range(BT):
                            t = g * GT + b * BT + i
                            ins = turn(o2[b][:, kb * S + i * P:kb * S + (i + 1) * P], prob[:, t, kb * P:(kb + 1) * P])
                    ins.then_inc(sm["pT_done"], 1)

            def c_out(g):
                pe.wait_ge(sm["pT0_copied"], g + 1)
                pe.wait_ge(sm["pT1_copied"], g + 1)
                pe.wait_ge(sm["v1_ready"], g + 1)
                o = claim(C_BANK["O"], sm["o_ready"], g + 1)
                for i, t in enumerate(tiles(g)):
                    b = t // BT
                    for kb in range(BT):
                        ins = mm(o[:, i * D:(i + 1) * D], probT[:, b, kb, (t % BT) * P:(t % BT + 1) * P],
                                 v1[:, b * BT + kb, :], kb == 0, kb == BT - 1)
                ins.then_inc(sm["o_done"], 1)

            def d_turn(g):
                pe.wait_ge(sm["d_ready"], g + 1)
                turn4(claim(C_BANK["DT"], sm["dT_copied"], g + 1), d_tok, g, sm["dT_done"])

            def linear(k):
                def run(g):
                    if k:
                        pe.wait_ge(hT_ready[k - 1], g + 1)
                    else:
                        pe.wait_ge(sm["dT_copied"], g + 1)
                    if g == 0 and k == 0:
                        pe.wait_ge(sm["eff_mean"], 2)
                    o = claim(C_BANK[f"L{k}"], n_ready[k], g + 1)
                    for i, t in enumerate(tiles(g)):
                        oi = o[:, i * D:(i + 1) * D]
                        mm(oi, h_T[k][:, t * P:(t + 1) * P], w_effT[:, 2 * k, :], True, False)
                        ins = mm(oi, ones3[:, :], bias3[:, R_LIN + k * D:R_LIN + (k + 1) * D], False, True)
                    ins.then_inc(lin_done[k], 1)
                return run

            def n_turn(k):
                def run(g):
                    pe.wait_ge(n_ready[k], g + 1)
                    turn4(claim(C_BANK[f"NT{k}"], gelu_ready[k], g + 1), n_tok, g, nT_done[k])
                return run

            def back(k):
                def run(g):
                    pe.wait_ge(gelu_ready[k], g + 1)
                    mm(claim(C_BANK[f"R{k}"], hT_ready[k], g + 1), w_effT[:, 2 * k + 1, :],
                       g_T[:, toks(g)]).then_inc(res_done[k], 1)
                return run

            def back_last(g):
                pe.wait_ge(gelu_ready[2], g + 1)
                o = claim(C_BANK["FIN"], sm["fin_ready"], g + 1)
                for i, t in enumerate(tiles(g)):
                    oi = o[:, i * D:(i + 1) * D]
                    mm(oi, g_T[:, t * P:(t + 1) * P], w_effT[:, 5, :], True, False)
                    mm(oi, h_T[2][:, t * P:(t + 1) * P], ident[:, :], False, False)
                    ins = mm(oi, ones3[:, :], bias3[:, R_LIN + 3 * D:R_LIN + 4 * D], False, True)
                ins.then_inc(sm["fin_done"], 1)

            flow(SECOND_BEATS, SECOND_EVERY, G, c_turn=c_turn, q1=c_query, k1=c_key, v1=c_value, score=c_score, pturn=c_pturn,
                 out=c_out, d_turn=d_turn, lin0=linear(0), lin1=linear(1), lin2=linear(2), nturn0=n_turn(0),
                 nturn1=n_turn(1), nturn2=n_turn(2), back0=back(0), back1=back(1), back2=back_last)

        @block.vector
        def _(dve):
            step = [0]

            def mark(ins):
                step[0] += 1
                ins.then_inc(sm["dve_step"], 1)

            def settle():
                dve.wait_ge(sm["dve_step"], step[0])

            def link(ins):
                mark(ins)
                settle()

            def layer_stats(n, src, g):
                L = ln[n]
                for i, t in enumerate(tiles(g)):
                    ins = dve.bn_stats(stats[:, t, :], src(i, t))
                link(ins)
                for t in tiles(g):
                    ins = dve.bn_aggr(L.mv[:, t, :], stats[:, t, :])
                ins.then_inc(L.stats_ready, 1)

            def normalise(n, dst, src, g, done):
                L = ln[n]
                dve.wait_ge(L.rstd_ready, g + 1)
                for i, t in enumerate(tiles(g)):
                    ins = dve.tensor_scalar(dst[:, t, 0:D], src(i, t), L.mv[:, t, 0:1], L.rstd[:, t:t + 1],
                                            ALU.subtract, ALU.mult)
                ins.then_inc(done, 1)

            def of(tensor):
                return lambda i, t: tensor[:, t, 0:D]

            def of_bank(b):
                return lambda i, t: bank[b][:, i * D:(i + 1) * D]

            def bias_split(g):
                if g:
                    return
                dve.wait_ge(sm["ld_bias"], 16 * 5)
                dve.wait_ge(sm["centred_set"], 1)
                link(dve.tensor_reduce(bias_mean[:, :], bias_rows[:, :], AX.X, ALU.add))
                link(dve.tensor_tensor(bias_mean[:, :], bias_mean[:, :], centred[:, :], ALU.mult))
                link(dve.tensor_scalar(bias_rows[:, :], bias_rows[:, :], bias_mean[:, :], None, ALU.subtract))
                for i, part in enumerate((bias_hi, bias_mid, bias_lo)):
                    dve.tensor_copy(part[:, :], bias_rows[:, :]).then_inc(sm["bias_parts"], 1)
                    dve.wait_ge(sm["bias_parts"], i + 1)
                    if i < 2:
                        link(dve.tensor_tensor(bias_rows[:, :], bias_rows[:, :], part[:, :], ALU.subtract))

            def a_stats(g):
                dve.wait_ge(ld_x[g], 16)
                layer_stats("a_in", of(x0), g)

            def kv_evac(g):
                if g == 0:
                    dve.wait_ge(sm["ones_set"], 2)
                dve.wait_ge(sm["kv1_done"], g + 1)
                t = g * GT + 2
                kv = bank[A_BANK["KV1"]].rearrange("p (t c) -> p t c", t=2)
                dve.tensor_scalar(k_tok[:, t:t + 2, :], kv[:, :, 0:D], 0.0, None, ALU.max)
                dve.tensor_copy(v_tok[:, t:t + 2, 0:D], kv[:, :, D:2 * D]).then_inc(sm["kv1_ready"], 1)

            def kv_mask(g):
                dve.wait_ge(sm["ksum_done"], g + 1)
                if g == 0:
                    dve.wait_ge(sm["heads_set"], 1)
                kv = bank[A_BANK["MIX"]].rearrange("p (b c) -> p b c", b=GB)
                bs = slice(g * GB, (g + 1) * GB)
                dve.tensor_tensor(kv_blk[:, bs, 0:D], kv[:, :, 0:D],
                                  head_block[:, :].unsqueeze(1).to_broadcast([P, GB, D]), ALU.mult)
                dve.tensor_tensor(kv_blk[:, bs, D:D + H], kv[:, :, D:D + 1].to_broadcast([P, GB, H]),
                                  head_col[:, :].unsqueeze(1).to_broadcast([P, GB, H]), ALU.mult).then_inc(sm["kv_ready"], 1)

            def divide(g):
                dve.wait_ge(sm["ctx_done"], g + 1)
                c = slice(g * GT, (g + 1) * GT)
                o = banks[:, 5:7, :].rearrange("p b (i c) -> p (b i) c", i=2)
                link(dve.tensor_scalar(den[:, c, :], o[:, :, D:D + H], DENOM_EPS, None, ALU.max))
                link(dve.reciprocal(rden[:, c, :], den[:, c, :]))
                for i, t in enumerate(tiles(g)):
                    ins = dve.tensor_tensor(y0[:, t, :].rearrange("p (h d) -> p h d", h=H),
                                            o[:, i, 0:D].rearrange("p (h d) -> p h d", h=H),
                                            rden[:, t, :].unsqueeze(2).to_broadcast([P, H, HD]), ALU.mult)
                ins.then_inc(sm["y0_ready"], 1)

            def mid_stats(g):
                dve.wait_ge(sm["y1_ready"], g + 1)
                layer_stats("a_mid", of(y1), g)

            def mid_scale(g):
                c = slice(g * GT, (g + 1) * GT)
                dve.wait_ge(sm["ld_small"], 64)
                dve.wait_ge(sm["mid_ready"], g + 1)
                link(dve.tensor_tensor(z[:, c, :], z[:, c, :], gamma_all[:, :].unsqueeze(1).to_broadcast([P, GT, D]), ALU.mult))
                link(dve.tensor_tensor(z[:, c, :], z[:, c, :], beta_all[:, :].unsqueeze(1).to_broadcast([P, GT, D]), ALU.add))

            def out_stats_a(g):
                layer_stats("a_out", of(z), g)

            def b_stats(g):
                dve.wait_ge(sm["x1_ready"], g + 1)
                layer_stats("b_in", of(x1), g)

            def b_norm(g):
                normalise("b_in", tab, of(x1), g, sm["b_ready"])

            flow(FIRST_BEATS, FIRST_EVERY, G, a_stats=a_stats, bias=bias_split, kv1_evac=kv_evac, mask=kv_mask, divide=divide,
                 m_stats=mid_stats, m_scale=mid_scale, o_stats=out_stats_a, b_stats=b_stats, b_norm=b_norm)

            dve.wait_ge(sm["logit_done"], G)
            logits = bank[7][:, 0:T * E].rearrange("p (t e) -> p t e", t=T)
            spread = lambda v: v.unsqueeze(2).to_broadcast([P, T, E])
            link(dve.tensor_reduce(logit_max[:, :], logits, AX.X, ALU.max))
            dve.tensor_tensor(shifted[:, :, :], logits, spread(logit_max[:, :]), ALU.subtract).then_inc(sm["shifted_ready"], 1)
            dve.wait_ge(sm["exp_ready"], 1)
            link(dve.tensor_reduce(expsum[:, :], expd[:, :, :], AX.X, ALU.add))
            link(dve.reciprocal(rexpsum[:, :], expsum[:, :]))
            link(dve.tensor_tensor(tab[:, :, D:ROW], expd[:, :, :], spread(rexpsum[:, :]), ALU.mult))
            dve.tensor_copy(sc_et[:, :, :], tab[:, :, D:ROW].rearrange("p t e -> p e t")).then_inc(sm["scores_ready"], 1)

            mark(dve.memset(cand[:, :], 1 << (SCORE_BITS - 1)))
            dve.wait_ge(sm["prep_copied"], 3)
            dve.tensor_copy(bv_cols[:, :], vec[:, V_BV1:V_BV1 + 1].to_broadcast([P, P])).then_inc(sm["bv_ready"], 1)
            dve.wait_ge(sm["scoreT_done"], 1)
            dve.tensor_copy(scoreT[:, :], bank[7][:, 0:P]).then_inc(sm["scoreT_ready"], 1)
            dve.wait_ge(sm["scoreT_ready"], 1)
            settle()
            for k in range(SCORE_BITS):
                bit = SCORE_BITS - 1 - k
                now, then = cand[:, k % 2:k % 2 + 1], cand[:, (k + 1) % 2:(k + 1) % 2 + 1]
                dve.tensor_scalar(hits[:, :], scoreT[:, :], now.bitcast(F32), None, ALU.is_ge, ALU.add,
                                  accum_out=hit_count[:, :]).then_inc(sm["cand_counted"], 1)
                mark(dve.tensor_scalar(then, now, (1 << bit) >> 1, None, ALU.bitwise_xor))
                dve.wait_ge(sm["cand_summed"], k + 1)
                dve.tensor_scalar(below[:, :], bank[0][:, 0:1], float(KEEP) - 0.5, None, ALU.is_lt).then_inc(sm["cand_taken"], 1)
                dve.wait_ge(sm["cand_taken"], k + 1)
                settle()
                link(dve.scalar_tensor_tensor(then, below[:, :], bit, then, ALU.logical_shift_left, ALU.bitwise_xor))
            cut = cand[:, SCORE_BITS % 2:SCORE_BITS % 2 + 1].bitcast(F32)

            dve.tensor_scalar(above[:, :], scoreT[:, :], cut, None, ALU.is_gt, ALU.add, accum_out=above_count[:, :])
            mark(dve.tensor_scalar(tied[:, :], scoreT[:, :], cut, None, ALU.is_equal, ALU.add, accum_out=tied_count[:, :]))
            settle()
            dve.wait_ge(sm["consts"], 1)
            dve.tensor_tensor_scan(tie_rank[:, :], tied[:, :], zeros[:, 0:P], 0.0, ALU.add, ALU.add).then_inc(sm["sel_counted"], 1)
            dve.wait_ge(sm["sel_summed"], 1)
            dve.wait_ge(sm["sel_counted"], 1)
            link(dve.tensor_scalar(tie_room[:, 0:1], bank[0][:, 0:1], -1.0, float(KEEP), ALU.mult, ALU.add))
            dve.tensor_tensor(tie_room[:, 1:2], tie_room[:, 0:1], bank[0][:, 1:2], ALU.subtract).then_inc(sm["room_ready"], 1)
            dve.wait_ge(sm["room_ready"], 1)
            link(dve.scalar_tensor_tensor(tie_kept[:, :], tie_rank[:, :], tie_room[:, 1:2], tied[:, :], ALU.is_le, ALU.mult))
            link(dve.tensor_tensor_scan(kept_rank[:, :], above[:, :], tie_kept[:, :], 0.0, ALU.add, ALU.add))
            dve.tensor_copy(kept_count[:, :], kept_rank[:, P - 1:P]).then_inc(sm["kept_counted"], 1)
            dve.wait_ge(sm["kept_summed"], 1)
            dve.tensor_copy(kept_first[:, :], bank[7][:, 0:1]).then_inc(sm["first_ready"], 1)
            dve.wait_ge(sm["first_ready"], 1)
            dve.tensor_scalar(rank_all[:, :], kept_rank[:, :], kept_first[:, :], None, ALU.add)
            link(dve.tensor_scalar(rank_last[:, :], kept_rank[:, P - 1:P], kept_first[:, :], None, ALU.add))
            dve.tensor_tensor(rank_by_expert[:, :, :], own_expert[:, :].unsqueeze(2).to_broadcast([P, E, P]),
                              rank_all[:, :].unsqueeze(1).to_broadcast([P, E, P]), ALU.mult)
            link(dve.tensor_scalar(from_first[:, :], slot_free[:, :], kept_first[:, :], None, ALU.is_ge))
            dve.scalar_tensor_tensor(slot_row[:, :], slot_free[:, :], rank_last[:, :], from_first[:, :], ALU.is_lt, ALU.mult).then_inc(sm["slots_ready"], 1)
            dve.wait_ge(sm["start_done"], 1)
            dve.tensor_copy(first_token[:, :, :], bank[6][:, 0:SC * E].rearrange("p (c e) -> p c e", c=SC)).then_inc(sm["first_token_ready"], 1)
            dve.wait_ge(sm["first_token_ready"], 1)
            for e in range(E):
                dve.wait_ge(sm["slots_done"], e + 1)
                dve.tensor_tensor(passed[:, e % 2, :, :], bank[SLOT_BANKS[e]].rearrange("p (c k) -> p c k", c=SC),
                                  slot_part[:, :].unsqueeze(2).to_broadcast([P, SC, P]), ALU.is_le).then_inc(sm["slots_used"], 1)
                dve.wait_ge(sm["slots_used"], e + 1)
                link(dve.tensor_reduce(passed_count[:, :, e], passed[:, e % 2, :, :], AX.X, ALU.add))
                dve.tensor_tensor(token_of[:, :, e], passed_count[:, :, e], first_token[:, :, e], ALU.add).then_inc(sm["token_ready"], 1)

            def g_evac(e):
                if e >= 2:
                    dve.wait_ge(sm["h_done"], (e - 1) * J)
                dve.wait_ge(sm["gT_done"], e + 1)
                dve.tensor_copy(xgT[:, e % 2, :], bank[e % 2]).then_inc(sm["gT_copied"], 1)

            def gate(e):
                if e >= 2:
                    dve.wait_ge(scattered[e % 2], 16 * SC * (e // 2))
                dve.wait_ge(sm["y_done"], e + 1)
                for c in range(SC):
                    ins = dve.tensor_scalar(yg[:, e % 2, c, :], bank[6 + e % 2][:, c * D:(c + 1) * D],
                                            xg[:, e, c, D + e:D + e + 1], None, ALU.mult)
                ins.then_inc(sm["yg_ready"], 1)

            dve.wait_ge(gathered[0], 16 * SC)
            g_evac(0)
            for e in range(E):
                if e + 1 < E:
                    g_evac(e + 1)
                if e:
                    gate(e - 1)
            gate(E - 1)

            def c_first(g):
                dve.wait_ge(sm["moe_loaded"], 16)
                layer_stats("b_out", of(moe), g)

            def c_stats(g):
                dve.wait_ge(sm["x2_ready"], g + 1)
                layer_stats("c_in", of(x2), g)

            def c_norm(g):
                normalise("c_in", c_tok, of(x2), g, sm["c_ready"])

            def v1_evac(g):
                dve.wait_ge(sm["v1_done"], g + 1)
                dve.tensor_copy(v1[:, g * GT:(g + 1) * GT, :], bank[C_BANK["V"]].rearrange("p (t d) -> p t d", t=GT)).then_inc(sm["v1_ready"], 1)

            def score_max(g):
                c = slice(g * GT, (g + 1) * GT)
                dve.wait_ge(sm["s_done"], g + 1)
                link(dve.tensor_reduce(smax[:, c], banks[:, C_BANK["S0"]:C_BANK["S1"] + 1, :].rearrange("p b (i k) -> p (b i) k", k=S), AX.X, ALU.max))
                dve.tensor_scalar(nsmax[:, c], smax[:, c], -ATT_SCALE, None, ALU.mult).then_inc(sm["smax_ready"], 1)

            def p_evac(g):
                dve.wait_ge(sm["pT_done"], GB * g + 1)
                dve.tensor_copy(probT[:, GB * g, :, :], bank[C_BANK["P0"]].rearrange("p (k q) -> p k q", k=BT)).then_inc(sm["pT0_copied"], 1)

            def o_norm(g):
                c = slice(g * GT, (g + 1) * GT)
                dve.wait_ge(sm["p_ready"], g + 1)
                mark(dve.reciprocal(rsum[:, c], psum_p[:, c]))
                dve.wait_ge(sm["prep_copied"], 7)
                dve.wait_ge(sm["o_done"], g + 1)
                settle()
                for i, t in enumerate(tiles(g)):
                    ins = dve.scalar_tensor_tensor(o_tok[:, t, :], bank[C_BANK["O"]][:, i * D:(i + 1) * D], rsum[:, t:t + 1],
                                                   bo_all[:, :], ALU.mult, ALU.add)
                ins.then_inc(sm["o_ready"], 1)

            def mix_stats(g):
                dve.wait_ge(sm["o_ready"], g + 1)
                layer_stats("c_out", of(o_tok), g)

            def d_stats(g):
                dve.wait_ge(sm["x3_ready"], g + 1)
                layer_stats("d_in", of(x3), g)

            def d_norm(g):
                normalise("d_in", d_tok, of(x3), g, sm["d_ready"])

            def lin_stats(k):
                def run(g):
                    dve.wait_ge(lin_done[k], g + 1)
                    layer_stats(f"d{k}", of_bank(C_BANK[f"L{k}"]), g)
                return run

            def residual(k):
                def run(g):
                    dve.wait_ge(res_done[k], g + 1)
                    b = V_BIAS + 2 * k + 1
                    dve.scalar_tensor_tensor(h_T[k + 1][:, toks(g)], bank[C_BANK[f"R{k}"]], vec[:, b:b + 1],
                                             h_T[k][:, toks(g)], ALU.add, ALU.add).then_inc(hT_ready[k], 1)
                return run

            def out_stats(g):
                dve.wait_ge(sm["fin_ready"], g + 1)
                layer_stats("d_out", of(h_out), g)

            def out_norm(g):
                normalise("d_out", u, of(h_out), g, sm["uo_ready"])

            flow(SECOND_BEATS, SECOND_EVERY, G, c_first=c_first, c_stats=c_stats, c_norm=c_norm, v1_evac=v1_evac,
                 score_max=score_max, p0=p_evac, o_norm=o_norm, o_stats=mix_stats, d_stats=d_stats, d_norm=d_norm,
                 lstats0=lin_stats(0), lstats1=lin_stats(1), lstats2=lin_stats(2), res0=residual(0), res1=residual(1),
                 ostats=out_stats, onorm=out_norm)


_INS = ['L0_attn_x', 'L0_attn_Wq', 'L0_attn_bq', 'L0_attn_Wk', 'L0_attn_bk', 'L0_attn_Wv', 'L0_attn_bv',
        'L0_attn_gamma', 'L0_attn_beta', 'L0_ffn_Wr', 'L0_ffn_W1', 'L0_ffn_b1', 'L0_ffn_W2', 'L0_ffn_b2',
        'L1_attn_Wq', 'L1_attn_bq', 'L1_attn_Wk', 'L1_attn_bk', 'L1_attn_Wv', 'L1_attn_bv', 'L1_attn_Wo',
        'L1_attn_bo', 'L1_ffn_qweights', 'L1_ffn_scales', 'L1_ffn_biases', 'L1_ffn_lora_a', 'L1_ffn_lora_b',
        'L1_ffn_ln_gamma', 'L1_ffn_ln_beta']


def kernel(**inputs):
    import numpy as _np
    import concourse.bacc as _bacc
    from concourse import mybir as _mybir
    from concourse.bass_utils import run_bass_kernel_spmd as _run

    nc = _bacc.Bacc("TRN2", target_bir_lowering=False, num_devices=1)
    arrays, args = {}, {}
    for name in _INS:
        x = _np.ascontiguousarray(inputs[name])
        arrays[f"in_{name}_dram"] = x
        args[name] = nc.dram_tensor(f"in_{name}_dram", x.shape, _mybir.dt.from_np(x.dtype), kind="ExternalInput").ap()
    shape = inputs["L0_attn_x"].shape
    args["out"] = nc.dram_tensor("out_0_dram", shape, _mybir.dt.float32, kind="ExternalOutput").ap()
    sandwich_kernel(nc, args)
    r = _run(nc, [arrays], core_ids=[0])
    return r.results[0]["out_0_dram"]
```

```python
from contextlib import ExitStack

import concourse.bass as bass
from concourse import mybir

ALU = mybir.AluOpType
ACT = mybir.ActivationFunctionType
AX = mybir.AxisListType
F32 = mybir.dt.float32
F16 = mybir.dt.float16
BF16 = mybir.dt.bfloat16
I32 = mybir.dt.int32
U32 = mybir.dt.uint32

P = 128
LN_EPS = 1e-5
DENOM_EPS = 1e-6
SCORE_BITS = 30


def flow(beats, every, groups, **steps):
    for _, g, name in sorted((beats[name] + every * g, g, name) for name in steps for g in range(groups)):
        steps[name](g)


def sandwich_kernel(nc, a):
    B, S, D = a["L0_attn_x"].shape
    E, _, HID = a["L0_ffn_W1"].shape
    N = B * S
    T = N // P
    GT = 4
    G = T // GT
    GN = GT * P
    BT = S // P
    GB = GT // BT
    H = 16
    HD = D // H
    KEEP = max(4, -(-N * 2 // E))
    SC = KEEP // P
    J = HID // P
    ROW = D + E
    NL = a["L1_ffn_qweights"].shape[0]
    R = a["L1_ffn_lora_a"].shape[1]
    NS = a["L1_ffn_scales"].shape[2]
    ATT_SCALE = 1.0 / float(D // 2) ** 0.5
    assert D == P and E * T == P and GT % BT == 0 and KEEP % P == 0

    ctx = ExitStack()
    with ctx:
        def sb(name, shape, dt=F32):
            return ctx.enter_context(nc.sbuf_tensor(name, shape, dt))

        def ps(name, shape, dt=F32):
            return ctx.enter_context(nc.psum_tensor(name, shape, dt))

        def sem(name):
            return ctx.enter_context(nc.semaphore(name))

        table = nc.dram_tensor("token_table", [N, ROW], F32, kind="Internal").ap()
        moe_sum = nc.dram_tensor("moe_sum", [N, D], F32, kind="Internal").ap()

        ident = sb("ident", [P, P])
        head_block = sb("head_block", [P, P])
        head_col = sb("head_col", [P, H])
        same_expert = sb("same_expert", [P, P], BF16)
        tile_before = sb("tile_before", [P, P], BF16)
        own_expert = sb("own_expert", [P, E], F16)
        tile_start_i = sb("tile_start_i", [P, E], I32)
        tile_start = sb("tile_start", [P, E], F16)
        tile_start_f = sb("tile_start_f", [P, E])
        slot_i = sb("slot_i", [P, KEEP], I32)
        slot_free = sb("slot_free", [P, KEEP])
        slot_part_i = sb("slot_part_i", [P, SC], I32)
        slot_part = sb("slot_part", [P, SC])
        zeros = sb("zeros", [P, T * D])
        ones3 = sb("ones3", [3, P], BF16)
        ones_row = sb("ones_row", [1, P])
        minus_half = sb("minus_half", [P, GT])

        w_raw = sb("w_raw", [P, 7, P])
        w_qT = sb("w_qT", [P, P])
        w_kvT = sb("w_kvT", [P, 2, P])
        w1_qT = sb("w1_qT", [P, P])
        w1_kT = sb("w1_kT", [P, P])
        w1_oT = sb("w1_oT", [P, P])
        w1_vo = sb("w1_vo", [P, P])
        bv_cols = sb("bv_cols", [P, P])
        bo_row = sb("bo_row", [1, P])
        bo_all = sb("bo_all", [P, P])
        NV = 32 + 15
        bq_col = sb("bq_col", [P, 1])
        vec_rows = sb("vec_rows", [NV, P])
        vec = sb("vec", [P, NV])
        NB = 2 * D + E * D + 4 * D
        NR = NB // D
        bias_rows = sb("bias_rows", [NR, D])
        bias_mean = sb("bias_mean", [NR, 1])
        centred = sb("centred", [NR, 1])
        bias_hi = sb("bias_hi", [NR, D], BF16)
        bias_mid = sb("bias_mid", [NR, D], BF16)
        bias_lo = sb("bias_lo", [NR, D], BF16)
        w_sum = sb("w_sum", [P, NL])
        w_nmean = sb("w_nmean", [P, NL])
        bias3 = sb("bias3", [3, NB], BF16)
        gamma_all = sb("gamma_all", [P, D])
        beta_all = sb("beta_all", [P, D])
        wr = sb("wr", [P, E])
        w1 = sb("w1", [P, E, HID])
        w2 = sb("w2", [P, E, J, D])
        q_int = sb("q_int", [P, NL, D], I32)
        q_scale = sb("q_scale", [P, NL, NS])
        q_w = sb("q_w", [P, NL, D])
        q_ws = sb("q_ws", [P, NL, D])
        lora_a = sb("lora_a", [R, NL, D])
        lora_b = sb("lora_b", [P, NL, R])
        lora_bT = sb("lora_bT", [R, NL, D])
        w_effT = sb("w_effT", [P, NL, D])

        x0 = sb("x0", [P, T, D])
        a_tok = sb("a_tok", [P, T, D])
        hT = sb("hT", [P, 2, J, KEEP])
        hT_flat = hT[:, :, :, :].rearrange("p a j k -> p (a j k)")
        aT = hT_flat[:, 0:T * P]
        qT = hT_flat[:, T * P:2 * T * P]
        xg = sb("xg", [P, E, SC, ROW])
        xg_flat = xg[:, :, :, :].rearrange("p e c r -> p (e c r)")
        k_tok = xg_flat[:, 0:T * D].rearrange("p (t d) -> p t d", d=D)
        VW = D + 4
        v_tok = xg_flat[:, T * D:T * (D + VW)].rearrange("p (t d) -> p t d", d=VW)
        kv_blk = sb("kv_blk", [P, B, D + H])
        den = sb("den", [P, T, H])
        rden = sb("rden", [P, T, H])
        y0 = sb("y0", [P, T, D])
        y1 = sb("y1", [P, T, D])
        z = sb("z", [P, T, D])
        u = y0
        x1 = sb("x1", [P, T, D])
        tab = sb("tab", [P, T, ROW])
        bT = sb("bT", [P, T * P])
        stats = sb("stats", [P, T, 6])

        class Norm:
            def __init__(self, name):
                self.mv = sb(f"mv_{name}", [P, T, 2])
                self.ve = sb(f"ve_{name}", [P, T])
                self.rstd = sb(f"rstd_{name}", [P, T])
                self.nmean = sb(f"nmean_{name}", [P, T])
                self.shift = sb(f"shift_{name}", [P, T])
                self.stats_ready = sem(f"stats_{name}")
                self.rstd_ready = sem(f"rstd_{name}_ready")

        ln = {n: Norm(n) for n in ("a_in", "a_mid", "a_out", "b_in", "b_out", "c_in", "c_out",
                                   "d_in", "d0", "d1", "d2", "d_out")}

        table_out = sb("table_out", [P, 1])
        logit_max = sb("logit_max", [P, T])
        shifted = sb("shifted", [P, T, E])
        expd = sb("expd", [P, T, E])
        expsum = sb("expsum", [P, T])
        rexpsum = sb("rexpsum", [P, T])
        sc_et = sb("sc_et", [P, E, T])
        scoreT = sb("scoreT", [P, P])
        ROUNDS = SCORE_BITS // 2
        ROUND_SHIFT = [SCORE_BITS - 2 * (k + 1) for k in range(ROUNDS)]
        quarters = sb("quarters", [P, 4], I32)
        cand = sb("cand", [P, 2, 4], I32)
        reached = sb("reached", [P, 3])
        reached_count = sb("reached_count", [P, 1])
        quarter = sb("quarter", [P, 1], I32)
        hits = sb("hits", [P, 3, P], BF16)
        hit_count = sb("hit_count", [P, 3], BF16)
        above = sb("above", [P, P], BF16)
        tied = sb("tied", [P, P], BF16)
        above_count = sb("above_count", [P, 1], BF16)
        tied_count = sb("tied_count", [P, 1], BF16)
        tie_room = sb("tie_room", [P, 2])
        tie_rank = sb("tie_rank", [P, P])
        tie_kept = sb("tie_kept", [P, P])
        kept_rank = sb("kept_rank", [P, P])
        kept_count = sb("kept_count", [P, 1], BF16)
        kept_first = sb("kept_first", [P, 1])
        rank_all = sb("rank_all", [P, P], F16)
        rank_last = sb("rank_last", [P, 1])
        rank_by_expert = sb("rank_by_expert", [P, E, P], F16)
        from_first = sb("from_first", [P, KEEP], F16)
        slot_row = sb("slot_row", [P, KEEP], F16)
        passed = sb("passed", [P, SC, P], BF16)
        passed_count = sb("passed_count", [P, SC, E])
        first_token = sb("first_token", [P, SC, E])
        token_of = sb("token_of", [P, SC, E], U32)

        SLOT_BANKS = (2, 3, 4, 5, 0, 7, 6, 1)
        LISTS_FIRST = 5
        AHEAD = 6

        a_flat = a_tok[:, :, :].rearrange("p t d -> p (t d)")
        xgT = a_flat[:, 0:2 * KEEP].rearrange("p (a k) -> p a k", a=2)
        YB = 4
        yg = y0[:, :, :].rearrange("p (a c) d -> p a c d", a=YB)
        moe = y1

        x2 = x0
        c_tok = a_tok
        cT = aT
        q1T = qT
        k1T = xg_flat[:, T * D:2 * T * D]
        v1 = k_tok
        smax = sb("smax", [P, T])
        nsmax = sb("nsmax", [P, T])
        prob = w1[:, :, :].rearrange("p e h -> p (e h)").rearrange("p (t s) -> p t s", s=S)
        psum_p = sb("psum_p", [P, T])
        rsum = sb("rsum", [P, T])
        probT = w2[:, :, :, :].rearrange("p e j d -> p (e j d)").rearrange("p (b k q) -> p b k q", b=B, k=BT)
        o_tok = y0
        x3 = x1
        d_tok = y0
        h_T = [bT, q1T, k1T]
        n_tok = y1
        g_T = aT
        w_out = z
        h_out = z
        y_out = zeros[:, :].rearrange("p (t d) -> p t d", d=D)

        banks = ps("banks", [P, 8, 512])
        bank = [banks[:, i, :] for i in range(8)]

        names = """constants
        ld_first ld_w ld_vec ld_bias ld_small ld_experts ld_lin
        prep_done prep_copied q_ready bv_ready fin_done fin_ready
        eff_mean bias_parts bias_ready
        a_ready aT_done aT_copied q_done qT_ready kv0_done kv1_done kv0_ready kv1_ready ksum_done kv_ready ctx_done y0_ready y1_ready mid_ready
        u_ready x1_ready
        b_ready bT_done bT_copied logit_done shifted_ready exp_ready scores_ready scoreT_done scoreT_ready
        cand_counted cand_summed cand_taken room_ready first_ready sel_counted sel_summed kept_counted kept_summed slots_ready ranks_ready slots_done slots_used start_done first_token_ready
        token_ready table_written zero_written
        gT_done gT_copied h_done h_ready y_done yg_ready
        uc_ready x2_ready c_ready cT_done cT_copied q1_done q1_ready k1_done k1_ready v1_done v1_ready
        s_done smax_ready p_ready pT_done pT0_copied pT1_copied o_done o_ready ud_ready x3_ready
        d_ready dT_done dT_copied uo_ready out_ready out_written
        dve_step pool_step""".split()
        sm = {n: sem(n) for n in names}
        ld_x = [sem(f"ld_x{g}") for g in range(G)]
        gathered = [sem(f"gathered{i}") for i in range(E)]
        moe_loaded = [sem(f"moe_loaded{g}") for g in range(G)]
        scattered = [sem(f"scattered{i}") for i in range(2)]
        lin_done = [sem(f"lin_done{k}") for k in range(3)]
        n_ready = [sem(f"n_ready{k}") for k in range(3)]
        nT_done = [sem(f"nT_done{k}") for k in range(3)]
        gelu_ready = [sem(f"gelu_ready{k}") for k in range(3)]
        res_done = [sem(f"res_done{k}") for k in range(2)]
        hT_ready = [sem(f"hT_ready{k}") for k in range(2)]

        x_dram = a["L0_attn_x"].rearrange("b (t p) d -> p (b t) d", p=P)
        out_dram = a["out"].rearrange("b (t p) d -> p (b t) d", p=P)
        moe_dram = moe_sum.rearrange("(t p) d -> p t d", p=P)

        def tiles(g):
            return range(g * GT, (g + 1) * GT)

        def toks(g):
            return slice(g * GN, (g + 1) * GN)

        IDENT_SET, ONES_SET, CENTRED_SET, HEADS_SET, EXPERTS_SET, SLOTS_SET = range(1, 7)
        V_B1, V_BQ1, V_BK1, V_BV1, V_G, V_BE, V_BIAS = 0, 32, 33, 34, 35, 38, 41
        R_KV, R_B2, R_LIN = 0, 2 * D, 2 * D + E * D

        A_BANK = dict(T=1, Q=2, KV0=0, KV1=1, MIX=0, C0=5, C1=6, BT=4)
        C_BANK = dict(TURN=7, Q=3, K=6, V=7, O=2, S0=4, S1=5, P0=1, P1=2, DT=5, L0=3, L1=0, L2=7, NT0=4, NT1=2, NT2=3, R0=5, R1=6, FIN=4)
        FIRST_BEATS = dict(a_stats=0, bias=1, r_a_in=28, masks=29, a_norm=99, a_turn=139, a_evac=140, kv1=149,
                           kv1_evac=170, kv0=184, q=193, kv0_evac=201, mix=205, q_evac=220, mask=226, ctx=244,
                           divide=247, y1=260, m_stats=280, r_a_mid=301, m_norm=318, m_scale=343, o_stats=354,
                           r_a_out=379, o_norm=398, weights=418, x1=419, vectors=419, weights_out=428, b_stats=494,
                           b_turn=498, r_b_in=507, b_norm=571, logits=580, b_evac=605)
        SECOND_BEATS = dict(c_first=0, r_b_out=20, n_b_out=83, x2=104, c_stats=136, r_c_in=146, c_norm=163,
                            c_turn=163, c_evac=177, k1=190, q1=198, k1_evac=202, q1_evac=202, v1=210, v1_evac=217,
                            score=229, score_max=238, exps=266, pturn=290, p1=303, p0=304, out=322, o_norm=344,
                            o_stats=345, r_c_out=375, n_c_out=393, x3=414, d_stats=431, r_d_in=452, d_norm=466,
                            d_turn=482, d_evac=494, lin0=503, lstats0=517, r_d0=524, lnorm0=553, gelu0=564,
                            nturn0=566, back0=577, res0=586, lin1=608, lstats1=627, r_d1=637, lnorm1=657, nturn1=667,
                            gelu1=671, back1=684, res1=701, lin2=726, r_d2=738, lstats2=740, lnorm2=771, nturn2=802,
                            gelu2=815, back2=825, fin=860, ostats=873, r_out=879, onorm=941, y=961)
        WEIGHT_BANK, VECTOR_BANK = A_BANK["Q"], A_BANK["BT"]
        FIRST_BANK = 7
        FIRST_EVERY, SECOND_EVERY = 63, 66

        block = ctx.enter_context(nc.Block())

        @block.sync
        def _(sp):
            row = lambda n: a[n].rearrange("(o d) -> o d", o=1)

            def load_x(g):
                sp.dma_start(x0[:, g * GT:(g + 1) * GT, :], x_dram[:, g * GT:(g + 1) * GT, :]).then_inc(ld_x[g], 16)

            load_x(0)
            sp.dma_start(bias_rows[2:2 + E, :], a["L0_ffn_b2"]).then_inc(sm["ld_bias"], 16)
            sp.dma_start(bias_rows[2 + E:5 + E, :], a["L1_ffn_biases"][0:5:2, :]).then_inc(sm["ld_bias"], 16)
            sp.dma_start(bias_rows[5 + E:6 + E, :], a["L1_ffn_biases"][5:6, :]).then_inc(sm["ld_bias"], 16)
            sp.dma_start(bq_col[:, :], a["L0_attn_bq"].rearrange("(d o) -> d o", o=1)).then_inc(sm["ld_first"], 16)
            load_x(1)
            load_x(2)
            for r, part in enumerate((bias_hi, bias_mid, bias_lo)):
                sp.wait_ge(sm["bias_parts"], r + 1)
                sp.dma_start(bias3[r:r + 1, :].rearrange("o (r d) -> o r d", d=D), part[:, :]).then_inc(sm["bias_ready"], 16)
            load_x(3)
            for i, n in ((3, "L1_attn_Wq"), (4, "L1_attn_Wk"), (5, "L1_attn_Wv"), (6, "L1_attn_Wo")):
                sp.dma_start(w_raw[:, i, :], a[n]).then_inc(sm["ld_w"], 16)
            for dst, n in ((V_BQ1, "L1_attn_bq"), (V_BK1, "L1_attn_bk"), (V_BV1, "L1_attn_bv")):
                sp.dma_start(vec_rows[dst:dst + 1, :], row(n)).then_inc(sm["ld_vec"], 16)
            sp.dma_start(vec_rows[V_B1:V_B1 + E * J, :], a["L0_ffn_b1"].rearrange("e (j p) -> (e j) p", p=P)).then_inc(sm["ld_vec"], 16)
            sp.dma_start(vec_rows[V_G:V_G + 3, :], a["L1_ffn_ln_gamma"]).then_inc(sm["ld_vec"], 16)
            sp.dma_start(vec_rows[V_BE:V_BE + 3, :], a["L1_ffn_ln_beta"]).then_inc(sm["ld_vec"], 16)
            sp.dma_start(vec_rows[V_BIAS:V_BIAS + NL, :], a["L1_ffn_biases"]).then_inc(sm["ld_vec"], 16)
            sp.dma_start(gamma_all[:, :], row("L0_attn_gamma").to_broadcast([P, D])).then_inc(sm["ld_small"], 16)
            sp.dma_start(beta_all[:, :], row("L0_attn_beta").to_broadcast([P, D])).then_inc(sm["ld_small"], 16)
            sp.dma_start(wr[:, :], a["L0_ffn_Wr"]).then_inc(sm["ld_small"], 16)
            sp.dma_start(bo_row[:, :], row("L1_attn_bo")).then_inc(sm["ld_small"], 16)
            sp.dma_start(q_int[:, :, :], a["L1_ffn_qweights"].rearrange("l o i -> o l i")).then_inc(sm["ld_lin"], 16)
            sp.dma_start(q_scale[:, :, :], a["L1_ffn_scales"].rearrange("l o s -> o l s")).then_inc(sm["ld_lin"], 16)
            sp.dma_start(lora_a[:, :, :], a["L1_ffn_lora_a"].rearrange("l r i -> r l i")).then_inc(sm["ld_lin"], 16)
            sp.dma_start(lora_b[:, :, :], a["L1_ffn_lora_b"].rearrange("l o r -> o l r")).then_inc(sm["ld_lin"], 16)
            sp.dma_start(w1[:, :, :], a["L0_ffn_W1"].rearrange("e d h -> d e h")).then_inc(sm["ld_experts"], 16)
            sp.dma_start(w2[:, :, :, :], a["L0_ffn_W2"].rearrange("e (j p) d -> p e j d", p=P)).then_inc(sm["ld_experts"], 16)
            sp.wait_ge(sm["constants"], SLOTS_SET)
            sp.dma_start(moe_dram, zeros[:, :].rearrange("p (t d) -> p t d", d=D)).then_inc(sm["zero_written"], 16)
            sp.wait_ge(sm["scores_ready"], 1)
            sp.dma_start(table.rearrange("(t p) c -> p t c", p=P), tab[:, :, :]).then_inc(sm["table_written"], 16)
            sp.wait_ge(scattered[(E - 1) % 2], 16 * SC * (E // 2))
            for g in range(G):
                c = slice(g * GT, (g + 1) * GT)
                sp.dma_start(moe[:, c, :], moe_dram[:, c, :]).then_inc(moe_loaded[g], 16)
            for g in range(G):
                sp.wait_ge(sm["out_ready"], g + 1)
                sp.dma_start(out_dram[:, g * GT:(g + 1) * GT, :], y_out[:, g * GT:(g + 1) * GT, :]).then_inc(sm["out_written"], 16)
            sp.wait_ge(sm["out_written"], 16 * G)

        @block.gpsimd
        def _(pool):
            step = [0]

            def link(ins):
                step[0] += 1
                ins.then_inc(sm["pool_step"], 1)
                pool.wait_ge(sm["pool_step"], step[0])

            def band(view, pattern, mult):
                base, pat = pattern
                link(pool.affine_select(out=view, in_=view, compare_op=ALU.is_ge, fill=0.0, base=base,
                                        pattern=pat, channel_multiplier=mult))

            pool.memset(minus_half[:, :], -0.5)
            link(pool.memset(ident[:, :], 0.0))
            pool.affine_select(out=ident[:, :], in_=ident[:, :], compare_op=ALU.not_equal, fill=1.0, base=0,
                               pattern=[[-1, P]], channel_multiplier=1).then_inc(sm["constants"], 1)
            pool.memset(ones3[:, :], 1.0)
            pool.memset(ones_row[:, :], 1.0)
            pool.memset(v_tok[:, :, D:D + 1], 1.0).then_inc(sm["constants"], 1)
            link(pool.memset(centred[:, :], 1.0 / D))
            band(centred[:, :], (-(2 + E), [[0, 1]]), 1)
            pool.affine_select(out=centred[:, :], in_=centred[:, :], compare_op=ALU.is_ge, fill=0.0, base=2 + E + 2,
                               pattern=[[0, 1]], channel_multiplier=-1).then_inc(sm["constants"], 1)

            def masks(g):
                if g:
                    return
                link(pool.memset(head_block[:, :], 1.0))
                hb = head_block[:, :].rearrange("p (h d) -> p h d", d=HD)
                band(hb, (0, [[-HD, H], [0, HD]]), 1)
                band(hb, (HD - 1, [[HD, H], [0, HD]]), -1)
                link(pool.memset(head_col[:, :], 1.0))
                band(head_col[:, :], (0, [[-HD, H]]), 1)
                pool.affine_select(out=head_col[:, :], in_=head_col[:, :], compare_op=ALU.is_ge, fill=0.0, base=HD - 1,
                                   pattern=[[HD, H]], channel_multiplier=-1).then_inc(sm["constants"], 1)

            def route_masks():
                pool.iota(quarters[:, :], [[1, 4]], base=0, channel_multiplier=0)
                link(pool.memset(same_expert[:, :], 1.0))
                se = same_expert[:, :].rearrange("p (e t) -> p e t", t=T)
                band(se, (0, [[-T, E], [0, T]]), 1)
                band(se, (T - 1, [[T, E], [0, T]]), -1)
                link(pool.tensor_copy(tile_before[:, :], same_expert[:, :]))
                pool.affine_select(out=tile_before[:, :], in_=tile_before[:, :], compare_op=ALU.is_ge, fill=0.0, base=-1,
                                   pattern=[[1, P]], channel_multiplier=-1).then_inc(sm["constants"], 1)

            def slot_constants():
                link(pool.memset(own_expert[:, :], 1.0))
                band(own_expert[:, :], (0, [[-T, E]]), 1)
                band(own_expert[:, :], (T - 1, [[T, E]]), -1)
                link(pool.iota(tile_start_i[:, :], [[-T * P, E]], base=0, channel_multiplier=P))
                link(pool.tensor_copy(tile_start_f[:, :], tile_start_i[:, :]))
                pool.tensor_tensor(tile_start[:, :], tile_start_f[:, :], own_expert[:, :], ALU.mult)
                link(pool.iota(slot_i[:, :], [[1, KEEP]], base=0, channel_multiplier=0))
                pool.tensor_copy(slot_free[:, :], slot_i[:, :])
                link(pool.iota(slot_part_i[:, :], [[P, SC]], base=0, channel_multiplier=1))
                pool.tensor_copy(slot_part[:, :], slot_part_i[:, :])
                pool.memset(zeros[:, :], 0.0).then_inc(sm["constants"], 1)

            def rstd(n, shift=False):
                def run(g):
                    L = ln[n]
                    c = slice(g * GT, (g + 1) * GT)
                    pool.wait_ge(L.stats_ready, g + 1)
                    ve = pool.tensor_scalar(L.ve[:, c], L.mv[:, c, 1], LN_EPS, None, ALU.add)
                    step[0] += 1
                    ve.then_inc(sm["pool_step"], 1)
                    if shift:
                        nm = pool.tensor_scalar(L.nmean[:, c], L.mv[:, c, 0], -1.0, None, ALU.mult)
                        step[0] += 1
                        nm.then_inc(sm["pool_step"], 1)
                    pool.wait_ge(sm["pool_step"], step[0])
                    root = pool.tensor_tensor(L.rstd[:, c], L.ve[:, c], minus_half[:, :], ALU.pow)
                    if shift:
                        link(root)
                        pool.tensor_tensor(L.shift[:, c], L.nmean[:, c], L.rstd[:, c], ALU.mult).then_inc(L.rstd_ready, 1)
                    else:
                        root.then_inc(L.rstd_ready, 1)
                return run

            def add(out, in0, in1, waits, done):
                def run(g):
                    c = slice(g * GT, (g + 1) * GT)
                    for s in waits:
                        pool.wait_ge(sm[s], g + 1)
                    pool.tensor_tensor(out[:, c, :], in0[:, c, :], in1[:, c, :], ALU.add).then_inc(sm[done], 1)
                return run

            flow(FIRST_BEATS, FIRST_EVERY, G, r_a_in=rstd("a_in", True), masks=masks,
                 y1=add(y1, y0, a_tok, ["y0_ready"], "y1_ready"), r_a_mid=rstd("a_mid", True), r_a_out=rstd("a_out", True),
                 x1=add(x1, x0, u, ["u_ready"], "x1_ready"), r_b_in=rstd("b_in"))
            route_masks()

            pool.wait_ge(sm["ld_lin"], 64)
            link(pool.tensor_scalar(q_w[:, :, :], q_int[:, :, :], 1.0 / 7.5, -1.0, ALU.mult, ALU.add))
            pool.tensor_tensor(q_ws[:, :, :].rearrange("p l (s k) -> p (l s) k", s=NS),
                               q_w[:, :, :].rearrange("p l (s k) -> p (l s) k", s=NS),
                               q_scale[:, :, :].rearrange("p l s -> p (l s)").unsqueeze(2).to_broadcast([P, NL * NS, D // NS]),
                               ALU.mult).then_inc(sm["q_ready"], 1)
            slot_constants()

            def gather(e):
                pool.wait_ge(sm["token_ready"], e + 1)
                for c in range(SC):
                    pool.indirect_dma_start(
                        out=xg[:, e, c, :], out_offset=None, in_=table,
                        in_offset=bass.IndirectOffsetOnAxis(ap=token_of[:, c, e:e + 1], axis=0)).then_inc(gathered[e], 16)

            def scatter(e):
                if e:
                    pool.wait_ge(scattered[(e - 1) % 2], 16 * SC * ((e - 1) // 2 + 1))
                else:
                    pool.wait_ge(sm["zero_written"], 16)
                for c in range(SC):
                    pool.wait_ge(sm["yg_ready"], SC * e + c + 1)
                    pool.indirect_dma_start(
                        out=moe_sum, out_offset=bass.IndirectOffsetOnAxis(ap=token_of[:, c, e:e + 1], axis=0),
                        in_=yg[:, e % YB, c, :], in_offset=None, compute_op=ALU.add).then_inc(scattered[e % 2], 16)

            pool.wait_ge(sm["table_written"], 16)
            for e in range(AHEAD):
                gather(e)
            for e in range(E):
                scatter(e)
                if e + AHEAD < E:
                    gather(e + AHEAD)

            flow(SECOND_BEATS, SECOND_EVERY, G, r_b_out=rstd("b_out", True), x2=add(x2, x1, z, ["uc_ready"], "x2_ready"),
                 r_c_in=rstd("c_in"), r_c_out=rstd("c_out", True), x3=add(x3, x2, w_out, ["ud_ready"], "x3_ready"),
                 r_d_in=rstd("d_in"), r_d0=rstd("d0"), r_d1=rstd("d1"), r_d2=rstd("d2"), r_out=rstd("d_out"),
                 y=add(y_out, x3, u, ["uo_ready"], "out_ready"))

        @block.scalar
        def _(act):
            def copy(dst, src, func=ACT.Copy, **kw):
                return act.activation(dst, src, func, **kw)

            def normalise(n, dst, src, g, done):
                L = ln[n]
                act.wait_ge(L.rstd_ready, g + 1)
                for t in tiles(g):
                    ins = copy(dst[:, t, :], src[:, t, :], ACT.Identity, scale=L.rstd[:, t:t + 1], bias=L.shift[:, t:t + 1])
                ins.then_inc(done, 1)

            row = lambda n: a[n].rearrange("(o d) -> o d", o=1)
            for i, n in enumerate(("L0_attn_Wq", "L0_attn_Wk", "L0_attn_Wv")):
                act.dma_start(w_raw[:, i, :], a[n]).then_inc(sm["ld_first"], 16)
            for r, n in enumerate(("L0_attn_bk", "L0_attn_bv")):
                act.dma_start(bias_rows[r:r + 1, :], row(n)).then_inc(sm["ld_bias"], 16)

            def a_norm(g):
                normalise("a_in", a_tok, x0, g, sm["a_ready"])
                if g == 0:
                    act.wait_ge(sm["prep_done"], 1)
                    copy(w_qT[:, :], bank[FIRST_BANK][:, 0:P])
                    copy(w_kvT[:, :, :], bank[FIRST_BANK][:, P:3 * P].rearrange("p (a b) -> p a b", a=2)).then_inc(sm["prep_copied"], 1)

            def weights_out(g):
                if g:
                    return
                act.wait_ge(sm["prep_done"], 2)
                copy(w1_qT[:, :], bank[WEIGHT_BANK][:, 0:P])
                copy(w1_kT[:, :], bank[WEIGHT_BANK][:, P:2 * P])
                copy(w1_oT[:, :], bank[WEIGHT_BANK][:, 2 * P:3 * P]).then_inc(sm["prep_copied"], 1)
                act.wait_ge(sm["prep_done"], 3)
                copy(vec[:, :], bank[VECTOR_BANK][:, 0:NV]).then_inc(sm["prep_copied"], 1)

            def a_evac(g):
                act.wait_ge(sm["aT_done"], g + 1)
                copy(aT[:, toks(g)], bank[A_BANK["T"]]).then_inc(sm["aT_copied"], 1)

            def q_evac(g):
                if g == 0:
                    act.wait_ge(sm["ld_first"], 16 * 4)
                act.wait_ge(sm["q_done"], g + 1)
                copy(qT[:, toks(g)], bank[A_BANK["Q"]], ACT.Relu, bias=bq_col[:, :]).then_inc(sm["qT_ready"], 1)

            def kv_evac(g):
                act.wait_ge(sm["kv0_done"], g + 1)
                t = g * GT
                kv = bank[A_BANK["KV0"]].rearrange("p (t c) -> p t c", t=2)
                copy(k_tok[:, t:t + 2, :], kv[:, :, 0:D], ACT.Relu)
                copy(v_tok[:, t:t + 2, 0:D], kv[:, :, D:2 * D]).then_inc(sm["kv0_ready"], 1)

            def b_evac(g):
                act.wait_ge(sm["bT_done"], g + 1)
                copy(bT[:, toks(g)], bank[A_BANK["BT"]]).then_inc(sm["bT_copied"], 1)

            flow(FIRST_BEATS, FIRST_EVERY, G, a_norm=a_norm, a_evac=a_evac,
                 q_evac=q_evac, kv0_evac=kv_evac, m_norm=lambda g: normalise("a_mid", z, y1, g, sm["mid_ready"]),
                 o_norm=lambda g: normalise("a_out", u, z, g, sm["u_ready"]), weights_out=weights_out, b_evac=b_evac)

            def load_table(func):
                copy(table_out[:, :], minus_half[:, 0:1], func)

            act.wait_ge(sm["shifted_ready"], 1)
            copy(expd[:, :, :], shifted[:, :, :], ACT.Exp).then_inc(sm["exp_ready"], 1)

            for h in range(2):
                act.wait_ge(sm["prep_done"], 4 + h)
                copy(lora_bT[:, 3 * h:3 * h + 3, :], bank[1 + h][0:R, 0:3 * P].rearrange("p (a b) -> p a b", a=3)).then_inc(sm["prep_copied"], 1)
            act.wait_ge(sm["prep_done"], 6)
            copy(w1_vo[:, :], bank[3][:, 0:P]).then_inc(sm["prep_copied"], 1)
            act.wait_ge(sm["prep_done"], 7)
            copy(bo_all[:, :], bank[3][:, 0:P]).then_inc(sm["prep_copied"], 1)
            for h in range(2):
                act.wait_ge(sm["prep_done"], 8 + h)
                for i in range(3 * h, 3 * h + 3):
                    ins = copy(w_effT[:, i, :], bank[5 + h][:, (i % 3) * P:(i % 3 + 1) * P], accum_out=w_sum[:, i:i + 1])
                ins.then_inc(sm["prep_copied"], 1)
            act.wait_ge(sm["prep_copied"], 9)
            copy(w_nmean[:, :], w_sum[:, :], scale=-1.0 / D).then_inc(sm["eff_mean"], 1)
            act.wait_ge(sm["eff_mean"], 1)
            for i in range(0, NL, 2):
                ins = copy(w_effT[:, i, :], w_effT[:, i, :], ACT.Identity, bias=w_nmean[:, i:i + 1])
            ins.then_inc(sm["eff_mean"], 1)

            load_table(ACT.Gelu)
            for e in range(E):
                for j in range(J):
                    act.wait_ge(sm["h_done"], e * J + j + 1)
                    if j == 0 and e >= 2:
                        act.wait_ge(sm["y_done"], SC // 2 * (e - 1))
                    copy(hT[:, e % 2, j, :], bank[2 + j], ACT.Gelu,
                         bias=vec[:, V_B1 + e * J + j:V_B1 + e * J + j + 1]).then_inc(sm["h_ready"], 1)

            load_table(ACT.Exp)

            def c_evac(g):
                act.wait_ge(sm["cT_done"], g + 1)
                copy(cT[:, toks(g)], bank[C_BANK["TURN"]]).then_inc(sm["cT_copied"], 1)

            def q1_evac(g):
                act.wait_ge(sm["q1_done"], g + 1)
                copy(q1T[:, toks(g)], bank[C_BANK["Q"]], ACT.Identity, bias=vec[:, V_BQ1:V_BQ1 + 1]).then_inc(sm["q1_ready"], 1)

            def k1_evac(g):
                act.wait_ge(sm["k1_done"], g + 1)
                copy(k1T[:, toks(g)], bank[C_BANK["K"]], ACT.Identity, bias=vec[:, V_BK1:V_BK1 + 1]).then_inc(sm["k1_ready"], 1)

            def exps(g):
                act.wait_ge(sm["smax_ready"], g + 1)
                for t in tiles(g):
                    i = t - g * GT
                    ins = copy(prob[:, t, :], bank[C_BANK[f"S{i // 2}"]][:, (i % 2) * S:(i % 2 + 1) * S], ACT.Exp,
                               bias=nsmax[:, t:t + 1], scale=ATT_SCALE, accum_out=psum_p[:, t:t + 1])
                ins.then_inc(sm["p_ready"], 1)

            def p_evac(g):
                act.wait_ge(sm["pT_done"], GB * g + GB)
                copy(probT[:, GB * g + 1, :, :], bank[C_BANK["P1"]].rearrange("p (k q) -> p k q", k=BT)).then_inc(sm["pT1_copied"], 1)

            def d_evac(g):
                act.wait_ge(sm["dT_done"], g + 1)
                copy(h_T[0][:, toks(g)], bank[C_BANK["DT"]]).then_inc(sm["dT_copied"], 1)

            def gelu(k):
                def run(g):
                    act.wait_ge(nT_done[k], g + 1)
                    if k:
                        act.wait_ge(res_done[k - 1], g + 1)
                    copy(g_T[:, toks(g)], bank[C_BANK[f"NT{k}"]], ACT.Gelu, scale=vec[:, V_G + k:V_G + k + 1],
                         bias=vec[:, V_BE + k:V_BE + k + 1]).then_inc(gelu_ready[k], 1)
                return run

            def lin_norm(k):
                def run(g):
                    L = ln[f"d{k}"]
                    act.wait_ge(L.rstd_ready, g + 1)
                    for i, t in enumerate(tiles(g)):
                        ins = copy(n_tok[:, t, :], bank[C_BANK[f"L{k}"]][:, i * D:(i + 1) * D], scale=L.rstd[:, t:t + 1])
                    ins.then_inc(n_ready[k], 1)
                return run

            def fin_evac(g):
                act.wait_ge(sm["fin_done"], g + 1)
                copy(h_out[:, g * GT:(g + 1) * GT, :], bank[C_BANK["FIN"]].rearrange("p (t d) -> p t d", t=GT)).then_inc(sm["fin_ready"], 1)

            flow(SECOND_BEATS, SECOND_EVERY, G, n_b_out=lambda g: normalise("b_out", z, moe, g, sm["uc_ready"]), c_evac=c_evac,
                 q1_evac=q1_evac, k1_evac=k1_evac, exps=exps, p1=p_evac,
                 n_c_out=lambda g: normalise("c_out", w_out, o_tok, g, sm["ud_ready"]), d_evac=d_evac,
                 lnorm0=lin_norm(0), lnorm1=lin_norm(1), lnorm2=lin_norm(2), gelu0=gelu(0), gelu1=gelu(1), gelu2=gelu(2),
                 fin=fin_evac)

        @block.tensor
        def _(pe):
            tenant = {}

            def claim(b, leaves, count):
                if b in tenant:
                    pe.wait_ge(*tenant[b])
                tenant[b] = (leaves, count)
                return bank[b]

            def mm(out, lhsT, rhs, start=True, stop=True):
                return pe.matmul(out, lhsT, rhs, start=start, stop=stop)

            def turn(out, in_, n=P):
                return pe.transpose(out, in_, ident[0:n, 0:n])

            def turn4(o, src, g, done):
                for i, t in enumerate(tiles(g)):
                    ins = turn(o[:, i * P:(i + 1) * P], src[:, t, 0:P])
                ins.then_inc(done, 1)

            pe.wait_ge(sm["constants"], IDENT_SET)
            pe.wait_ge(sm["ld_first"], 16 * 4)
            o = claim(FIRST_BANK, sm["prep_copied"], 1)
            for i in range(3):
                ins = turn(o[:, i * P:(i + 1) * P], w_raw[:, i, :])
            ins.then_inc(sm["prep_done"], 1)

            def weights(g):
                if g:
                    return
                pe.wait_ge(sm["ld_w"], 16 * 4)
                o = claim(WEIGHT_BANK, sm["prep_copied"], 2)
                for i, w in enumerate((3, 4, 6)):
                    ins = turn(o[:, i * P:(i + 1) * P], w_raw[:, w, :])
                ins.then_inc(sm["prep_done"], 1)

            def vectors(g):
                if g:
                    return
                pe.wait_ge(sm["ld_vec"], 16 * 7)
                turn(claim(VECTOR_BANK, sm["prep_copied"], 3)[:, 0:NV], vec_rows[:, :], NV).then_inc(sm["prep_done"], 1)

            def a_turn(g):
                pe.wait_ge(sm["a_ready"], g + 1)
                turn4(claim(A_BANK["T"], sm["aT_copied"], g + 1), a_tok, g, sm["aT_done"])

            def a_query(g):
                pe.wait_ge(sm["aT_copied"], g + 1)
                if g == 0:
                    pe.wait_ge(sm["prep_copied"], 1)
                mm(claim(A_BANK["Q"], sm["qT_ready"], g + 1), w_qT[:, :], aT[:, toks(g)]).then_inc(sm["q_done"], 1)

            def a_key_value(i):
                def run(g):
                    pe.wait_ge(sm["aT_copied"], g + 1)
                    if g == 0:
                        pe.wait_ge(sm["bias_ready"], 48)
                        pe.wait_ge(sm["constants"], ONES_SET)
                    o = claim(A_BANK[f"KV{i}"], sm[f"kv{i}_ready"], g + 1)
                    for j in range(2):
                        t = g * GT + 2 * i + j
                        oj = o[:, j * 2 * D:(j + 1) * 2 * D]
                        mm(oj, aT[:, t * P:(t + 1) * P], w_kvT[:, :, :].rearrange("p a b -> p (a b)"), True, False)
                        ins = mm(oj, ones3[:, :], bias3[:, R_KV:R_KV + 2 * D], False, True)
                    ins.then_inc(sm[f"kv{i}_done"], 1)
                return run

            def a_mix(g):
                pe.wait_ge(sm["kv0_ready"], g + 1)
                pe.wait_ge(sm["kv1_ready"], g + 1)
                if g == 0:
                    pe.wait_ge(sm["constants"], ONES_SET)
                o = claim(A_BANK["MIX"], sm["kv_ready"], g + 1)
                for b in range(GB):
                    for i in range(BT):
                        t = g * GT + b * BT + i
                        ins = mm(o[:, b * 256:b * 256 + D + 1], k_tok[:, t, :], v_tok[:, t, 0:D + 1], i == 0, i == BT - 1)
                ins.then_inc(sm["ksum_done"], 1)

            def a_ctx(g):
                pe.wait_ge(sm["kv_ready"], g + 1)
                pe.wait_ge(sm["qT_ready"], g + 1)
                o2 = [claim(A_BANK[f"C{i}"], sm["y0_ready"], g + 1) for i in range(2)]
                for i, t in enumerate(tiles(g)):
                    ins = mm(o2[i // 2][:, (i % 2) * 256:(i % 2) * 256 + D + H], qT[:, t * P:(t + 1) * P], kv_blk[:, t // BT, :])
                ins.then_inc(sm["ctx_done"], 1)

            def b_turn(g):
                pe.wait_ge(sm["b_ready"], g + 1)
                turn4(claim(A_BANK["BT"], sm["bT_copied"], g + 1), tab, g, sm["bT_done"])

            def logits(g):
                pe.wait_ge(sm["bT_copied"], g + 1)
                if g == 0:
                    pe.wait_ge(sm["ld_small"], 64)
                    claim(7, sm["shifted_ready"], 1)
                for t in tiles(g):
                    ins = mm(bank[7][:, t * E:(t + 1) * E], bT[:, t * P:(t + 1) * P], wr[:, :])
                ins.then_inc(sm["logit_done"], 1)

            flow(FIRST_BEATS, FIRST_EVERY, G, a_turn=a_turn, q=a_query, kv0=a_key_value(0), kv1=a_key_value(1), mix=a_mix,
                 ctx=a_ctx, weights=weights, vectors=vectors, b_turn=b_turn, logits=logits)

            pe.wait_ge(sm["scores_ready"], 1)
            turn(claim(7, sm["scoreT_ready"], 1)[:, 0:P], sc_et[:, :, :].rearrange("p e t -> p (e t)")).then_inc(sm["scoreT_done"], 1)

            def lora_turn(h):
                def run():
                    pe.wait_ge(sm["ld_lin"], 64)
                    o = claim(1 + h, sm["prep_copied"], 3 + h + 1)
                    for i in range(3):
                        ins = turn(o[0:R, i * P:(i + 1) * P], lora_b[:, 3 * h + i, :])
                    ins.then_inc(sm["prep_done"], 1)
                return run

            def value_out():
                mm(claim(3, sm["prep_copied"], 6)[:, 0:P], w_raw[:, 5, :], w1_oT[:, :]).then_inc(sm["prep_done"], 1)

            def bias_out():
                pe.wait_ge(sm["bv_ready"], 1)
                pe.wait_ge(sm["ld_small"], 64)
                o = claim(3, sm["prep_copied"], 7)[:, 0:P]
                mm(o, bv_cols[:, :], w1_oT[:, :], True, False)
                mm(o, ones_row[:, :], bo_row[:, :], False, True).then_inc(sm["prep_done"], 1)

            def effective(i):
                def run():
                    if i == 0:
                        pe.wait_ge(sm["q_ready"], 1)
                        pe.wait_ge(sm["prep_copied"], 5)
                    if i % 3 == 0:
                        claim(5 + i // 3, sm["prep_copied"], 7 + i // 3 + 1)
                    o = bank[5 + i // 3][:, (i % 3) * P:(i % 3 + 1) * P]
                    mm(o, q_ws[:, i, :], ident[:, :], True, False)
                    ins = mm(o, lora_a[:, i, :], lora_bT[:, i, :], False, True)
                    if i % 3 == 2:
                        ins.then_inc(sm["prep_done"], 1)
                return run

            between = dict(enumerate([lora_turn(0), lora_turn(1), value_out, bias_out] + [effective(i) for i in range(NL)], 3))
            pe.wait_ge(sm["constants"], EXPERTS_SET)
            for k in range(ROUNDS):
                pe.wait_ge(sm["cand_counted"], k + 1)
                o = claim(0, sm["cand_taken"], k + 1)
                mm(o[:, 0:3], same_expert[:, :], hit_count[:, :]).then_inc(sm["cand_summed"], 1)
                if k in between:
                    between[k]()
            pe.wait_ge(sm["sel_counted"], 1)
            o = claim(0, sm["room_ready"], 1)
            mm(o[:, 0:1], same_expert[:, :], above_count[:, :])
            mm(o[:, 1:2], tile_before[:, :], tied_count[:, :]).then_inc(sm["sel_summed"], 1)
            pe.wait_ge(sm["kept_counted"], 1)
            mm(claim(7, sm["first_ready"], 1)[:, 0:1], tile_before[:, :], kept_count[:, :]).then_inc(sm["kept_summed"], 1)
            pe.wait_ge(sm["slots_ready"], 1)
            o = claim(6, sm["first_token_ready"], 1)
            pe.wait_ge(sm["constants"], SLOTS_SET)
            for c in range(SC):
                ins = mm(o[:, c * E:(c + 1) * E], slot_row[:, c * P:(c + 1) * P], tile_start[:, :])
            ins.then_inc(sm["start_done"], 1)
            def slot_ranks(e):
                pe.wait_ge(sm["ranks_ready"], 1 if e < 2 else 2)
                o = claim(SLOT_BANKS[e], sm["slots_used"], e + 1)
                for c in range(SC):
                    ins = mm(o[:, c * P:(c + 1) * P], slot_row[:, c * P:(c + 1) * P], rank_by_expert[:, e, :])
                ins.then_inc(sm["slots_done"], 1)

            for e in range(E):
                slot_ranks(e)

            def g_turn(e):
                pe.wait_ge(gathered[e], 16 * SC)
                o = claim(e % 2, sm["gT_copied"], e + 1)
                for c in range(SC):
                    ins = turn(o[:, c * P:(c + 1) * P], xg[:, e, c, 0:D])
                ins.then_inc(sm["gT_done"], 1)

            def hidden(e):
                pe.wait_ge(sm["gT_copied"], e + 1)
                if e == 0:
                    pe.wait_ge(sm["ld_experts"], 32)
                for j in range(J):
                    mm(claim(2 + j, sm["h_ready"], e * J + j + 1), w1[:, e, j * P:(j + 1) * P],
                       xgT[:, e % 2, :]).then_inc(sm["h_done"], 1)

            def outer(e):
                pe.wait_ge(sm["h_ready"], (e + 1) * J)
                if e == 0:
                    pe.wait_ge(sm["ld_experts"], 32)
                for c in range(SC):
                    half, at = divmod(c, 2)
                    if at == 0:
                        o = claim(6 + half, sm["yg_ready"], SC * e + c + 2)
                    oc = o[:, at * D:(at + 1) * D]
                    for j in range(J):
                        mm(oc, hT[:, e % 2, j, c * P:(c + 1) * P], w2[:, e, j, :], j == 0, False)
                    ins = mm(oc, ones3[:, :], bias3[:, R_B2 + e * D:R_B2 + (e + 1) * D], False, True)
                    if at == 1:
                        ins.then_inc(sm["y_done"], 1)

            g_turn(0)
            for e in range(E):
                if e == E - 1:
                    outer(e - 1)
                hidden(e)
                if e + 1 < E:
                    g_turn(e + 1)
                if 0 < e < E - 1:
                    outer(e - 1)
            outer(E - 1)

            def c_turn(g):
                pe.wait_ge(sm["c_ready"], g + 1)
                turn4(claim(C_BANK["TURN"], sm["cT_copied"], g + 1), c_tok, g, sm["cT_done"])

            def c_query(g):
                pe.wait_ge(sm["cT_copied"], g + 1)
                mm(claim(C_BANK["Q"], sm["q1_ready"], g + 1), w1_qT[:, :], cT[:, toks(g)]).then_inc(sm["q1_done"], 1)

            def c_key(g):
                pe.wait_ge(sm["cT_copied"], g + 1)
                mm(claim(C_BANK["K"], sm["k1_ready"], g + 1), w1_kT[:, :], cT[:, toks(g)]).then_inc(sm["k1_done"], 1)

            def c_value(g):
                pe.wait_ge(sm["cT_copied"], g + 1)
                o = claim(C_BANK["V"], sm["v1_ready"], g + 1)
                for i, t in enumerate(tiles(g)):
                    ins = mm(o[:, i * D:(i + 1) * D], cT[:, t * P:(t + 1) * P], w1_vo[:, :])
                ins.then_inc(sm["v1_done"], 1)

            def c_score(g):
                pe.wait_ge(sm["q1_ready"], g + 1)
                pe.wait_ge(sm["k1_ready"], g + 1)
                o2 = [claim(C_BANK[f"S{i}"], sm["p_ready"], g + 1) for i in range(2)]
                for i, t in enumerate(tiles(g)):
                    b = t // BT
                    ins = mm(o2[i // 2][:, (i % 2) * S:(i % 2 + 1) * S], q1T[:, t * P:(t + 1) * P], k1T[:, b * S:(b + 1) * S])
                ins.then_inc(sm["s_done"], 1)

            def c_pturn(g):
                pe.wait_ge(sm["p_ready"], g + 1)
                o2 = [claim(C_BANK["P0"], sm["pT0_copied"], g + 1), claim(C_BANK["P1"], sm["pT1_copied"], g + 1)]
                for b in range(GB):
                    for kb in range(BT):
                        for i in range(BT):
                            t = g * GT + b * BT + i
                            ins = turn(o2[b][:, kb * S + i * P:kb * S + (i + 1) * P], prob[:, t, kb * P:(kb + 1) * P])
                    ins.then_inc(sm["pT_done"], 1)

            def c_out(g):
                pe.wait_ge(sm["pT0_copied"], g + 1)
                pe.wait_ge(sm["pT1_copied"], g + 1)
                pe.wait_ge(sm["v1_ready"], g + 1)
                o = claim(C_BANK["O"], sm["o_ready"], g + 1)
                for i, t in enumerate(tiles(g)):
                    b = t // BT
                    for kb in range(BT):
                        ins = mm(o[:, i * D:(i + 1) * D], probT[:, b, kb, (t % BT) * P:(t % BT + 1) * P],
                                 v1[:, b * BT + kb, :], kb == 0, kb == BT - 1)
                ins.then_inc(sm["o_done"], 1)

            def d_turn(g):
                pe.wait_ge(sm["d_ready"], g + 1)
                turn4(claim(C_BANK["DT"], sm["dT_copied"], g + 1), d_tok, g, sm["dT_done"])

            def linear(k):
                def run(g):
                    if k:
                        pe.wait_ge(hT_ready[k - 1], g + 1)
                    else:
                        pe.wait_ge(sm["dT_copied"], g + 1)
                    if g == 0 and k == 0:
                        pe.wait_ge(sm["eff_mean"], 2)
                    o = claim(C_BANK[f"L{k}"], n_ready[k], g + 1)
                    for i, t in enumerate(tiles(g)):
                        oi = o[:, i * D:(i + 1) * D]
                        mm(oi, h_T[k][:, t * P:(t + 1) * P], w_effT[:, 2 * k, :], True, False)
                        ins = mm(oi, ones3[:, :], bias3[:, R_LIN + k * D:R_LIN + (k + 1) * D], False, True)
                    ins.then_inc(lin_done[k], 1)
                return run

            def n_turn(k):
                def run(g):
                    pe.wait_ge(n_ready[k], g + 1)
                    turn4(claim(C_BANK[f"NT{k}"], gelu_ready[k], g + 1), n_tok, g, nT_done[k])
                return run

            def back(k):
                def run(g):
                    pe.wait_ge(gelu_ready[k], g + 1)
                    mm(claim(C_BANK[f"R{k}"], hT_ready[k], g + 1), w_effT[:, 2 * k + 1, :],
                       g_T[:, toks(g)]).then_inc(res_done[k], 1)
                return run

            def back_last(g):
                pe.wait_ge(gelu_ready[2], g + 1)
                o = claim(C_BANK["FIN"], sm["fin_ready"], g + 1)
                for i, t in enumerate(tiles(g)):
                    oi = o[:, i * D:(i + 1) * D]
                    mm(oi, g_T[:, t * P:(t + 1) * P], w_effT[:, 5, :], True, False)
                    mm(oi, h_T[2][:, t * P:(t + 1) * P], ident[:, :], False, False)
                    ins = mm(oi, ones3[:, :], bias3[:, R_LIN + 3 * D:R_LIN + 4 * D], False, True)
                ins.then_inc(sm["fin_done"], 1)

            flow(SECOND_BEATS, SECOND_EVERY, G, c_turn=c_turn, q1=c_query, k1=c_key, v1=c_value, score=c_score, pturn=c_pturn,
                 out=c_out, d_turn=d_turn, lin0=linear(0), lin1=linear(1), lin2=linear(2), nturn0=n_turn(0),
                 nturn1=n_turn(1), nturn2=n_turn(2), back0=back(0), back1=back(1), back2=back_last)

        @block.vector
        def _(dve):
            step = [0]

            def mark(ins):
                step[0] += 1
                ins.then_inc(sm["dve_step"], 1)

            def settle():
                dve.wait_ge(sm["dve_step"], step[0])

            def link(ins):
                mark(ins)
                settle()

            def layer_stats(n, src, g):
                L = ln[n]
                for i, t in enumerate(tiles(g)):
                    ins = dve.bn_stats(stats[:, t, :], src(i, t))
                link(ins)
                for t in tiles(g):
                    ins = dve.bn_aggr(L.mv[:, t, :], stats[:, t, :])
                ins.then_inc(L.stats_ready, 1)

            def normalise(n, dst, src, g, done):
                L = ln[n]
                dve.wait_ge(L.rstd_ready, g + 1)
                for i, t in enumerate(tiles(g)):
                    ins = dve.tensor_scalar(dst[:, t, 0:D], src(i, t), L.mv[:, t, 0:1], L.rstd[:, t:t + 1],
                                            ALU.subtract, ALU.mult)
                ins.then_inc(done, 1)

            def of(tensor):
                return lambda i, t: tensor[:, t, 0:D]

            def of_bank(b):
                return lambda i, t: bank[b][:, i * D:(i + 1) * D]

            def bias_split(g):
                if g:
                    return
                dve.wait_ge(sm["ld_bias"], 16 * 5)
                dve.wait_ge(sm["constants"], CENTRED_SET)
                link(dve.tensor_reduce(bias_mean[:, :], bias_rows[:, :], AX.X, ALU.add))
                link(dve.tensor_tensor(bias_mean[:, :], bias_mean[:, :], centred[:, :], ALU.mult))
                link(dve.tensor_scalar(bias_rows[:, :], bias_rows[:, :], bias_mean[:, :], None, ALU.subtract))
                for i, part in enumerate((bias_hi, bias_mid, bias_lo)):
                    dve.tensor_copy(part[:, :], bias_rows[:, :]).then_inc(sm["bias_parts"], 1)
                    dve.wait_ge(sm["bias_parts"], i + 1)
                    if i < 2:
                        link(dve.tensor_tensor(bias_rows[:, :], bias_rows[:, :], part[:, :], ALU.subtract))

            def a_stats(g):
                dve.wait_ge(ld_x[g], 16)
                layer_stats("a_in", of(x0), g)

            def kv_evac(g):
                if g == 0:
                    dve.wait_ge(sm["constants"], ONES_SET)
                dve.wait_ge(sm["kv1_done"], g + 1)
                t = g * GT + 2
                kv = bank[A_BANK["KV1"]].rearrange("p (t c) -> p t c", t=2)
                dve.tensor_scalar(k_tok[:, t:t + 2, :], kv[:, :, 0:D], 0.0, None, ALU.max)
                dve.tensor_copy(v_tok[:, t:t + 2, 0:D], kv[:, :, D:2 * D]).then_inc(sm["kv1_ready"], 1)

            def kv_mask(g):
                dve.wait_ge(sm["ksum_done"], g + 1)
                if g == 0:
                    dve.wait_ge(sm["constants"], HEADS_SET)
                kv = bank[A_BANK["MIX"]].rearrange("p (b c) -> p b c", b=GB)
                bs = slice(g * GB, (g + 1) * GB)
                dve.tensor_tensor(kv_blk[:, bs, 0:D], kv[:, :, 0:D],
                                  head_block[:, :].unsqueeze(1).to_broadcast([P, GB, D]), ALU.mult)
                dve.tensor_tensor(kv_blk[:, bs, D:D + H], kv[:, :, D:D + 1].to_broadcast([P, GB, H]),
                                  head_col[:, :].unsqueeze(1).to_broadcast([P, GB, H]), ALU.mult).then_inc(sm["kv_ready"], 1)

            def divide(g):
                dve.wait_ge(sm["ctx_done"], g + 1)
                c = slice(g * GT, (g + 1) * GT)
                o = banks[:, 5:7, :].rearrange("p b (i c) -> p (b i) c", i=2)
                link(dve.tensor_scalar(den[:, c, :], o[:, :, D:D + H], DENOM_EPS, None, ALU.max))
                link(dve.reciprocal(rden[:, c, :], den[:, c, :]))
                for i, t in enumerate(tiles(g)):
                    ins = dve.tensor_tensor(y0[:, t, :].rearrange("p (h d) -> p h d", h=H),
                                            o[:, i, 0:D].rearrange("p (h d) -> p h d", h=H),
                                            rden[:, t, :].unsqueeze(2).to_broadcast([P, H, HD]), ALU.mult)
                ins.then_inc(sm["y0_ready"], 1)

            def mid_stats(g):
                dve.wait_ge(sm["y1_ready"], g + 1)
                layer_stats("a_mid", of(y1), g)

            def mid_scale(g):
                c = slice(g * GT, (g + 1) * GT)
                dve.wait_ge(sm["ld_small"], 64)
                dve.wait_ge(sm["mid_ready"], g + 1)
                link(dve.tensor_tensor(z[:, c, :], z[:, c, :], gamma_all[:, :].unsqueeze(1).to_broadcast([P, GT, D]), ALU.mult))
                link(dve.tensor_tensor(z[:, c, :], z[:, c, :], beta_all[:, :].unsqueeze(1).to_broadcast([P, GT, D]), ALU.add))

            def branch_stats(g):
                layer_stats("a_out", of(z), g)

            def b_stats(g):
                dve.wait_ge(sm["x1_ready"], g + 1)
                layer_stats("b_in", of(x1), g)

            def b_norm(g):
                normalise("b_in", tab, of(x1), g, sm["b_ready"])

            flow(FIRST_BEATS, FIRST_EVERY, G, a_stats=a_stats, bias=bias_split, kv1_evac=kv_evac, mask=kv_mask, divide=divide,
                 m_stats=mid_stats, m_scale=mid_scale, o_stats=branch_stats, b_stats=b_stats, b_norm=b_norm)

            dve.wait_ge(sm["logit_done"], G)
            logits = bank[7][:, 0:T * E].rearrange("p (t e) -> p t e", t=T)
            spread = lambda v: v.unsqueeze(2).to_broadcast([P, T, E])
            link(dve.tensor_reduce(logit_max[:, :], logits, AX.X, ALU.max))
            dve.tensor_tensor(shifted[:, :, :], logits, spread(logit_max[:, :]), ALU.subtract).then_inc(sm["shifted_ready"], 1)
            dve.wait_ge(sm["exp_ready"], 1)
            link(dve.tensor_reduce(expsum[:, :], expd[:, :, :], AX.X, ALU.add))
            link(dve.reciprocal(rexpsum[:, :], expsum[:, :]))
            link(dve.tensor_tensor(tab[:, :, D:ROW], expd[:, :, :], spread(rexpsum[:, :]), ALU.mult))
            dve.tensor_copy(sc_et[:, :, :], tab[:, :, D:ROW].rearrange("p t e -> p e t")).then_inc(sm["scores_ready"], 1)

            dve.wait_ge(sm["constants"], EXPERTS_SET)
            mark(dve.tensor_scalar(cand[:, 0, :], quarters[:, :], ROUND_SHIFT[0], None, ALU.logical_shift_left))
            dve.wait_ge(sm["prep_copied"], 3)
            dve.tensor_copy(bv_cols[:, :], vec[:, V_BV1:V_BV1 + 1].to_broadcast([P, P])).then_inc(sm["bv_ready"], 1)
            dve.wait_ge(sm["scoreT_done"], 1)
            dve.tensor_copy(scoreT[:, :], bank[7][:, 0:P]).then_inc(sm["scoreT_ready"], 1)
            dve.wait_ge(sm["scoreT_ready"], 1)
            settle()
            for k in range(ROUNDS):
                now, then = cand[:, k % 2, :], cand[:, (k + 1) % 2, :]
                for j in (1, 2, 3):
                    ins = dve.tensor_scalar(hits[:, j - 1, :], scoreT[:, :], now[:, j:j + 1].bitcast(F32), None, ALU.is_ge, ALU.add,
                                            accum_out=hit_count[:, j - 1:j])
                ins.then_inc(sm["cand_counted"], 1)
                if k + 1 < ROUNDS:
                    mark(dve.scalar_tensor_tensor(then, quarters[:, :], ROUND_SHIFT[k + 1], now[:, 0:1].to_broadcast([P, 4]),
                                                  ALU.logical_shift_left, ALU.bitwise_xor))
                else:
                    mark(dve.tensor_copy(then[:, 0:1], now[:, 0:1]))
                dve.wait_ge(sm["cand_summed"], k + 1)
                dve.tensor_scalar(reached[:, :], bank[0][:, 0:3], float(KEEP) - 0.5, None, ALU.is_ge, ALU.add,
                                  accum_out=reached_count[:, :]).then_inc(sm["cand_taken"], 1)
                dve.wait_ge(sm["cand_taken"], k + 1)
                link(dve.tensor_copy(quarter[:, :], reached_count[:, :]))
                width = 4 if k + 1 < ROUNDS else 1
                link(dve.scalar_tensor_tensor(then[:, 0:width], quarter[:, :].to_broadcast([P, width]), ROUND_SHIFT[k],
                                              then[:, 0:width], ALU.logical_shift_left, ALU.bitwise_xor))
            cut = cand[:, ROUNDS % 2, 0:1].bitcast(F32)

            dve.tensor_scalar(above[:, :], scoreT[:, :], cut, None, ALU.is_gt, ALU.add, accum_out=above_count[:, :])
            mark(dve.tensor_scalar(tied[:, :], scoreT[:, :], cut, None, ALU.is_equal, ALU.add, accum_out=tied_count[:, :]))
            settle()
            dve.wait_ge(sm["constants"], SLOTS_SET)
            dve.tensor_tensor_scan(tie_rank[:, :], tied[:, :], zeros[:, 0:P], 0.0, ALU.add, ALU.add).then_inc(sm["sel_counted"], 1)
            dve.wait_ge(sm["sel_summed"], 1)
            dve.wait_ge(sm["sel_counted"], 1)
            link(dve.tensor_scalar(tie_room[:, 0:1], bank[0][:, 0:1], -1.0, float(KEEP), ALU.mult, ALU.add))
            dve.tensor_tensor(tie_room[:, 1:2], tie_room[:, 0:1], bank[0][:, 1:2], ALU.subtract).then_inc(sm["room_ready"], 1)
            dve.wait_ge(sm["room_ready"], 1)
            link(dve.scalar_tensor_tensor(tie_kept[:, :], tie_rank[:, :], tie_room[:, 1:2], tied[:, :], ALU.is_le, ALU.mult))
            link(dve.tensor_tensor_scan(kept_rank[:, :], above[:, :], tie_kept[:, :], 0.0, ALU.add, ALU.add))
            dve.tensor_copy(kept_count[:, :], kept_rank[:, P - 1:P]).then_inc(sm["kept_counted"], 1)
            dve.wait_ge(sm["kept_summed"], 1)
            dve.tensor_copy(kept_first[:, :], bank[7][:, 0:1]).then_inc(sm["first_ready"], 1)
            dve.wait_ge(sm["first_ready"], 1)
            dve.tensor_scalar(rank_all[:, :], kept_rank[:, :], kept_first[:, :], None, ALU.add)
            mark(dve.tensor_scalar(rank_last[:, :], kept_rank[:, P - 1:P], kept_first[:, :], None, ALU.add))
            mark(dve.tensor_scalar(from_first[:, :], slot_free[:, :], kept_first[:, :], None, ALU.is_ge))
            settle()
            dve.scalar_tensor_tensor(slot_row[:, :], slot_free[:, :], rank_last[:, :], from_first[:, :], ALU.is_lt, ALU.mult).then_inc(sm["slots_ready"], 1)
            for part in (slice(0, 2), slice(2, E)):
                n = part.stop - part.start
                dve.tensor_tensor(rank_by_expert[:, part, :], own_expert[:, part].unsqueeze(2).to_broadcast([P, n, P]),
                                  rank_all[:, :].unsqueeze(1).to_broadcast([P, n, P]), ALU.mult).then_inc(sm["ranks_ready"], 1)
            dve.wait_ge(sm["start_done"], 1)
            dve.tensor_copy(first_token[:, :, :], bank[6][:, 0:SC * E].rearrange("p (c e) -> p c e", c=SC)).then_inc(sm["first_token_ready"], 1)
            dve.wait_ge(sm["first_token_ready"], 1)
            def token_list(e):
                dve.wait_ge(sm["slots_done"], e + 1)
                for c in range(SC):
                    ins = dve.tensor_scalar(passed[:, c, :], bank[SLOT_BANKS[e]][:, c * P:(c + 1) * P], slot_part[:, c:c + 1], None,
                                            ALU.is_le, ALU.add, accum_out=passed_count[:, c, e:e + 1])
                ins.then_inc(sm["slots_used"], 1)
                dve.wait_ge(sm["slots_used"], e + 1)
                dve.tensor_tensor(token_of[:, :, e], passed_count[:, :, e], first_token[:, :, e], ALU.add).then_inc(sm["token_ready"], 1)

            def g_evac(e):
                if e >= 2:
                    dve.wait_ge(sm["h_done"], (e - 1) * J)
                dve.wait_ge(sm["gT_done"], e + 1)
                dve.tensor_copy(xgT[:, e % 2, :], bank[e % 2]).then_inc(sm["gT_copied"], 1)

            def gate(e):
                if e >= YB:
                    dve.wait_ge(scattered[e % 2], 16 * SC * ((e - YB) // 2 + 1))
                for c in range(SC):
                    half, at = divmod(c, 2)
                    if at == 0:
                        dve.wait_ge(sm["y_done"], SC // 2 * e + half + 1)
                    dve.tensor_scalar(yg[:, e % YB, c, :], bank[6 + half][:, at * D:(at + 1) * D],
                                      xg[:, e, c, D + e:D + e + 1], None, ALU.mult).then_inc(sm["yg_ready"], 1)

            for e in range(LISTS_FIRST):
                token_list(e)
            g_evac(0)
            for e in range(LISTS_FIRST, E):
                token_list(e)
            for e in range(E):
                if e + 1 < E:
                    g_evac(e + 1)
                if e:
                    gate(e - 1)
            gate(E - 1)

            def c_first(g):
                dve.wait_ge(moe_loaded[g], 16)
                layer_stats("b_out", of(moe), g)

            def c_stats(g):
                dve.wait_ge(sm["x2_ready"], g + 1)
                layer_stats("c_in", of(x2), g)

            def c_norm(g):
                normalise("c_in", c_tok, of(x2), g, sm["c_ready"])

            def v1_evac(g):
                dve.wait_ge(sm["v1_done"], g + 1)
                dve.tensor_copy(v1[:, g * GT:(g + 1) * GT, :], bank[C_BANK["V"]].rearrange("p (t d) -> p t d", t=GT)).then_inc(sm["v1_ready"], 1)

            def score_max(g):
                c = slice(g * GT, (g + 1) * GT)
                dve.wait_ge(sm["s_done"], g + 1)
                link(dve.tensor_reduce(smax[:, c], banks[:, C_BANK["S0"]:C_BANK["S1"] + 1, :].rearrange("p b (i k) -> p (b i) k", k=S), AX.X, ALU.max))
                dve.tensor_scalar(nsmax[:, c], smax[:, c], -ATT_SCALE, None, ALU.mult).then_inc(sm["smax_ready"], 1)

            def p_evac(g):
                dve.wait_ge(sm["pT_done"], GB * g + 1)
                dve.tensor_copy(probT[:, GB * g, :, :], bank[C_BANK["P0"]].rearrange("p (k q) -> p k q", k=BT)).then_inc(sm["pT0_copied"], 1)

            def o_norm(g):
                c = slice(g * GT, (g + 1) * GT)
                dve.wait_ge(sm["p_ready"], g + 1)
                mark(dve.reciprocal(rsum[:, c], psum_p[:, c]))
                dve.wait_ge(sm["prep_copied"], 7)
                dve.wait_ge(sm["o_done"], g + 1)
                settle()
                for i, t in enumerate(tiles(g)):
                    ins = dve.scalar_tensor_tensor(o_tok[:, t, :], bank[C_BANK["O"]][:, i * D:(i + 1) * D], rsum[:, t:t + 1],
                                                   bo_all[:, :], ALU.mult, ALU.add)
                ins.then_inc(sm["o_ready"], 1)

            def mix_stats(g):
                dve.wait_ge(sm["o_ready"], g + 1)
                layer_stats("c_out", of(o_tok), g)

            def d_stats(g):
                dve.wait_ge(sm["x3_ready"], g + 1)
                layer_stats("d_in", of(x3), g)

            def d_norm(g):
                normalise("d_in", d_tok, of(x3), g, sm["d_ready"])

            def lin_stats(k):
                def run(g):
                    dve.wait_ge(lin_done[k], g + 1)
                    layer_stats(f"d{k}", of_bank(C_BANK[f"L{k}"]), g)
                return run

            def residual(k):
                def run(g):
                    dve.wait_ge(res_done[k], g + 1)
                    b = V_BIAS + 2 * k + 1
                    dve.scalar_tensor_tensor(h_T[k + 1][:, toks(g)], bank[C_BANK[f"R{k}"]], vec[:, b:b + 1],
                                             h_T[k][:, toks(g)], ALU.add, ALU.add).then_inc(hT_ready[k], 1)
                return run

            def out_stats(g):
                dve.wait_ge(sm["fin_ready"], g + 1)
                layer_stats("d_out", of(h_out), g)

            def out_norm(g):
                normalise("d_out", u, of(h_out), g, sm["uo_ready"])

            flow(SECOND_BEATS, SECOND_EVERY, G, c_first=c_first, c_stats=c_stats, c_norm=c_norm, v1_evac=v1_evac,
                 score_max=score_max, p0=p_evac, o_norm=o_norm, o_stats=mix_stats, d_stats=d_stats, d_norm=d_norm,
                 lstats0=lin_stats(0), lstats1=lin_stats(1), lstats2=lin_stats(2), res0=residual(0), res1=residual(1),
                 ostats=out_stats, onorm=out_norm)


_INS = ['L0_attn_x', 'L0_attn_Wq', 'L0_attn_bq', 'L0_attn_Wk', 'L0_attn_bk', 'L0_attn_Wv', 'L0_attn_bv',
        'L0_attn_gamma', 'L0_attn_beta', 'L0_ffn_Wr', 'L0_ffn_W1', 'L0_ffn_b1', 'L0_ffn_W2', 'L0_ffn_b2',
        'L1_attn_Wq', 'L1_attn_bq', 'L1_attn_Wk', 'L1_attn_bk', 'L1_attn_Wv', 'L1_attn_bv', 'L1_attn_Wo',
        'L1_attn_bo', 'L1_ffn_qweights', 'L1_ffn_scales', 'L1_ffn_biases', 'L1_ffn_lora_a', 'L1_ffn_lora_b',
        'L1_ffn_ln_gamma', 'L1_ffn_ln_beta']


def kernel(**inputs):
    import numpy as _np
    import concourse.bacc as _bacc
    from concourse import mybir as _mybir
    from concourse.bass_utils import run_bass_kernel_spmd as _run

    nc = _bacc.Bacc("TRN2", target_bir_lowering=False, num_devices=1)
    arrays, args = {}, {}
    for name in _INS:
        x = _np.ascontiguousarray(inputs[name])
        arrays[f"in_{name}_dram"] = x
        args[name] = nc.dram_tensor(f"in_{name}_dram", x.shape, _mybir.dt.from_np(x.dtype), kind="ExternalInput").ap()
    shape = inputs["L0_attn_x"].shape
    args["out"] = nc.dram_tensor("out_0_dram", shape, _mybir.dt.float32, kind="ExternalOutput").ap()
    sandwich_kernel(nc, args)
    r = _run(nc, [arrays], core_ids=[0])
    return r.results[0]["out_0_dram"]
```
